# Optimizing a Trainium2 kernel written in Bass

```python
import numpy as np
import jax
import jax.numpy as jnp

def _softmax(x, axis=-1):
    return jax.nn.softmax(x, axis=axis)

def _gelu(x):
    return jax.nn.gelu(x, approximate=True)

def _silu(x):
    return jax.nn.silu(x)

def _sigmoid(x):
    return jax.nn.sigmoid(x)

def _layernorm(x, axis=-1, eps=1e-05):
    m = jnp.mean(x, axis=axis, keepdims=True)
    v = jnp.var(x, axis=axis, keepdims=True)
    return (x - m) / jnp.sqrt(v + eps)

def _scatter_add(tgt, idx, src, axis=0):
    return tgt.at[idx].add(src)

def _segment_sum(src, seg, n):
    return jax.ops.segment_sum(src, seg, n)
kernel_name = 'mk_gnn_preln_d4_gnn_r8_cdf101'

def setup_inputs(seed: int=0):
    np.random.seed(seed)
    _w = jnp.asarray

    def _rec_inputs():
        import jax
        import jax.numpy as jnp
        _gk = jax.random.key(seed)
        x = -0.0003713 + 1 * jax.random.normal(jax.random.fold_in(_gk, 1), (6250, 256), jnp.float32)
        src = jax.random.randint(jax.random.fold_in(_gk, 2), (100000,), 0, 6250, jnp.int32)
        dst = jax.random.randint(jax.random.fold_in(_gk, 3), (100000,), 0, 6250, jnp.int32)
        _o = jnp.argsort(dst, stable=True)
        src = src[_o]
        dst = dst[_o]
        edge_attr_128 = -5.16925e-05 + 1.00005 * jax.random.normal(jax.random.fold_in(_gk, 11), (100000, 128), jnp.float32)
        edge_attr_64 = 0.000312547 + 1.00004 * jax.random.normal(jax.random.fold_in(_gk, 12), (100000, 64), jnp.float32)
        return (x, src, dst, edge_attr_128, edge_attr_64)
    x, src, dst, edge_attr_128, edge_attr_64 = _rec_inputs()

    def _L0_gnn_setup():
        import jax, jax.numpy as jnp
        import numpy as np
        N_NODES = 6250

        def _sage_conv(x, src, dst, W_l, b_l, W_r):
            gathered = jnp.take(x, src, axis=0)
            summed = jax.ops.segment_sum(gathered, dst, num_segments=N_NODES)
            deg = jax.ops.segment_sum(jnp.ones_like(dst, dtype=x.dtype), dst, num_segments=N_NODES)
            mean_nb = summed / jnp.maximum(deg, 1.0)[:, None]
            return mean_nb @ W_l + b_l + x @ W_r
        key = jax.random.key(seed)
        ks = jax.random.split(key, 8)
        d = 256
        E = 100000
        s = 1.0 / np.sqrt(d)
        x = jax.random.normal(ks[0], (N_NODES, d), dtype=jnp.float32)
        ei = jax.random.randint(ks[1], (2, E), 0, N_NODES, dtype=jnp.int64)
        W1_l = jax.random.normal(ks[2], (d, d), dtype=jnp.float32) * s
        b1 = jnp.zeros((d,), dtype=jnp.float32)
        W1_r = jax.random.normal(ks[3], (d, d), dtype=jnp.float32) * s
        W2_l = jax.random.normal(ks[4], (d, d), dtype=jnp.float32) * s
        b2 = jnp.zeros((d,), dtype=jnp.float32)
        W2_r = jax.random.normal(ks[5], (d, d), dtype=jnp.float32) * s
        return {'x': x, 'ei': ei, 'W1_l': W1_l, 'b1': b1, 'W1_r': W1_r, 'W2_l': W2_l, 'b2': b2, 'W2_r': W2_r}
    _L0_gnn_all = _L0_gnn_setup()
    _L0_gnn_in = {k: v for k, v in _L0_gnn_all.items() if k in ('W1_l', 'b1', 'W1_r', 'W2_l', 'b2', 'W2_r')}
    del _L0_gnn_all

    def _L1_gnn_setup():
        import jax, jax.numpy as jnp
        import numpy as np
        N, E, H, DE = (1250, 31250, 256, 64)
        EPS = 1e-05

        def _lin_init(k, fan_in, shape):
            s = 1.0 / np.sqrt(fan_in)
            return jax.random.uniform(k, shape, jnp.float32, -s, s)
        key = jax.random.key(seed)
        ks = jax.random.split(key, 12)
        x = jax.random.normal(ks[0], (N, H), jnp.float32)
        edge_index = jax.random.randint(ks[1], (2, E), 0, N)
        edge_attr = jax.random.normal(ks[2], (E, DE), jnp.float32)
        d_in = H + DE
        W1 = _lin_init(ks[3], d_in, (d_in, H))
        b1 = _lin_init(ks[4], d_in, (H,))
        W2 = _lin_init(ks[5], H, (H, H))
        b2 = _lin_init(ks[6], H, (H,))
        Wg = _lin_init(ks[7], d_in, (d_in, H))
        bg = _lin_init(ks[8], d_in, (H,))
        gamma = jnp.ones((H,), jnp.float32)
        beta = jnp.zeros((H,), jnp.float32)
        return {'x': x, 'edge_index': edge_index, 'edge_attr': edge_attr, 'W1': W1, 'b1': b1, 'W2': W2, 'b2': b2, 'Wg': Wg, 'bg': bg, 'gamma': gamma, 'beta': beta}
    _L1_gnn_all = _L1_gnn_setup()
    _L1_gnn_in = {k: v for k, v in _L1_gnn_all.items() if k in ('W1', 'b1', 'W2', 'b2', 'Wg', 'bg', 'gamma', 'beta')}
    del _L1_gnn_all

    def _L2_gnn_setup():
        import jax, jax.numpy as jnp
        import numpy as np
        N_NODES = 12500
        BN_EPS = 1e-05

        def gcn_conv(x, src, dst, W, b, n):
            h = x @ W
            loop = jnp.arange(n, dtype=src.dtype)
            s = jnp.concatenate([src, loop])
            d = jnp.concatenate([dst, loop])
            deg = jax.ops.segment_sum(jnp.ones(s.shape, h.dtype), d, num_segments=n)
            dinv = jnp.where(deg > 0, jax.lax.rsqrt(jnp.maximum(deg, 1.0)), 0.0)
            norm = dinv[s] * dinv[d]
            msg = h[s] * norm[:, None]
            out = jax.ops.segment_sum(msg, d, num_segments=n)
            return out + b

        def batch_norm(x, gamma, beta):
            mean = jnp.mean(x, axis=0)
            var = jnp.mean(jnp.square(x - mean), axis=0)
            return (x - mean) * jax.lax.rsqrt(var + BN_EPS) * gamma + beta
        key = jax.random.key(seed)
        ks = jax.random.split(key, 10)
        d0, d1, d2 = (256, 128, 64)
        d_cat = d0 + d1 + d2
        inp = {'node_features': jax.random.normal(ks[0], (N_NODES, d0), jnp.float32), 'edge_idx': jax.random.randint(ks[1], (2, 200000), 0, N_NODES, jnp.int64), 'W1': jax.random.normal(ks[2], (d0, d1), jnp.float32) * (1.0 / np.sqrt(d0)), 'b1': jnp.zeros((d1,), jnp.float32), 'g1': jnp.ones((d1,), jnp.float32), 'be1': jnp.zeros((d1,), jnp.float32), 'W2': jax.random.normal(ks[3], (d1, d2), jnp.float32) * (1.0 / np.sqrt(d1)), 'b2': jnp.zeros((d2,), jnp.float32), 'g2': jnp.ones((d2,), jnp.float32), 'be2': jnp.zeros((d2,), jnp.float32), 'Wfc': jax.random.normal(ks[4], (d_cat, d0), jnp.float32) * (1.0 / np.sqrt(d_cat)), 'bfc': jnp.zeros((d0,), jnp.float32)}
        return inp
    _L2_gnn_all = _L2_gnn_setup()
    _L2_gnn_in = {k: v for k, v in _L2_gnn_all.items() if k in ('W1', 'b1', 'g1', 'be1', 'W2', 'b2', 'g2', 'be2', 'Wfc', 'bfc')}
    del _L2_gnn_all

    def _L3_gnn_setup():
        import jax, jax.numpy as jnp
        import numpy as np
        N_NODES = 6250
        N_EDGES = 100000
        IN_DIM = 256
        OUT_DIM = 256
        HEADS = 1
        EDGE_DIM = 128
        NEG_SLOPE = 0.01
        key = jax.random.key(seed)
        ks = jax.random.split(key, 8)
        x = jax.random.normal(ks[0], (N_NODES, IN_DIM), dtype=jnp.float32)
        edge_index = jax.random.randint(ks[1], (2, N_EDGES), 0, N_NODES, dtype=jnp.int64)
        edge_attr = jax.random.normal(ks[2], (N_EDGES, EDGE_DIM), dtype=jnp.float32)
        hc = HEADS * OUT_DIM
        Wn = jax.random.normal(ks[3], (hc, IN_DIM), dtype=jnp.float32) / np.sqrt(IN_DIM)
        bn = jnp.zeros((hc,), dtype=jnp.float32)
        We = jax.random.normal(ks[4], (hc, EDGE_DIM), dtype=jnp.float32) / np.sqrt(EDGE_DIM)
        be = jnp.zeros((hc,), dtype=jnp.float32)
        attn = jax.random.normal(ks[5], (1, HEADS, OUT_DIM), dtype=jnp.float32) * np.sqrt(2.0 / (HEADS * OUT_DIM + 1))
        return {'x': x, 'edge_index': edge_index, 'edge_attr': edge_attr, 'Wn': Wn, 'bn': bn, 'We': We, 'be': be, 'attn': attn}
    _L3_gnn_all = _L3_gnn_setup()
    _L3_gnn_in = {k: v for k, v in _L3_gnn_all.items() if k in ('Wn', 'bn', 'We', 'be', 'attn')}
    del _L3_gnn_all
    return {'x': x, 'src': src, 'dst': dst, 'edge_attr_128': edge_attr_128, 'edge_attr_64': edge_attr_64, 'L0_gnn_W1_l': _L0_gnn_in['W1_l'], 'L0_gnn_b1': _L0_gnn_in['b1'], 'L0_gnn_W1_r': _L0_gnn_in['W1_r'], 'L0_gnn_W2_l': _L0_gnn_in['W2_l'], 'L0_gnn_b2': _L0_gnn_in['b2'], 'L0_gnn_W2_r': _L0_gnn_in['W2_r'], 'L1_gnn_W1': _L1_gnn_in['W1'], 'L1_gnn_b1': _L1_gnn_in['b1'], 'L1_gnn_W2': _L1_gnn_in['W2'], 'L1_gnn_b2': _L1_gnn_in['b2'], 'L1_gnn_Wg': _L1_gnn_in['Wg'], 'L1_gnn_bg': _L1_gnn_in['bg'], 'L1_gnn_gamma': _L1_gnn_in['gamma'], 'L1_gnn_beta': _L1_gnn_in['beta'], 'L2_gnn_W1': _L2_gnn_in['W1'], 'L2_gnn_b1': _L2_gnn_in['b1'], 'L2_gnn_g1': _L2_gnn_in['g1'], 'L2_gnn_be1': _L2_gnn_in['be1'], 'L2_gnn_W2': _L2_gnn_in['W2'], 'L2_gnn_b2': _L2_gnn_in['b2'], 'L2_gnn_g2': _L2_gnn_in['g2'], 'L2_gnn_be2': _L2_gnn_in['be2'], 'L2_gnn_Wfc': _L2_gnn_in['Wfc'], 'L2_gnn_bfc': _L2_gnn_in['bfc'], 'L3_gnn_Wn': _L3_gnn_in['Wn'], 'L3_gnn_bn': _L3_gnn_in['bn'], 'L3_gnn_We': _L3_gnn_in['We'], 'L3_gnn_be': _L3_gnn_in['be'], 'L3_gnn_attn': _L3_gnn_in['attn']}

def reference(x, src, dst, edge_attr_128, edge_attr_64, L0_gnn_W1_l, L0_gnn_b1, L0_gnn_W1_r, L0_gnn_W2_l, L0_gnn_b2, L0_gnn_W2_r, L1_gnn_W1, L1_gnn_b1, L1_gnn_W2, L1_gnn_b2, L1_gnn_Wg, L1_gnn_bg, L1_gnn_gamma, L1_gnn_beta, L2_gnn_W1, L2_gnn_b1, L2_gnn_g1, L2_gnn_be1, L2_gnn_W2, L2_gnn_b2, L2_gnn_g2, L2_gnn_be2, L2_gnn_Wfc, L2_gnn_bfc, L3_gnn_Wn, L3_gnn_bn, L3_gnn_We, L3_gnn_be, L3_gnn_attn):
    import jax
    import jax.numpy as jnp

    def _L0_gnn_ref(x, ei, W1_l, b1, W1_r, W2_l, b2, W2_r):
        import jax, jax.numpy as jnp
        import numpy as np
        N_NODES = 6250

        def _sage_conv(x, src, dst, W_l, b_l, W_r):
            gathered = jnp.take(x, src, axis=0)
            summed = jax.ops.segment_sum(gathered, dst, num_segments=N_NODES)
            deg = jax.ops.segment_sum(jnp.ones_like(dst, dtype=x.dtype), dst, num_segments=N_NODES)
            mean_nb = summed / jnp.maximum(deg, 1.0)[:, None]
            return mean_nb @ W_l + b_l + x @ W_r
        src, dst = (ei[0], ei[1])
        h = jax.nn.relu(_sage_conv(x, src, dst, W1_l, b1, W1_r))
        h = _sage_conv(h, src, dst, W2_l, b2, W2_r)
        return h

    def _L1_gnn_ref(x, edge_index, edge_attr, W1, b1, W2, b2, Wg, bg, gamma, beta):
        import jax, jax.numpy as jnp
        import numpy as np
        N, E, H, DE = (1250, 31250, 256, 64)
        EPS = 1e-05

        def _lin_init(k, fan_in, shape):
            s = 1.0 / np.sqrt(fan_in)
            return jax.random.uniform(k, shape, jnp.float32, -s, s)
        src, dst = (edge_index[0], edge_index[1])
        ei = jnp.concatenate([x[src], edge_attr], axis=-1)
        core = jnp.maximum(ei @ W1 + b1, 0.0) @ W2 + b2
        gate = jax.nn.sigmoid(ei @ Wg + bg)
        msg = gate * core
        agg = jax.ops.segment_sum(msg, dst, num_segments=x.shape[0])
        out = agg + x
        mu = jnp.mean(out, axis=-1, keepdims=True)
        var = jnp.var(out, axis=-1, keepdims=True)
        out = (out - mu) * jax.lax.rsqrt(var + EPS) * gamma + beta
        return out

    def _L2_gnn_ref(node_features, edge_idx, W1, b1, g1, be1, W2, b2, g2, be2, Wfc, bfc):
        import jax, jax.numpy as jnp
        import numpy as np
        N_NODES = 12500
        BN_EPS = 1e-05

        def gcn_conv(x, src, dst, W, b, n):
            h = x @ W
            loop = jnp.arange(n, dtype=src.dtype)
            s = jnp.concatenate([src, loop])
            d = jnp.concatenate([dst, loop])
            deg = jax.ops.segment_sum(jnp.ones(s.shape, h.dtype), d, num_segments=n)
            dinv = jnp.where(deg > 0, jax.lax.rsqrt(jnp.maximum(deg, 1.0)), 0.0)
            norm = dinv[s] * dinv[d]
            msg = h[s] * norm[:, None]
            out = jax.ops.segment_sum(msg, d, num_segments=n)
            return out + b

        def batch_norm(x, gamma, beta):
            mean = jnp.mean(x, axis=0)
            var = jnp.mean(jnp.square(x - mean), axis=0)
            return (x - mean) * jax.lax.rsqrt(var + BN_EPS) * gamma + beta
        n = node_features.shape[0]
        src, dst = (edge_idx[0], edge_idx[1])
        feats = [node_features]
        x = node_features
        x = gcn_conv(x, src, dst, W1, b1, n)
        x = jax.nn.relu(batch_norm(x, g1, be1))
        feats.append(x)
        x = gcn_conv(x, src, dst, W2, b2, n)
        x = jax.nn.relu(batch_norm(x, g2, be2))
        feats.append(x)
        cat = jnp.concatenate(feats, axis=1)
        return jax.nn.relu(cat @ Wfc + bfc)

    def _L3_gnn_ref(x, edge_index, edge_attr, Wn, bn, We, be, attn):
        import jax, jax.numpy as jnp
        import numpy as np
        N_NODES = 6250
        N_EDGES = 100000
        IN_DIM = 256
        OUT_DIM = 256
        HEADS = 1
        EDGE_DIM = 128
        NEG_SLOPE = 0.01
        N = x.shape[0]
        H, C = (attn.shape[1], attn.shape[2])
        src, dst = (edge_index[0], edge_index[1])
        h = x @ Wn.T + bn
        e = edge_attr @ We.T + be
        xj = h[src].reshape(-1, H, C)
        ee = e.reshape(-1, H, C)
        a = jax.nn.leaky_relu(jnp.sum((xj + ee) * attn, axis=-1), NEG_SLOPE)
        m = jax.ops.segment_max(a, dst, num_segments=N)
        a = jnp.exp(a - m[dst])
        denom = jax.ops.segment_sum(a, dst, num_segments=N)
        a = a / (denom[dst] + 1e-16)
        msg = (xj * a[..., None]).reshape(-1, H * C)
        out = jax.ops.segment_sum(msg, dst, num_segments=N)
        return jax.nn.relu(out)
    edge_index = jnp.stack([src, dst])
    h = jnp.maximum(_layernorm(x, axis=-1), 0.0)
    x = x + _L0_gnn_ref(h, edge_index, L0_gnn_W1_l, L0_gnn_b1, L0_gnn_W1_r, L0_gnn_W2_l, L0_gnn_b2, L0_gnn_W2_r)
    h = jnp.maximum(_layernorm(x, axis=-1), 0.0)
    x = x + _L1_gnn_ref(h, edge_index, edge_attr_64, L1_gnn_W1, L1_gnn_b1, L1_gnn_W2, L1_gnn_b2, L1_gnn_Wg, L1_gnn_bg, L1_gnn_gamma, L1_gnn_beta)
    h = jnp.maximum(_layernorm(x, axis=-1), 0.0)
    x = x + _L2_gnn_ref(h, edge_index, L2_gnn_W1, L2_gnn_b1, L2_gnn_g1, L2_gnn_be1, L2_gnn_W2, L2_gnn_b2, L2_gnn_g2, L2_gnn_be2, L2_gnn_Wfc, L2_gnn_bfc)
    h = jnp.maximum(_layernorm(x, axis=-1), 0.0)
    x = x + _L3_gnn_ref(h, edge_index, edge_attr_128, L3_gnn_Wn, L3_gnn_bn, L3_gnn_We, L3_gnn_be, L3_gnn_attn)
    return x

_drawn_inputs = setup_inputs


def setup_inputs(seed=0):
    import zlib

    import numpy as np

    out = dict(_drawn_inputs(seed))
    spreads = {'L0_gnn_b1': (0.0, 0.1),
     'L0_gnn_b2': (0.0, 0.1),
     'L1_gnn_gamma': (1.0, 0.2),
     'L1_gnn_beta': (0.0, 0.1),
     'L2_gnn_b1': (0.0, 0.8),
     'L2_gnn_g1': (1.0, 0.2),
     'L2_gnn_be1': (0.0, 0.493),
     'L2_gnn_b2': (0.0, 0.8),
     'L2_gnn_g2': (1.0, 0.6),
     'L2_gnn_be2': (0.0, 0.8),
     'L2_gnn_bfc': (0.0, 0.1),
     'L3_gnn_bn': (0.0, 0.1),
     'L3_gnn_be': (0.0, 0.8)}
    factors = {'L1_gnn_bg': 8.0}
    for name, (base, spread) in spreads.items():
        noise = np.random.default_rng([zlib.crc32(name.encode()), seed]).standard_normal(out[name].shape)
        drawn = base * np.exp(spread * noise) if base else spread * noise
        out[name] = jnp.asarray(drawn.astype(out[name].dtype))
    for name, factor in factors.items():
        out[name] = (out[name] * factor).astype(out[name].dtype)
    return out
```

```python
import itertools
from contextlib import ExitStack

import concourse.bass as bass
from concourse import mybir

ALU = mybir.AluOpType
ACT = mybir.ActivationFunctionType
F32 = mybir.dt.float32
I32 = mybir.dt.int32
AX_X = mybir.AxisListType.X

P = 128
HALF = 4
BODY = 2 * HALF
EPS = 1e-5
FAR = 2.0 ** 20
BIG = 1e30
FLOOR = -1e29


CONSTANTS = 7
SCOPES = itertools.count()


def ceil_div(a, b):
    return -(-a // b)


class Core:
    pass


def scope(nc, ctx):
    n = next(SCOPES)

    def sb(name, shape, dt=F32):
        return ctx.enter_context(nc.sbuf_tensor(f"{name}_{n}", shape, dt))

    def ps(name, shape, dt=F32):
        return ctx.enter_context(nc.psum_tensor(f"{name}_{n}", shape, dt))

    sems = []

    def sem(name):
        sems.append(nc.alloc_semaphore(name))
        return sems[-1]

    def clear():
        if sems:
            nc.clear_and_free_semaphores(sems)
            nc.all_engine_barrier(sem_only=True)
    ctx.callback(clear)
    return sb, ps, sem


def hold(eng, held):
    eng.sem_inc(held, 1)


def chain(eng, sem, start=0):
    count = [0]

    def link(ins):
        count[0] += 1
        ins.then_inc(sem, 1)
        eng.wait_ge(sem, start + count[0])
    return link



def load_and_constants(nc, k, x):
    with ExitStack() as ctx:
        sb, ps, sem = scope(nc, ctx)
        zeroed, loaded, row_i = sem("x_pad_zeroed"), sem("x_loaded"), sb("row_i", [P, P], I32)
        made = k.constants_made
        block = ctx.enter_context(nc.Block())
        full = k.N // P
        rest = k.N - full * P

        @block.gpsimd
        def _(pool):
            pool.memset(k.X[:, full:k.NB, :], 0.0).then_inc(zeroed, 1)
            pool.memset(k.ones[:, :], 1.0).then_inc(made, 1)
            pool.memset(k.valid[:, :], 1.0).then_inc(made, 1)
            pool.memset(k.ident[:, :], 1.0).then_inc(made, 1)
            pool.iota(row_i[:, :], pattern=[[1, P]], base=0, channel_multiplier=0).then_inc(made, 1)
            pool.wait_ge(made, 4)
            pool.affine_select(out=k.ident[:, :], in_=k.ident[:, :], pattern=[[-1, P]], base=0,
                               channel_multiplier=1, compare_op=ALU.is_equal, fill=0.0).then_inc(made, 1)
            pool.affine_select(out=k.valid[:, :], in_=k.valid[:, :], pattern=[[0, P]], base=rest - 1,
                               channel_multiplier=-1, compare_op=ALU.is_ge, fill=0.0).then_inc(made, 1)
            pool.tensor_copy(k.iota[:, :], row_i[:, :]).then_inc(made, 1)
            pool.wait_ge(made, CONSTANTS)

        @block.sync
        def _(sp):
            sp.dma_start(k.X[:, 0:full, :], x[0:full * P, :].rearrange("(b p) d -> p b d", p=P)).then_inc(loaded, 16)
            sp.wait_ge(zeroed, 1)
            sp.dma_start(k.X[0:rest, full, :], x[full * P:k.N, :]).then_inc(loaded, 16)
            sp.wait_ge(loaded, 32)


def step_tables(nc, k, src, dst, tiles_dram):
    T, C = k.T, k.NSTEP_PAD // P
    full = k.E // P
    whole = full // P
    some = full - whole * P
    first_own = P - (k.E - full * P)
    assert T == full + 1 and C * P >= T + k.NBU - 1 and C == whole + 1
    with ExitStack() as ctx:
        sb, ps, sem = scope(nc, ctx)
        raw = sb("raw", [P, C, 2, P], I32)
        rows = sb("rows", [P, C, 2, P])
        lane_no_i = sb("lane_no_i", [P, P], I32)
        tile_no_i = sb("tile_no_i", [P, C], I32)
        all_no_i = sb("all_no_i", [P, C * P], I32)
        upto = sb("upto", [P, P])
        dup, dup2 = sb("dup", [P, P]), sb("dup2", [P, P])
        tile_no, all_no = sb("tile_no", [P, C]), sb("all_no", [P, C * P])
        lo, hi = sb("lo", [P, C]), sb("hi", [P, C])
        lo_i, hi_i = sb("lo_i", [P, C], I32), sb("hi_i", [P, C], I32)
        cnt, incl, start = sb("cnt", [P, C]), sb("incl", [P, C]), sb("start", [P, C])
        incl_r, start_r = sb("incl_r", [P, C * P]), sb("start_r", [P, C * P])
        junk = sb("junk", [P, C * P])
        t_of, b_of, t_of_i = sb("t_of", [P, C]), sb("b_of", [P, C]), sb("t_of_i", [P, C], I32)
        base, b_in, b128 = sb("base", [P, C]), sb("b_in", [P, C]), sb("b128", [P, C])
        picked = sb("picked", [P, C, 2 * P])
        p_small = ps("p_small", [P, 512])
        p_rows = ps("p_rows", [P, 2, 1024])
        cleared, loaded, consts, counted, summed = (sem(n) for n in ("tab_cleared", "tab_loaded", "tab_consts", "tab_counted", "tab_summed"))
        placed, spread, rows_ready, rows_stored = (sem(n) for n in ("tab_placed", "tab_spread", "tab_rows_ready", "tab_rows_stored"))
        steps_ready, gathered, rel_ready, turned, link_s = (sem(n) for n in ("tab_steps_ready", "tab_gathered", "tab_rel_ready", "tab_turned", "tab_dve_chain"))
        block = ctx.enter_context(nc.Block())

        @block.sync
        def _(sp):
            sp.wait_ge(cleared, 1)
            for i, a in enumerate((dst, src)):
                sp.dma_start(raw[:, 0:whole, i, :], a[0:whole * P * P].rearrange("(c p l) -> p c l", p=P, l=P)).then_inc(loaded, 16)
                sp.dma_start(raw[0:some, whole, i, :], a[whole * P * P:full * P].rearrange("(p l) -> p l", l=P)).then_inc(loaded, 16)
                sp.dma_start(raw[some:some + 1, whole, i, :], a[k.E - P:k.E].unsqueeze(0)).then_inc(loaded, 16)
            sp.wait_ge(rows_ready, 1)
            sp.dma_start(tiles_dram.rearrange("(c p) w -> p c w", p=P), rows[:, :, :, :].rearrange("p c a l -> p c (a l)")).then_inc(rows_stored, 16)

        @block.gpsimd
        def _(pool):
            pool.memset(raw[:, :, :, :], 0).then_inc(cleared, 1)
            pool.iota(lane_no_i[:, :], pattern=[[1, P]], base=0, channel_multiplier=P)
            pool.iota(tile_no_i[:, :], pattern=[[P, C]], base=0, channel_multiplier=1)
            pool.iota(all_no_i[:, :], pattern=[[1, C * P]], base=0, channel_multiplier=0)
            pool.memset(upto[:, :], 1.0).then_inc(consts, 1)
            pool.wait_ge(consts, 1)
            pool.affine_select(out=upto[:, :], in_=upto[:, :], pattern=[[1, P]], base=0,
                               channel_multiplier=-1, compare_op=ALU.is_ge, fill=0.0).then_inc(consts, 1)
            pool.wait_ge(rows_stored, 16)
            pool.wait_ge(steps_ready, 1)
            for c in range(C):
                pool.indirect_dma_start(out=picked[:, c, :], out_offset=None, in_=tiles_dram,
                                        in_offset=bass.IndirectOffsetOnAxis(ap=t_of_i[:, c:c + 1], axis=0)).then_inc(gathered, 16)

        @block.vector
        def _(v):
            link = chain(v, link_s)
            v.wait_ge(consts, 2)
            link(v.tensor_copy(dup[:, :], lane_no_i[:, :]))
            link(v.tensor_scalar(dup2[:, :], dup[:, :], float(some * P), FAR, ALU.is_ge, ALU.mult))
            link(v.tensor_scalar(dup[:, :], dup[:, :], float(some * P + first_own), None, ALU.is_lt))
            link(v.tensor_tensor(dup[:, :], dup[:, :], dup2[:, :], ALU.mult))
            link(v.tensor_copy(tile_no[:, :], tile_no_i[:, :]))
            link(v.tensor_copy(all_no[:, :], all_no_i[:, :]))
            v.wait_ge(loaded, 96)
            link(v.tensor_copy(rows[:, :, :, :], raw[:, :, :, :]))
            link(v.tensor_reduce(hi[:, :], rows[:, :, 0, :], AX_X, ALU.max))
            v.tensor_tensor(rows[:, whole, 0, :], rows[:, whole, 0, :], dup[:, :], ALU.add).then_inc(rows_ready, 1)
            v.wait_ge(rows_ready, 1)
            link(v.tensor_reduce(lo[:, :], rows[:, :, 0, :], AX_X, ALU.min))
            link(v.tensor_copy(hi_i[:, :], hi[:, :]))
            link(v.tensor_copy(lo_i[:, :], lo[:, :]))
            link(v.tensor_scalar(hi_i[:, :], hi_i[:, :], 7, None, ALU.arith_shift_right))
            link(v.tensor_scalar(lo_i[:, :], lo_i[:, :], 7, None, ALU.arith_shift_right))
            link(v.tensor_copy(hi[:, :], hi_i[:, :]))
            link(v.tensor_copy(lo[:, :], lo_i[:, :]))
            link(v.tensor_tensor(cnt[:, :], hi[:, :], lo[:, :], ALU.subtract))
            link(v.tensor_scalar(hi[:, :], tile_no[:, :], float(T), None, ALU.is_lt))
            v.scalar_tensor_tensor(cnt[:, :], cnt[:, :], 1.0, hi[:, :], ALU.add, ALU.mult).then_inc(counted, 1)
            v.wait_ge(counted, 1)
            v.wait_ge(summed, 1)
            link(v.tensor_copy(incl[:, :], p_small[:, 0:C]))
            link(v.tensor_tensor(start[:, :], cnt[:, :], incl[:, :], ALU.subtract))
            v.tensor_tensor(start[:, :], start[:, :], lo[:, :], ALU.add).then_inc(placed, 1)
            v.wait_ge(spread, 1)
            link(v.tensor_copy(incl_r[:, :], p_rows[:, 0, 0:C * P]))
            link(v.tensor_copy(start_r[:, :], p_rows[:, 1, 0:C * P]))
            for c in range(C):
                link(v.tensor_scalar(junk[:, :], incl_r[:, :], tile_no[:, c:c + 1], 0.0, ALU.is_le, ALU.add, accum_out=t_of[:, c:c + 1]))
            link(v.tensor_scalar(t_of[:, :], t_of[:, :], float(T - 1), None, ALU.min))
            for c in range(C):
                link(v.scalar_tensor_tensor(junk[:, :], all_no[:, :], t_of[:, c:c + 1], start_r[:, :], ALU.is_equal, ALU.mult, accum_out=b_of[:, c:c + 1]))
            v.tensor_copy(t_of_i[:, :], t_of[:, :]).then_inc(steps_ready, 1)
            link(v.tensor_tensor(b_of[:, :], b_of[:, :], tile_no[:, :], ALU.add))
            link(v.tensor_scalar(b128[:, :], b_of[:, :], float(P), None, ALU.mult))
            link(v.tensor_scalar(b_in[:, :], b_of[:, :], float(k.NB - 1), 0.0, ALU.min, ALU.max))
            link(v.tensor_scalar(base[:, :], t_of[:, :], float(P), float(k.E - P), ALU.mult, ALU.min))
            v.wait_ge(gathered, 16 * C)
            for c in range(C):
                v.tensor_scalar(picked[:, c, 0:P], picked[:, c, 0:P], b128[:, c:c + 1], None, ALU.subtract).then_inc(rel_ready, 1)
            v.wait_ge(turned, 1)
            link(v.tensor_copy(k.drelS[:, :], p_rows[:, 0, 0:C * P]))
            link(v.tensor_copy(k.srcS[:, :], p_rows[:, 1, 0:C * P]))
            v.tensor_copy(junk[:, 0:1], base[:, 0:1]).then_inc(rel_ready, 1)
            v.wait_ge(turned, 2)
            link(v.tensor_copy(k.baseT[0:1, :], p_rows[0:1, 0, 0:C * P]))
            link(v.tensor_copy(k.blkT[0:1, :], p_rows[0:1, 1, 0:C * P]))

        @block.tensor
        def _(pe):
            pe.wait_ge(consts, 2)
            pe.wait_ge(counted, 1)
            for c in range(C):
                last = pe.matmul(p_small[:, c:c + 1], upto[:, :], cnt[:, c:c + 1], start=True, stop=(c == 0))
                for d in range(c):
                    last = pe.matmul(p_small[:, c:c + 1], k.ones[:, :], cnt[:, d:d + 1], start=False, stop=(d == c - 1))
            last.then_inc(summed, 1)

            def spread_rows(i, a):
                for c in range(C):
                    last = pe.matmul(p_rows[:, i, c * P:(c + 1) * P], a[:, c:c + 1].to_broadcast([P, P]), k.ident[:, :], start=True, stop=True)
                return last
            pe.wait_ge(placed, 1)
            spread_rows(0, incl)
            spread_rows(1, start).then_inc(spread, 1)
            pe.wait_ge(rel_ready, C)
            for c in range(C):
                for i in range(2):
                    last = pe.transpose(p_rows[:, i, c * P:(c + 1) * P], picked[:, c, i * P:(i + 1) * P], k.ident[:, :])
            last.then_inc(turned, 1)
            pe.wait_ge(rel_ready, C + 1)
            spread_rows(0, base)
            spread_rows(1, b_in).then_inc(turned, 1)



def layer_norm_stats(nc, k, name, src_of, rstd, shift):
    with ExitStack() as ctx:
        sb, ps, sem = scope(nc, ctx)
        st = sb("st", [P, k.NB, 6])
        mean, half, var = sb("mean", [P, k.NB]), sb("half", [P, k.NB]), sb("var", [P, k.NB])
        stats, var_ready, std_ready, link_s = sem(f"{name}_stats"), sem(f"{name}_var_ready"), sem(f"{name}_std_ready"), sem(f"{name}_dve_chain")
        block = ctx.enter_context(nc.Block())

        @block.vector
        def _(v):
            link = chain(v, link_s)
            with v.Fori(0, k.NB // 2) as j:
                for u in range(2):
                    v.bn_stats(st[:, bass.ds(2 * j + u, 1), :].rearrange("p b s -> p (b s)"), src_of(2 * j + u)).then_inc(stats, 1)
            v.wait_ge(stats, k.NB)
            link(v.tensor_tensor(mean[:, :], st[:, :, 1], st[:, :, 4], ALU.add))
            link(v.tensor_tensor(half[:, :], st[:, :, 1], st[:, :, 4], ALU.subtract))
            link(v.tensor_tensor(var[:, :], st[:, :, 2], st[:, :, 5], ALU.add))
            link(v.tensor_scalar(half[:, :], half[:, :], 0.5, None, ALU.mult))
            link(v.tensor_tensor(half[:, :], half[:, :], half[:, :], ALU.mult))
            link(v.tensor_scalar(var[:, :], var[:, :], 1.0 / k.D, EPS, ALU.mult, ALU.add))
            v.tensor_tensor(var[:, :], var[:, :], half[:, :], ALU.add).then_inc(var_ready, 1)
            v.wait_ge(std_ready, 1)
            link(v.reciprocal(rstd[:, :], var[:, :]))
            link(v.scalar_tensor_tensor(shift[:, :], mean[:, :], -0.5, rstd[:, :], ALU.mult, ALU.mult))

        @block.scalar
        def _(act):
            act.wait_ge(var_ready, 1)
            act.activation(var[:, :], var[:, :], ACT.Sqrt).then_inc(std_ready, 1)


def norm_relu(nc, k, name, table=None):
    with ExitStack() as ctx:
        sb, ps, sem = scope(nc, ctx)
        rstd, shift = sb("rstd", [P, k.NB]), sb("shift", [P, k.NB])
        layer_norm_stats(nc, k, name, lambda b: k.X[:, bass.ds(b, 1), :].rearrange("p b d -> p (b d)"), rstd, shift)
        normed, ones_set, stored = sem(f"{name}_normed"), sem(f"{name}_ones_set"), sem(f"{name}_stored")
        with nc.Block() as block:
            @block.scalar
            def _(act):
                with act.Fori(0, k.NB // 2) as j:
                    for u in range(2):
                        b = 2 * j + u
                        act.activation(k.H[:, bass.ds(b, 1), 0:k.D], k.X[:, bass.ds(b, 1), :], ACT.Relu,
                                       bias=shift[:, bass.ds(b, 1)], scale=rstd[:, bass.ds(b, 1)]).then_inc(normed, 1)
                act.wait_ge(normed, k.NB)

            if table is not None:
                @block.gpsimd
                def _(pool):
                    pool.memset(k.H[:, :, k.D:k.D + 2], 1.0).then_inc(ones_set, 1)

                @block.sync
                def _(sp):
                    sp.wait_ge(normed, k.NB)
                    sp.wait_ge(ones_set, 1)
                    sp.dma_start(table.rearrange("(b p) w -> p b w", p=P), k.H[:, :, :]).then_inc(stored, 16)
                    sp.wait_ge(stored, 16)


def node_product(nc, k, name, loads, width, row, stage, finish):
    with ExitStack() as ctx:
        sb, ps, sem = scope(nc, ctx)
        dmas, weights, bias = loads(sb)
        chunks = len(weights)
        inb = [sb(f"in_rows{u}", [P, row]) for u in range(2)]
        turned = [sb(f"turned_sb{u}", [P, chunks * P]) for u in range(2)]
        p_turn = [ps(f"p_turn{u}", [P, chunks * P]) for u in range(2)]
        p_out = [ps(f"p_out{u}", [P, 512]) for u in range(2)]
        w_loaded = sem(f"{name}_w_loaded")
        staged = [sem(f"{name}_staged{u}") for u in range(2)]
        turned_p = [sem(f"{name}_turned{u}") for u in range(2)]
        copied = [sem(f"{name}_copied{u}") for u in range(2)]
        product = [sem(f"{name}_product{u}") for u in range(2)]
        finished = [sem(f"{name}_finished{u}") for u in range(2)]
        fin_engine, fin, extra = finish
        out_sb = [sb(f"out_sb{u}", [P, width]) for u in range(2)] if extra else None
        stored = [sem(f"{name}_stored{u}") for u in range(2)] if extra else None
        rounds = k.NB // 2
        block = ctx.enter_context(nc.Block())

        def stage_loop(eng, f):
            with eng.Fori(0, rounds) as j:
                for u in range(2):
                    eng.wait_ge(turned_p[u], j)
                    f(eng, inb[u], 2 * j + u).then_inc(staged[u], 1)

        def finish_one(eng, j, u):
            eng.wait_ge(product[u], j + 1)
            if extra:
                eng.wait_ge(stored[u], 16 * j)
            fin(eng, p_out[u], 2 * j + u, out_sb[u] if extra else None).then_inc(finished[u], 1)

        @block.sync
        def _(sp):
            for to, of in dmas:
                sp.dma_start(to, of).then_inc(w_loaded, 16)
            if extra:
                with sp.Fori(0, rounds) as j:
                    for u in range(2):
                        sp.wait_ge(finished[u], j + 1)
                        sp.dma_start(extra[bass.ds((2 * j + u) * P, P), :], out_sb[u][:, :]).then_inc(stored[u], 16)
                for u in range(2):
                    sp.wait_ge(stored[u], 16 * rounds)

        @block.tensor
        def _(pe):
            pe.wait_ge(w_loaded, 16 * len(dmas))
            with pe.Fori(0, rounds) as j:
                for u in range(2):
                    pe.wait_ge(staged[u], len(stage) * (j + 1))
                    pe.wait_ge(copied[u], j)
                    at = 0
                    for c, (K, _) in enumerate(weights):
                        last = pe.transpose(p_turn[u][0:K, c * P:(c + 1) * P], inb[u][:, at:at + K], k.ident[:, :])
                        at += K
                    last.then_inc(turned_p[u], 1)
                for u in range(2):
                    pe.wait_ge(copied[u], j + 1)
                    pe.wait_ge(finished[u], j)
                    for c, (K, w) in enumerate(weights):
                        last = pe.matmul(p_out[u][:, 0:width], turned[u][0:K, c * P:(c + 1) * P], w,
                                         start=(c == 0), stop=(c == chunks - 1 and bias is None))
                    if bias is not None:
                        last = pe.matmul(p_out[u][:, 0:width], k.ones[0:1, :], bias, start=False, stop=True)
                    last.then_inc(product[u], 1)

        Ks = [K for K, _ in weights]

        @block.scalar
        def _(act):
            with act.Fori(0, rounds) as j:
                for u in range(2):
                    act.wait_ge(turned_p[u], j + 1)
                    act.wait_ge(product[u], j)
                    n_full = sum(K == P for K in Ks)
                    last = act.copy(turned[u][:, 0:n_full * P], p_turn[u][:, 0:n_full * P])
                    for c, K in enumerate(Ks):
                        if K != P:
                            last = act.copy(turned[u][0:K, c * P:(c + 1) * P], p_turn[u][0:K, c * P:(c + 1) * P])
                    last.then_inc(copied[u], 1)
                if fin_engine == "scalar":
                    for u in range(2):
                        finish_one(act, j, u)
            if fin_engine == "scalar":
                for u in range(2):
                    act.wait_ge(finished[u], rounds)

        @block.gpsimd
        def _(pool):
            if "gpsimd" in stage:
                stage_loop(pool, stage["gpsimd"])

        @block.vector
        def _(v):
            with v.Fori(0, rounds) as j:
                if "vector" in stage:
                    for u in range(2):
                        v.wait_ge(turned_p[u], j)
                        stage["vector"](v, inb[u], 2 * j + u).then_inc(staged[u], 1)
                if fin_engine == "vector":
                    for u in range(2):
                        finish_one(v, j, u)
            if fin_engine == "vector":
                for u in range(2):
                    v.wait_ge(finished[u], rounds)


def rows_of(buf, b, lo, hi):
    return buf[:, bass.ds(b, 1), lo:hi].rearrange("p b d -> p (b d)")



def index_feed(act, k, idx, index_ready, gathered, j, h):
    act.wait_ge(gathered[h], 16 * HALF * j)
    act.copy(idx[:, h * HALF:(h + 1) * HALF], k.srcS[:, bass.ds(j * BODY + h * HALF, HALF)]).then_inc(index_ready[h], 1)


def gather_half(pool, k, table, G, idx, index_ready, rows_used, gathered, j, h):
    pool.wait_ge(index_ready[h], j + 1)
    pool.wait_ge(rows_used[h], j)
    hold(pool, k.held)
    for r in range(HALF):
        i = h * HALF + r
        pool.indirect_dma_start(out=G[:, i, :], out_offset=None, in_=table,
                                in_offset=bass.IndirectOffsetOnAxis(ap=idx[:, i:i + 1], axis=0)).then_inc(gathered[h], 16)


def pick_matrix(v, k, out, s, op=ALU.is_equal):
    return v.tensor_tensor(out, k.iota[:, :].unsqueeze(1).to_broadcast([P, HALF, P]),
                           k.drelS[:, bass.ds(s, HALF)].unsqueeze(2).to_broadcast([P, HALF, P]), op)


def blocks_of(eng, k, s):
    return [eng.value_load(k.blkT[0:1, bass.ds(s + r, 1)], min_val=0, max_val=k.NB - 1) for r in range(HALF)]


def sum_pass(nc, k, name, table, W, lo):
    with ExitStack() as ctx:
        sb, ps, sem = scope(nc, ctx)
        G = sb("G", [P, BODY, table.shape[1]])
        S = sb("S", [P, BODY, P])
        idx = sb("idx", [P, BODY], I32)
        psum = ps("p_sum", [P, BODY, 512])
        two = range(2)
        index_ready = [sem(f"{name}_index_ready{h}") for h in two]
        gathered = [sem(f"{name}_gathered{h}") for h in two]
        picks_ready = [sem(f"{name}_picks_ready{h}") for h in two]
        summed = [sem(f"{name}_summed{h}") for h in two]
        added = sem(f"{name}_added")
        block = ctx.enter_context(nc.Block())

        @block.scalar
        def _(act):
            with act.Fori(0, k.NSTEP // BODY) as j:
                for h in two:
                    index_feed(act, k, idx, index_ready, gathered, j, h)

        @block.gpsimd
        def _(pool):
            with pool.Fori(0, k.NSTEP // BODY) as j:
                for h in two:
                    gather_half(pool, k, table, G, idx, index_ready, summed, gathered, j, h)

        @block.tensor
        def _(pe):
            with pe.Fori(0, k.NSTEP // BODY) as j:
                for h in two:
                    pe.wait_ge(picks_ready[h], j + 1)
                    pe.wait_ge(gathered[h], 16 * HALF * (j + 1))
                    pe.wait_ge(added, j * BODY + (h + 1) * HALF)
                    for r in range(HALF):
                        i = h * HALF + r
                        last = pe.matmul(psum[:, i, 0:W], S[:, i, :], G[:, i, 0:W], start=True, stop=True)
                    last.then_inc(summed[h], 1)

        @block.vector
        def _(v):
            v.memset(k.AGG[:, :, lo:lo + W], 0.0).then_inc(added, BODY)
            with v.Fori(0, k.NSTEP // BODY) as j:
                for h in two:
                    v.wait_ge(summed[h], j)
                    pick_matrix(v, k, S[:, h * HALF:(h + 1) * HALF, :], j * BODY + h * HALF).then_inc(picks_ready[h], 1)
                for h in two:
                    b = blocks_of(v, k, j * BODY + h * HALF)
                    v.wait_ge(summed[h], j + 1)
                    for r in range(HALF):
                        i = h * HALF + r
                        v.wait_ge(added, BODY + j * BODY + i)
                        v.tensor_tensor(rows_of(k.AGG, b[r], lo, lo + W), rows_of(k.AGG, b[r], lo, lo + W),
                                        psum[:, i, 0:W], ALU.add).then_inc(added, 1)
            v.wait_ge(added, BODY + k.NSTEP)


def skewed(eng, bodies, ahead, behind):
    ahead(0, 0)
    with eng.Fori(0, bodies - 1) as j:
        ahead(j, 1)
        behind(j, 0)
        ahead(j + 1, 0)
        behind(j, 1)
    ahead(bodies - 1, 1)
    behind(bodies - 1, 0)
    behind(bodies - 1, 1)


def edge_mlp_pass(nc, k, name, table, ea, W1, Wg, W2, b2):
    D, A = k.D, ea.shape[1]
    bodies = k.NSTEP // BODY
    with ExitStack() as ctx:
        sb, ps, sem = scope(nc, ctx)
        G = sb("G", [P, BODY, 2 * D])
        S = sb("S", [P, HALF, P])
        idx = sb("idx", [P, BODY], I32)
        ea_in = sb("ea_in", [P, BODY, A])
        eaT = sb("eaT", [A, HALF * P])
        coreT = sb("coreT", [P, 2, HALF * P])
        gate = sb("gate", [P, HALF, D])
        msg = sb("msg", [P, HALF, D])
        w1b, wgb, w2 = sb("w1b", [A, D]), sb("wgb", [A, D]), sb("w2", [P, 2, D])
        b2r = sb("b2r", [1, D])
        p_eaT = ps("p_eaT", [A, HALF * P])
        p_coreT = ps("p_coreT", [P, 2, HALF * P])
        p_gate = ps("p_gate", [P, HALF, D])
        p_core = ps("p_core", [P, HALF, D])
        p_sum = ps("p_sum", [P, 2, D])
        two = range(2)
        index_ready = [sem(f"{name}_index_ready{h}") for h in two]
        gathered = [sem(f"{name}_gathered{h}") for h in two]
        ea_loaded = [sem(f"{name}_ea_loaded{h}") for h in two]
        ea_turned = [sem(f"{name}_ea_turned{h}") for h in two]
        gate_in = [sem(f"{name}_gate_in{h}") for h in two]
        (w_loaded, ea_copied, core_in, core_relu, gate_out, core_out, msg_ready,
         picks_ready, pair_summed, added) = (sem(f"{name}_{n}") for n in (
             "w_loaded", "ea_copied", "core_in", "core_relu", "gate_out", "core_out",
             "msg_ready", "picks_ready", "pair_summed", "added"))
        block = ctx.enter_context(nc.Block())

        @block.sync
        def _(sp):
            for to, of in ((w1b[:, :], W1[D:D + A, :]), (wgb[:, :], Wg[D:D + A, :]),
                           (w2[:, :, :], W2.rearrange("(c p) n -> p c n", p=P)), (b2r[:, :], b2.unsqueeze(0))):
                sp.dma_start(to, of).then_inc(w_loaded, 16)
            with sp.Fori(0, bodies) as j:
                for h in two:
                    sp.wait_ge(ea_turned[h], j)
                    load_attributes(sp, k, ea, ea_in, ea_loaded, j, h)
            for h in two:
                sp.wait_ge(ea_loaded[h], 16 * HALF * bodies)

        @block.gpsimd
        def _(pool):
            with pool.Fori(0, bodies) as j:
                for h in two:
                    gather_half(pool, k, table, G, idx, index_ready, gate_in, gathered, j, h)

        @block.tensor
        def _(pe):
            def inputs(j, h):
                n = 2 * j + h
                pe.wait_ge(ea_loaded[h], 16 * HALF * (j + 1))
                pe.wait_ge(ea_copied, n)
                hold(pe, k.held_pe)
                for r in range(HALF):
                    last = pe.transpose(p_eaT[:, r * P:(r + 1) * P], ea_in[:, h * HALF + r, :], k.ident[:, :])
                last.then_inc(ea_turned[h], 1)
                pe.wait_ge(ea_copied, n + 1)
                pe.wait_ge(gathered[h], 16 * HALF * (j + 1))
                pe.wait_ge(core_relu, n)
                for f in range(2):
                    pe.matmul(p_coreT[:, f, :], w1b[:, f * P:(f + 1) * P], eaT[:, :], start=True, stop=True)
                    for r in range(HALF):
                        last = pe.matmul(p_coreT[:, f, r * P:(r + 1) * P], G[:, h * HALF + r, f * P:(f + 1) * P],
                                         k.ident[:, :], start=False, stop=True, skip_group_check=True)
                last.then_inc(core_in, 1)
                pe.wait_ge(gate_out, n)
                for r in range(HALF):
                    pe.matmul(p_gate[:, r, :], eaT[:, r * P:(r + 1) * P], wgb[:, :], start=True, stop=False)
                    last = pe.matmul(p_gate[:, r, :], k.ident[:, :], G[:, h * HALF + r, D:2 * D], start=False, stop=True)
                last.then_inc(gate_in[h], 1)

            def outputs(j, h):
                n = 2 * j + h
                pe.wait_ge(core_relu, n + 1)
                pe.wait_ge(msg_ready, n)
                for r in range(HALF):
                    for f in range(2):
                        pe.matmul(p_core[:, r, :], coreT[:, f, r * P:(r + 1) * P], w2[:, f, :], start=(f == 0), stop=False)
                    last = pe.matmul(p_core[:, r, :], k.ones[0:1, :], b2r[:, :], start=False, stop=True)
                last.then_inc(core_out, 1)
                pe.wait_ge(msg_ready, n + 1)
                pe.wait_ge(picks_ready, n + 1)
                for q in range(2):
                    pe.wait_ge(added, n * HALF + 2 * q + 2)
                    for r in (2 * q, 2 * q + 1):
                        last = pe.matmul(p_sum[:, r % 2, :], S[:, r, :], msg[:, r, :], start=True, stop=True)
                    last.then_inc(pair_summed, 1)

            pe.wait_ge(w_loaded, 64)
            skewed(pe, bodies, inputs, outputs)

        @block.scalar
        def _(act):
            for h in two:
                index_feed(act, k, idx, index_ready, gathered, 0, h)
            with act.Fori(0, bodies) as j:
                for h in two:
                    n = 2 * j + h
                    act.wait_ge(ea_turned[h], j + 1)
                    act.wait_ge(gate_in[1 - h], j + h)
                    act.copy(eaT[:, :], p_eaT[:, :]).then_inc(ea_copied, 1)
                    act.wait_ge(core_in, n + 1)
                    act.wait_ge(core_out, n)
                    act.activation(coreT[:, 0, :], p_coreT[:, 0, :], ACT.Relu)
                    act.activation(coreT[:, 1, :], p_coreT[:, 1, :], ACT.Relu).then_inc(core_relu, 1)
                    index_feed(act, k, idx, index_ready, gathered, j + 1, h)
                    act.wait_ge(gate_in[h], j + 1)
                    act.wait_ge(msg_ready, n)
                    act.activation(gate[:, 0:2, :], p_gate[:, 0:2, :], ACT.Sigmoid)
                    act.activation(gate[:, 2:4, :], p_gate[:, 2:4, :], ACT.Sigmoid).then_inc(gate_out, 1)

        @block.vector
        def _(v):
            v.memset(k.AGG[:, :, 0:D], 0.0).then_inc(added, 2)
            with v.Fori(0, bodies) as j:
                for h in two:
                    n = 2 * j + h
                    v.wait_ge(pair_summed, 2 * n)
                    pick_matrix(v, k, S[:, :, :], j * BODY + h * HALF).then_inc(picks_ready, 1)
                    b = blocks_of(v, k, j * BODY + h * HALF)
                    v.wait_ge(core_out, n + 1)
                    v.wait_ge(gate_out, n + 1)
                    v.tensor_tensor(msg[:, 0:2, :], p_core[:, 0:2, :], gate[:, 0:2, :], ALU.mult)
                    v.tensor_tensor(msg[:, 2:4, :], p_core[:, 2:4, :], gate[:, 2:4, :], ALU.mult).then_inc(msg_ready, 1)
                    for r in range(HALF):
                        if r % 2 == 0:
                            v.wait_ge(pair_summed, 2 * n + r // 2 + 1)
                        v.wait_ge(added, 2 + n * HALF + r)
                        v.tensor_tensor(rows_of(k.AGG, b[r], 0, D), rows_of(k.AGG, b[r], 0, D), p_sum[:, r % 2, :],
                                        ALU.add).then_inc(added, 1)
            v.wait_ge(added, 2 + k.NSTEP)


def load_attributes(sp, k, ea, ea_in, ea_loaded, j, h):
    for r in range(HALF):
        i = h * HALF + r
        at = sp.value_load(k.baseT[0:1, bass.ds(j * BODY + i, 1)], min_val=0, max_val=k.E - P)
        sp.dma_start(ea_in[:, i, :], ea[bass.ds(at, P), :]).then_inc(ea_loaded[h], 16)


def attention_pass(nc, k, name, table, ea, v_row):
    D, A = k.D, ea.shape[1]
    W = D + 1
    bodies = k.NSTEP // BODY
    with ExitStack() as ctx:
        sb, ps, sem = scope(nc, ctx)
        G = sb("G", [P, BODY, D + 2])
        idx = sb("idx", [P, BODY], I32)
        ea_in = sb("ea_in", [P, BODY, A])
        other = sb("other", [P, HALF, P])
        masked = sb("masked", [P, 2, HALF, P])
        weight = sb("weight", [P, 2, HALF, P])
        top = sb("top", [P, k.NB])
        junk = sb("junk", [P, HALF, A])
        dot, logit = sb("dot", [P, HALF]), sb("logit", [P, HALF])
        step_top, old, new = sb("step_top", [P, HALF]), sb("old", [P, HALF]), sb("new", [P, HALF])
        minus, drop, scale = sb("minus", [P, 2, HALF]), sb("drop", [P, HALF]), sb("scale", [P, 2, HALF])
        p_turn = ps("p_turn", [P, HALF, P])
        p_shift = ps("p_shift", [P, HALF, P])
        p_sum = ps("p_sum", [P, HALF, 512])
        two = range(2)
        index_ready = [sem(f"{name}_index_ready{h}") for h in two]
        gathered = [sem(f"{name}_gathered{h}") for h in two]
        ea_loaded = [sem(f"{name}_ea_loaded{h}") for h in two]
        masked_ready = [sem(f"{name}_masked_ready{h}") for h in two]
        summed = [sem(f"{name}_summed{h}") for h in two]
        (turned, top_ready, drop_ready, scale_ready, shifted, weight_ready, added, link_s) = (sem(f"{name}_{n}") for n in (
            "turned", "top_ready", "drop_ready", "scale_ready", "shifted", "weight_ready", "added", "dve_chain"))
        block = ctx.enter_context(nc.Block())

        @block.sync
        def _(sp):
            with sp.Fori(0, bodies) as j:
                for h in two:
                    sp.wait_ge(masked_ready[h], j)
                    load_attributes(sp, k, ea, ea_in, ea_loaded, j, h)
            for h in two:
                sp.wait_ge(ea_loaded[h], 16 * HALF * bodies)

        @block.gpsimd
        def _(pool):
            with pool.Fori(0, bodies) as j:
                for h in two:
                    gather_half(pool, k, table, G, idx, index_ready, summed, gathered, j, h)

        @block.tensor
        def _(pe):
            def turn_then_shift(j, h, part):
                n = 2 * j + h
                if part == 0:
                    pe.wait_ge(masked_ready[h], j + 1)
                    pe.wait_ge(top_ready, n)
                    for r in range(HALF):
                        last = pe.transpose(p_turn[:, r, :], masked[:, h, r, :], k.ident[:, :])
                    last.then_inc(turned, 1)
                else:
                    pe.wait_ge(drop_ready, n + 1)
                    pe.wait_ge(weight_ready, n)
                    for r in range(HALF):
                        pe.matmul(p_shift[:, r, :], k.ident[:, :], masked[:, h, r, :], start=True, stop=False)
                        last = pe.matmul(p_shift[:, r, :], minus[:, h, r:r + 1].to_broadcast([P, P]), k.ident[:, :], start=False, stop=True)
                    last.then_inc(shifted, 1)

            def sums(j, h):
                n = 2 * j + h
                pe.wait_ge(weight_ready, n + 1)
                pe.wait_ge(added, n * HALF + HALF)
                for r in range(HALF):
                    last = pe.matmul(p_sum[:, r, 0:W], weight[:, h, r, :], G[:, h * HALF + r, 0:W], start=True, stop=True)
                last.then_inc(summed[h], 1)

            turn_then_shift(0, 0, 0)
            turn_then_shift(0, 0, 1)
            with pe.Fori(0, bodies - 1) as j:
                for now, then in (((j, 0), (j, 1)), ((j, 1), (j + 1, 0))):
                    turn_then_shift(*then, 0)
                    sums(*now)
                    turn_then_shift(*then, 1)
            turn_then_shift(bodies - 1, 1, 0)
            sums(bodies - 1, 0)
            turn_then_shift(bodies - 1, 1, 1)
            sums(bodies - 1, 1)

        @block.scalar
        def _(act):
            for h in two:
                index_feed(act, k, idx, index_ready, gathered, 0, h)
            with act.Fori(0, bodies) as j:
                for h in two:
                    n = 2 * j + h
                    act.wait_ge(drop_ready, n + 1)
                    act.wait_ge(added, n * HALF)
                    act.activation(scale[:, h, :], drop[:, :], ACT.Exp).then_inc(scale_ready, 1)
                    act.wait_ge(shifted, n + 1)
                    act.wait_ge(summed[h], j)
                    act.activation(weight[:, h, :, :], p_shift[:, :, :], ACT.Exp).then_inc(weight_ready, 1)
                    index_feed(act, k, idx, index_ready, gathered, j + 1, h)

        @block.vector
        def _(v):
            v.memset(top[:, :], FLOOR)
            v.memset(k.AGG[:, :, 0:W], 0.0).then_inc(added, HALF)
            v.wait_ge(added, HALF)
            links = 4 + HALF

            def weights(j, h):
                n = 2 * j + h
                link = chain(v, link_s, n * links)
                v.wait_ge(gathered[h], 16 * HALF * (j + 1))
                v.wait_ge(ea_loaded[h], 16 * HALF * (j + 1))
                for r in range(HALF):
                    i = h * HALF + r
                    ins = v.tensor_tensor_reduce(junk[:, r, :], ea_in[:, i, :], v_row, 1.0, G[:, i, D + 1:D + 2],
                                                 ALU.mult, ALU.add, dot[:, r:r + 1])
                link(ins)
                link(v.scalar_tensor_tensor(logit[:, :], dot[:, :], 0.01, dot[:, :], ALU.mult, ALU.max))
                link(pick_matrix(v, k, other[:, :, :], j * BODY + h * HALF, ALU.not_equal))
                v.scalar_tensor_tensor(masked[:, h, :, :], other[:, :, :], -BIG,
                                       logit[:, :].unsqueeze(2).to_broadcast([P, HALF, P]), ALU.mult, ALU.add).then_inc(masked_ready[h], 1)
                b = blocks_of(v, k, j * BODY + h * HALF)
                v.wait_ge(turned, n + 1)
                v.tensor_reduce(step_top[:, :], p_turn[:, :, :], AX_X, ALU.max).then_inc(top_ready, 1)
                v.wait_ge(top_ready, n + 1)
                for r in range(HALF):
                    v.tensor_scalar(old[:, r:r + 1], top[:, bass.ds(b[r], 1)], 1.0, None, ALU.mult)
                    link(v.tensor_tensor(top[:, bass.ds(b[r], 1)], top[:, bass.ds(b[r], 1)], step_top[:, r:r + 1], ALU.max))
                    ins = v.tensor_scalar(new[:, r:r + 1], top[:, bass.ds(b[r], 1)], 1.0, None, ALU.mult)
                link(ins)
                v.wait_ge(scale_ready, n)
                v.tensor_tensor(drop[:, :], old[:, :], new[:, :], ALU.subtract)
                v.tensor_scalar(minus[:, h, :], new[:, :], -1.0, None, ALU.mult).then_inc(drop_ready, 1)

            def add(j, h):
                n = 2 * j + h
                b = blocks_of(v, k, j * BODY + h * HALF)
                v.wait_ge(scale_ready, n + 1)
                v.wait_ge(summed[h], j + 1)
                for r in range(HALF):
                    v.wait_ge(added, HALF + n * HALF + r)
                    v.scalar_tensor_tensor(rows_of(k.AGG, b[r], 0, W), rows_of(k.AGG, b[r], 0, W), scale[:, h, r:r + 1],
                                           p_sum[:, r, 0:W], ALU.mult, ALU.add).then_inc(added, 1)

            skewed(v, bodies, weights, add)
            v.wait_ge(added, HALF + k.NSTEP)



def wide(a, n):
    return a.unsqueeze(2).to_broadcast([P, a.shape[1], n])


def every_block(a, nb):
    return a.unsqueeze(1).to_broadcast([P, nb, a.shape[1]])


def store_table(nc, k, name, table, of):
    with ExitStack() as ctx:
        sb, ps, sem = scope(nc, ctx)
        stored = sem(f"{name}_stored")
        with nc.Block() as block:
            @block.sync
            def _(sp):
                sp.dma_start(table.rearrange("(b p) w -> p b w", p=P), of).then_inc(stored, 16)
                sp.wait_ge(stored, 16)


def degrees(nc, k):
    with ExitStack() as ctx:
        sb, ps, sem = scope(nc, ctx)
        deg, plus = sb("deg", [P, k.NB]), sb("plus", [P, k.NB])
        link_s, plus_ready, root_ready = sem("deg_dve_chain"), sem("deg_plus_ready"), sem("deg_root_ready")
        with nc.Block() as block:
            @block.vector
            def _(v):
                link = chain(v, link_s)
                link(v.tensor_scalar(deg[:, :], k.AGG[:, :, k.D], 1.0, None, ALU.max))
                v.tensor_scalar(plus[:, :], k.AGG[:, :, k.D], 1.0, None, ALU.add).then_inc(plus_ready, 1)
                v.reciprocal(k.rdeg[:, :], deg[:, :])
                v.wait_ge(root_ready, 1)
                link(v.reciprocal(k.dinv[:, :], plus[:, :]))

            @block.scalar
            def _(act):
                act.wait_ge(plus_ready, 1)
                act.activation(plus[:, :], plus[:, :], ACT.Sqrt).then_inc(root_ready, 1)


def gated_output(nc, k, gamma, beta):
    D = k.D
    with ExitStack() as ctx:
        sb, ps, sem = scope(nc, ctx)
        rstd, shift = sb("rstd", [P, k.NB]), sb("shift", [P, k.NB])
        gam, bet = sb("gam", [P, D]), sb("bet", [P, D])
        with ExitStack() as first:
            loaded, summed = sem("gout_loaded"), sem("gout_summed")
            block = first.enter_context(nc.Block())

            @block.sync
            def _(sp):
                sp.dma_start(gam[:, :], gamma.partition_broadcast(P)).then_inc(loaded, 16)
                sp.dma_start(bet[:, :], beta.partition_broadcast(P)).then_inc(loaded, 16)
                sp.wait_ge(loaded, 32)

            @block.vector
            def _(v):
                v.tensor_tensor(k.AGG[:, :, 0:D], k.AGG[:, :, 0:D], k.H[:, :, 0:D], ALU.add).then_inc(summed, 1)
                v.wait_ge(summed, 1)
        layer_norm_stats(nc, k, "gout", lambda b: rows_of(k.AGG, b, 0, D), rstd, shift)
        normed, link_s = sem("gout_normed"), sem("gout_chain")
        with nc.Block() as block:
            @block.scalar
            def _(act):
                with act.Fori(0, k.NB // 2) as j:
                    for u in range(2):
                        b = 2 * j + u
                        act.activation(rows_of(k.AGG, b, 0, D), rows_of(k.AGG, b, 0, D), ACT.Identity,
                                       bias=shift[:, bass.ds(b, 1)], scale=rstd[:, bass.ds(b, 1)]).then_inc(normed, 1)

            @block.vector
            def _(v):
                link = chain(v, link_s)
                v.wait_ge(normed, k.NB)
                for op, row in ((ALU.mult, gam), (ALU.add, bet)):
                    link(v.tensor_tensor(k.AGG[:, :, 0:D], k.AGG[:, :, 0:D], every_block(row[:, :], k.NB), op))
                link(v.tensor_tensor(k.X[:, :, :], k.X[:, :, :], k.AGG[:, :, 0:D], ALU.add))


def graph_norm(nc, k, name, lo, W, own, b, gain, beta):
    nbu, rest = k.NBU, k.N - (k.NBU - 1) * P
    Z, T = k.AGG[:, :, lo:lo + W], k.AGG[:, :, own:own + W]
    with ExitStack() as ctx:
        sb, ps, sem = scope(nc, ctx)
        b_row, g_row, be_row = sb("b_row", [P, W]), sb("g_row", [P, W]), sb("be_row", [P, W])
        mean, var, rstd = sb("mean_row", [P, W]), sb("var_row", [P, W]), sb("rstd_row", [P, W])
        p_mean, p_var = ps("p_mean", [P, 512]), ps("p_var", [P, 512])
        loaded, z_ready, sq_ready, col_sums, link_s, var_ready, std_ready = (sem(f"{name}_{n}") for n in (
            "loaded", "z_ready", "squares_ready", "column_sums", "dve_chain", "var_ready", "std_ready"))
        block = ctx.enter_context(nc.Block())

        @block.sync
        def _(sp):
            for to, of in ((b_row, b), (g_row, gain), (be_row, beta)):
                sp.dma_start(to[:, :], of.partition_broadcast(P)).then_inc(loaded, 16)

        @block.tensor
        def _(pe):
            for i, (psum, at) in enumerate(((p_mean, lo), (p_var, own))):
                pe.wait_ge((z_ready, sq_ready)[i], 1)
                pe.matmul(psum[:, 0:W], k.ones[:, :], k.AGG[:, 0, at:at + W], start=True, stop=False)
                with pe.Fori(1, nbu - 1) as m:
                    pe.matmul(psum[:, 0:W], k.ones[:, :], rows_of(k.AGG, m, at, at + W), start=False, stop=False)
                pe.matmul(psum[:, 0:W], k.valid[:, :], k.AGG[:, nbu - 1, at:at + W], start=False, stop=True).then_inc(col_sums, 1)

        @block.scalar
        def _(act):
            act.wait_ge(var_ready, 1)
            act.activation(var[:, :], var[:, :], ACT.Sqrt).then_inc(std_ready, 1)

        @block.vector
        def _(v):
            link = chain(v, link_s)
            link(v.tensor_tensor(Z, Z, T, ALU.add))
            link(v.tensor_tensor(Z, Z, wide(k.dinv[:, :], W), ALU.mult))
            v.wait_ge(loaded, 48)
            v.tensor_tensor(Z, Z, every_block(b_row[:, :], k.NB), ALU.add).then_inc(z_ready, 1)
            v.wait_ge(col_sums, 1)
            link(v.tensor_scalar(mean[:, :], p_mean[:, 0:W], 1.0 / k.N, None, ALU.mult))
            link(v.tensor_tensor(Z, Z, every_block(mean[:, :], k.NB), ALU.subtract))
            v.tensor_tensor(T, Z, Z, ALU.mult).then_inc(sq_ready, 1)
            v.wait_ge(col_sums, 2)
            v.tensor_scalar(var[:, :], p_var[:, 0:W], 1.0 / k.N, EPS, ALU.mult, ALU.add).then_inc(var_ready, 1)
            v.wait_ge(std_ready, 1)
            link(v.reciprocal(rstd[:, :], var[:, :]))
            link(v.tensor_tensor(rstd[:, :], rstd[:, :], g_row[:, :], ALU.mult))
            link(v.tensor_tensor(Z, Z, every_block(rstd[:, :], k.NB), ALU.mult))
            link(v.tensor_tensor(Z, Z, every_block(be_row[:, :], k.NB), ALU.add))
            link(v.tensor_scalar(Z, Z, 0.0, None, ALU.max))


def attention_constants(nc, k, attn, We, be, v_row, attn_row, const):
    D, A = We.shape
    with ExitStack() as ctx:
        sb, ps, sem = scope(nc, ctx)
        a_col, be_col = sb("a_col", [P, D // P]), sb("be_col", [P, D // P])
        we = sb("we", [P, D // P, A])
        p_v = ps("p_v", [P, 512])
        loaded, made, copied = sem("att_loaded"), sem("att_made"), sem("att_copied")
        block = ctx.enter_context(nc.Block())
        flat = attn.rearrange("a h c -> (a h c)")

        @block.sync
        def _(sp):
            for c in range(D // P):
                sp.dma_start(a_col[:, c:c + 1], flat[c * P:(c + 1) * P].unsqueeze(1)).then_inc(loaded, 16)
                sp.dma_start(be_col[:, c:c + 1], be[c * P:(c + 1) * P].unsqueeze(1)).then_inc(loaded, 16)
            sp.dma_start(we[:, :, :], We.rearrange("(c p) n -> p c n", p=P)).then_inc(loaded, 16)
            sp.dma_start(attn_row[:, :], flat.partition_broadcast(P)).then_inc(loaded, 16)

        @block.tensor
        def _(pe):
            pe.wait_ge(loaded, 16 * (2 * (D // P) + 2))
            for c in range(D // P):
                pe.matmul(p_v[:, 0:A], a_col[:, c:c + 1].to_broadcast([P, P]), we[:, c, :], start=(c == 0), stop=(c == D // P - 1))
            for c in range(D // P):
                last = pe.matmul(p_v[:, A:A + 1], a_col[:, c:c + 1].to_broadcast([P, P]), be_col[:, c:c + 1],
                                 start=(c == 0), stop=(c == D // P - 1))
            last.then_inc(made, 1)

        @block.vector
        def _(v):
            v.wait_ge(made, 1)
            v.tensor_copy(v_row[:, :], p_v[:, 0:A]).then_inc(copied, 1)
            v.tensor_copy(const[:, :], p_v[:, A:A + 1]).then_inc(copied, 1)
            v.wait_ge(copied, 2)


def attention_output(nc, k, out):
    D = k.D
    full, rest = k.N // P, k.N - k.N // P * P
    with ExitStack() as ctx:
        sb, ps, sem = scope(nc, ctx)
        rden = sb("rden", [P, k.NB])
        link_s, done, stored = sem("out_dve_chain"), sem("out_done"), sem("out_stored")
        block = ctx.enter_context(nc.Block())

        @block.vector
        def _(v):
            link = chain(v, link_s)
            link(v.tensor_scalar(rden[:, :], k.AGG[:, :, D], 1e-16, None, ALU.add))
            link(v.reciprocal(rden[:, :], rden[:, :]))
            link(v.tensor_tensor(k.AGG[:, :, 0:D], k.AGG[:, :, 0:D], wide(rden[:, :], D), ALU.mult))
            v.scalar_tensor_tensor(k.X[:, :, :], k.AGG[:, :, 0:D], 0.0, k.X[:, :, :], ALU.max, ALU.add).then_inc(done, 1)

        @block.sync
        def _(sp):
            sp.wait_ge(done, 1)
            sp.dma_start(out[0:full * P, :].rearrange("(b p) d -> p b d", p=P), k.X[:, 0:full, :]).then_inc(stored, 16)
            sp.dma_start(out[full * P:k.N, :], k.X[0:rest, full, :]).then_inc(stored, 16)
            sp.wait_ge(stored, 32)



def gnn(nc, x, src, dst, edge_attr_128, edge_attr_64,
        L0_W1_l, L0_b1, L0_W1_r, L0_W2_l, L0_b2, L0_W2_r,
        L1_W1, L1_b1, L1_W2, L1_b2, L1_Wg, L1_bg, L1_gamma, L1_beta,
        L2_W1, L2_b1, L2_g1, L2_be1, L2_W2, L2_b2, L2_g2, L2_be2, L2_Wfc, L2_bfc,
        L3_Wn, L3_bn, L3_We, L3_be, L3_attn, out):
    k = Core()
    k.N, k.D = x.shape
    k.E = src.shape[0]
    k.T = ceil_div(k.E, P)
    k.NBU = ceil_div(k.N, P)
    k.NB = k.NBU + k.NBU % 2
    k.NSTEP = ceil_div(k.T + k.NBU - 1, BODY) * BODY
    k.NSTEP_PAD = ceil_div(k.NSTEP + BODY, P) * P
    D, NB = k.D, k.NB
    d1, d2 = L2_W1.shape[1], L2_W2.shape[1]
    rows = NB * P

    def dram(name, w, n=rows):
        return nc.dram_tensor(name, [n, w], F32, kind="Internal").ap()

    table_h0, table_h1 = dram("table_h0", D + 2), dram("table_h1", D + 2)
    table_mlp, table_g1, table_g2 = dram("table_mlp", 2 * D), dram("table_g1", d1), dram("table_g2", d2)
    table_att = dram("table_att", D + 2)
    tiles_dram = dram("tiles_dram", 2 * P, k.NSTEP_PAD)

    with ExitStack() as ctx:
        sb, ps, sem = scope(nc, ctx)
        k.X = sb("X", [P, NB, D])
        k.srcS, k.drelS = sb("srcS", [P, k.NSTEP_PAD], I32), sb("drelS", [P, k.NSTEP_PAD])
        k.baseT, k.blkT = sb("baseT", [1, k.NSTEP_PAD], I32), sb("blkT", [1, k.NSTEP_PAD], I32)
        k.ident, k.iota, k.ones, k.valid = sb("ident", [P, P]), sb("iota", [P, P]), sb("ones", [P, P]), sb("valid", [P, P])
        k.rdeg, k.dinv = sb("rdeg", [P, NB]), sb("dinv", [P, NB])

        k.constants_made = sem("constants_made")
        k.held, k.held_pe = sem("held_pool"), sem("held_pe")
        load_and_constants(nc, k, x)
        step_tables(nc, k, src, dst, tiles_dram)
        k.H = sb("H", [P, NB, D + 2])
        k.AGG = sb("AGG", [P, NB, D + 1])

        def matrix(sb, name, w):
            K, n = w.shape
            dmas, pieces = [], []
            for c in range(ceil_div(K, P)):
                rows_c = min(P, K - c * P)
                t = sb(f"{name}{c}", [P, n])
                dmas.append((t[0:rows_c, :], w[c * P:c * P + rows_c, :]))
                pieces.append((rows_c, t[0:rows_c, :]))
            return dmas, pieces

        def bias_row(sb, b):
            t = sb("bias_row", [1, b.shape[0]])
            return [(t[:, :], b.unsqueeze(0))], t[:, :]

        norm_relu(nc, k, "ln0", table_h0)
        sum_pass(nc, k, "sage1", table_h0, D + 1, 0)
        degrees(nc, k)

        def sage(name, Wl, b, Wr, finish):
            def loads(sb):
                d1_, p1 = matrix(sb, "wl", Wl)
                d2_, p2 = matrix(sb, "wr", Wr)
                d3_, bias = bias_row(sb, b)
                return d1_ + d2_ + d3_, p1 + p2, bias

            def mean(v, buf, blk):
                return v.tensor_scalar(buf[:, 0:D], rows_of(k.AGG, blk, 0, D), k.rdeg[:, bass.ds(blk, 1)], None, ALU.mult)

            def own(pool, buf, blk):
                return pool.tensor_copy(buf[:, D:2 * D], rows_of(k.H, blk, 0, D))
            node_product(nc, k, name, loads, D, 2 * D, {"vector": mean, "gpsimd": own}, finish)

        sage("sage1_out", L0_W1_l, L0_b1, L0_W1_r,
             ("scalar", lambda act, p, blk, o: act.activation(rows_of(k.H, blk, 0, D), p[:, 0:D], ACT.Relu), None))
        store_table(nc, k, "h1", table_h1, k.H[:, :, :])
        sum_pass(nc, k, "sage2", table_h1, D, 0)

        def add_to_x(v, p, blk, o):
            return v.tensor_tensor(rows_of(k.X, blk, 0, D), p[:, 0:D], rows_of(k.X, blk, 0, D), ALU.add)
        sage("sage2_out", L0_W2_l, L0_b2, L0_W2_r, ("vector", add_to_x, None))

        def own_h(pool, buf, blk):
            return pool.tensor_copy(buf[:, 0:D], rows_of(k.H, blk, 0, D))

        norm_relu(nc, k, "ln1")

        def mlp_loads(sb):
            both = [sb(f"w1g{c}", [P, 2 * D]) for c in range(D // P)]
            brow = sb("b1g", [1, 2 * D])
            dmas = [(both[c][:, i * D:(i + 1) * D], w[c * P:(c + 1) * P, :])
                    for c in range(D // P) for i, w in enumerate((L1_W1, L1_Wg))]
            dmas += [(brow[:, i * D:(i + 1) * D], b.unsqueeze(0)) for i, b in enumerate((L1_b1, L1_bg))]
            return dmas, [(P, w[:, :]) for w in both], brow[:, :]
        node_product(nc, k, "mlp_in", mlp_loads, 2 * D, D, {"gpsimd": own_h},
                     ("scalar", lambda act, p, blk, o: act.copy(o[:, :], p[:, :]), table_mlp))
        edge_mlp_pass(nc, k, "mlp", table_mlp, edge_attr_64, L1_W1, L1_Wg, L1_W2, L1_b2)
        gated_output(nc, k, L1_gamma, L1_beta)

        norm_relu(nc, k, "ln2")

        def scaled(lo, W):
            return lambda act, p, blk, o: act.activation(rows_of(k.AGG, blk, lo, lo + W), p[:, 0:W], ACT.Copy,
                                                         scale=k.dinv[:, bass.ds(blk, 1)])
        node_product(nc, k, "gcn1_in", lambda sb: (*matrix(sb, "w", L2_W1), None), d1, D, {"gpsimd": own_h},
                     ("scalar", scaled(d1, d1), None))
        store_table(nc, k, "g1", table_g1, k.AGG[:, :, d1:2 * d1])
        sum_pass(nc, k, "gcn1", table_g1, d1, 0)
        graph_norm(nc, k, "bn1", 0, d1, d1, L2_b1, L2_g1, L2_be1)
        node_product(nc, k, "gcn2_in", lambda sb: (*matrix(sb, "w", L2_W2), None), d2, d1,
                     {"gpsimd": lambda pool, buf, blk: pool.tensor_copy(buf[:, 0:d1], rows_of(k.AGG, blk, 0, d1))},
                     ("scalar", scaled(d1 + d2, d2), None))
        store_table(nc, k, "g2", table_g2, k.AGG[:, :, d1 + d2:d1 + 2 * d2])
        sum_pass(nc, k, "gcn2", table_g2, d2, d1)
        graph_norm(nc, k, "bn2", d1, d2, d1 + d2, L2_b2, L2_g2, L2_be2)

        def fc_loads(sb):
            dmas, pieces = matrix(sb, "wfc", L2_Wfc)
            d, bias = bias_row(sb, L2_bfc)
            return dmas + d, pieces, bias
        node_product(nc, k, "fc", fc_loads, D, D + d1 + d2,
                     {"gpsimd": own_h, "vector": lambda v, buf, blk: v.tensor_scalar(buf[:, D:D + d1 + d2], rows_of(k.AGG, blk, 0, d1 + d2), 1.0, None, ALU.mult)},
                     ("vector", lambda v, p, blk, o: v.scalar_tensor_tensor(rows_of(k.X, blk, 0, D), p[:, 0:D], 0.0,
                                                                            rows_of(k.X, blk, 0, D), ALU.max, ALU.add), None))

        norm_relu(nc, k, "ln3")
        v_row, attn_row, const = sb("v_row", [P, L3_We.shape[1]]), sb("attn_row", [P, D]), sb("const", [P, 1])
        attention_constants(nc, k, L3_attn, L3_We, L3_be, v_row, attn_row, const)
        wnT = sb("wnT", [P, D // P, D])
        turn_weights(nc, k, L3_Wn, wnT)
        prod, part = sb("prod", [P, D]), sb("part", [P, 2])
        node_rows_done = sem("att_in_rows")

        def att_loads(sb):
            d, bias = bias_row(sb, L3_bn)
            return d, [(P, wnT[:, c, :]) for c in range(D // P)], bias

        att_steps = [0]

        def att_row(v, p, blk, o):
            u = att_steps[0] % 2
            att_steps[0] += 1
            v.tensor_scalar(rows_of(k.H, blk, 0, D), p[:, 0:D], 1.0, None, ALU.mult)
            v.tensor_tensor_reduce(prod[:, :], p[:, 0:D], attn_row[:, :], 1.0, const[:, 0:1], ALU.mult, ALU.add,
                                   part[:, u:u + 1]).then_inc(node_rows_done, 1)
            v.wait_ge(node_rows_done, blk + 1)
            return v.tensor_scalar(rows_of(k.H, blk, D + 1, D + 2), part[:, u:u + 1], 1.0, None, ALU.mult)
        node_product(nc, k, "att_in", att_loads, D, D, {"gpsimd": own_h}, ("vector", att_row, None))
        store_table(nc, k, "att", table_att, k.H[:, :, :])
        attention_pass(nc, k, "att", table_att, edge_attr_128, v_row[:, :])
        attention_output(nc, k, out)


def turn_weights(nc, k, W, wT):
    n, m = W.shape
    with ExitStack() as ctx:
        sb, ps, sem = scope(nc, ctx)
        w_in = sb("w_in", [P, n // P, m])
        p_w = ps("p_w", [P, m // P, n])
        loaded, turned, copied = sem("wn_loaded"), sem("wn_turned"), sem("wn_copied")
        block = ctx.enter_context(nc.Block())

        @block.sync
        def _(sp):
            sp.dma_start(w_in[:, :, :], W.rearrange("(a p) m -> p a m", p=P)).then_inc(loaded, 16)

        @block.tensor
        def _(pe):
            pe.wait_ge(loaded, 16)
            for c in range(m // P):
                for a in range(n // P):
                    last = pe.transpose(p_w[:, c, a * P:(a + 1) * P], w_in[:, a, c * P:(c + 1) * P], k.ident[:, :])
            last.then_inc(turned, 1)

        @block.vector
        def _(v):
            v.wait_ge(turned, 1)
            v.tensor_copy(wT[:, :, :], p_w[:, :, :]).then_inc(copied, 1)
            v.wait_ge(copied, 1)


_INS = ['x', 'src', 'dst', 'edge_attr_128', 'edge_attr_64', 'L0_gnn_W1_l', 'L0_gnn_b1', 'L0_gnn_W1_r', 'L0_gnn_W2_l',
        'L0_gnn_b2', 'L0_gnn_W2_r', 'L1_gnn_W1', 'L1_gnn_b1', 'L1_gnn_W2', 'L1_gnn_b2', 'L1_gnn_Wg', 'L1_gnn_bg',
        'L1_gnn_gamma', 'L1_gnn_beta', 'L2_gnn_W1', 'L2_gnn_b1', 'L2_gnn_g1', 'L2_gnn_be1', 'L2_gnn_W2', 'L2_gnn_b2',
        'L2_gnn_g2', 'L2_gnn_be2', 'L2_gnn_Wfc', 'L2_gnn_bfc', 'L3_gnn_Wn', 'L3_gnn_bn', 'L3_gnn_We', 'L3_gnn_be',
        'L3_gnn_attn']


def build(nc, shapes):
    args = [nc.dram_tensor(f"in_{name}_dram", shape, dt, kind="ExternalInput").ap() for name, shape, dt in shapes]
    out = nc.dram_tensor("out_0_dram", shapes[0][1], F32, kind="ExternalOutput").ap()
    gnn(nc, *args, out)


def kernel(**inputs):
    import numpy as _np
    import concourse.bacc as _bacc
    from concourse import mybir as _mybir
    from concourse.bass_utils import run_bass_kernel_spmd as _run

    nc = _bacc.Bacc("TRN2", target_bir_lowering=False, num_devices=1)
    arrays, shapes = {}, []
    for name in _INS:
        a = _np.ascontiguousarray(inputs[name])
        arrays[f"in_{name}_dram"] = a
        shapes.append((name, a.shape, _mybir.dt.from_np(a.dtype)))
    build(nc, shapes)
    r = _run(nc, [arrays], core_ids=[0])
    return r.results[0]["out_0_dram"]
```

```python
import itertools
from contextlib import ExitStack

import concourse.bass as bass
from concourse import mybir

ALU = mybir.AluOpType
ACT = mybir.ActivationFunctionType
F32 = mybir.dt.float32
F32R = mybir.dt.float32r
I32 = mybir.dt.int32
AX_X = mybir.AxisListType.X

P = 128
QUAD = 4
EPS = 1e-5
FAR = 2.0 ** 20
BIG = 1e30
FLOOR = -1e29


CONSTANTS = 7
SCOPES = itertools.count()


def ceil_div(a, b):
    return -(-a // b)


class Core:
    pass


def scope(nc, ctx):
    n = next(SCOPES)

    def sb(name, shape, dt=F32):
        return ctx.enter_context(nc.sbuf_tensor(f"{name}_{n}", shape, dt))

    def ps(name, shape, dt=F32):
        return ctx.enter_context(nc.psum_tensor(f"{name}_{n}", shape, dt))

    sems = []

    def sem(name):
        sems.append(nc.alloc_semaphore(name))
        return sems[-1]

    def clear():
        if sems:
            nc.clear_and_free_semaphores(sems)
            nc.all_engine_barrier(sem_only=True)
    ctx.callback(clear)
    return sb, ps, sem


def hold(eng, held):
    eng.sem_inc(held, 1)


def chain(eng, sem, start=0):
    count = [0]

    def link(ins):
        count[0] += 1
        ins.then_inc(sem, 1)
        eng.wait_ge(sem, start + count[0])
    return link



def load_and_constants(nc, k, x):
    with ExitStack() as ctx:
        sb, ps, sem = scope(nc, ctx)
        zeroed, loaded, row_i = sem("x_pad_zeroed"), sem("x_loaded"), sb("row_i", [P, P], I32)
        made = k.constants_made
        block = ctx.enter_context(nc.Block())
        full = k.N // P
        rest = k.N - full * P

        @block.gpsimd
        def _(pool):
            pool.memset(k.X[:, full:k.NB, :], 0.0).then_inc(zeroed, 1)
            pool.memset(k.ones[:, :], 1.0).then_inc(made, 1)
            pool.memset(k.valid[:, :], 1.0).then_inc(made, 1)
            pool.memset(k.ident[:, :], 1.0).then_inc(made, 1)
            pool.iota(row_i[:, :], pattern=[[1, P]], base=0, channel_multiplier=0).then_inc(made, 1)
            pool.wait_ge(made, 4)
            pool.affine_select(out=k.ident[:, :], in_=k.ident[:, :], pattern=[[-1, P]], base=0,
                               channel_multiplier=1, compare_op=ALU.is_equal, fill=0.0).then_inc(made, 1)
            pool.affine_select(out=k.valid[:, :], in_=k.valid[:, :], pattern=[[0, P]], base=rest - 1,
                               channel_multiplier=-1, compare_op=ALU.is_ge, fill=0.0).then_inc(made, 1)
            pool.tensor_copy(k.iota[:, :], row_i[:, :]).then_inc(made, 1)
            pool.wait_ge(made, CONSTANTS)

        @block.sync
        def _(sp):
            sp.dma_start(k.X[:, 0:full, :], x[0:full * P, :].rearrange("(b p) d -> p b d", p=P)).then_inc(loaded, 16)
            sp.wait_ge(zeroed, 1)
            sp.dma_start(k.X[0:rest, full, :], x[full * P:k.N, :]).then_inc(loaded, 16)
            sp.wait_ge(loaded, 32)


def step_tables(nc, k, src, dst, tiles_dram):
    T, C = k.T, k.NSTEP_PAD // P
    full = k.E // P
    whole = full // P
    some = full - whole * P
    first_own = P - (k.E - full * P)
    assert T == full + 1 and C * P >= T + k.NBU - 1 and C == whole + 1
    with ExitStack() as ctx:
        sb, ps, sem = scope(nc, ctx)
        raw = sb("raw", [P, C, 2, P], I32)
        rows = sb("rows", [P, C, 2, P])
        lane_no_i = sb("lane_no_i", [P, P], I32)
        tile_no_i = sb("tile_no_i", [P, C], I32)
        all_no_i = sb("all_no_i", [P, C * P], I32)
        upto = sb("upto", [P, P])
        dup, dup2 = sb("dup", [P, P]), sb("dup2", [P, P])
        tile_no, all_no = sb("tile_no", [P, C]), sb("all_no", [P, C * P])
        lo, hi = sb("lo", [P, C]), sb("hi", [P, C])
        lo_i, hi_i = sb("lo_i", [P, C], I32), sb("hi_i", [P, C], I32)
        cnt, incl, start = sb("cnt", [P, C]), sb("incl", [P, C]), sb("start", [P, C])
        incl_r, start_r = sb("incl_r", [P, C * P]), sb("start_r", [P, C * P])
        junk = sb("junk", [P, C * P])
        t_of, b_of, t_of_i = sb("t_of", [P, C]), sb("b_of", [P, C]), sb("t_of_i", [P, C], I32)
        base, b_in, b128 = sb("base", [P, C]), sb("b_in", [P, C]), sb("b128", [P, C])
        picked = sb("picked", [P, C, 2 * P])
        p_small = ps("p_small", [P, 512])
        p_rows = ps("p_rows", [P, 2, 1024])
        cleared, loaded, consts, counted, summed = (sem(n) for n in ("tab_cleared", "tab_loaded", "tab_consts", "tab_counted", "tab_summed"))
        placed, spread, rows_ready, rows_stored = (sem(n) for n in ("tab_placed", "tab_spread", "tab_rows_ready", "tab_rows_stored"))
        steps_ready, gathered, rel_ready, turned, link_s = (sem(n) for n in ("tab_steps_ready", "tab_gathered", "tab_rel_ready", "tab_turned", "tab_dve_chain"))
        block = ctx.enter_context(nc.Block())

        @block.sync
        def _(sp):
            sp.wait_ge(cleared, 1)
            for i, a in enumerate((dst, src)):
                sp.dma_start(raw[:, 0:whole, i, :], a[0:whole * P * P].rearrange("(c p l) -> p c l", p=P, l=P)).then_inc(loaded, 16)
                sp.dma_start(raw[0:some, whole, i, :], a[whole * P * P:full * P].rearrange("(p l) -> p l", l=P)).then_inc(loaded, 16)
                sp.dma_start(raw[some:some + 1, whole, i, :], a[k.E - P:k.E].unsqueeze(0)).then_inc(loaded, 16)
            sp.wait_ge(rows_ready, 1)
            sp.dma_start(tiles_dram.rearrange("(c p) w -> p c w", p=P), rows[:, :, :, :].rearrange("p c a l -> p c (a l)")).then_inc(rows_stored, 16)

        @block.gpsimd
        def _(pool):
            pool.memset(raw[:, :, :, :], 0).then_inc(cleared, 1)
            pool.iota(lane_no_i[:, :], pattern=[[1, P]], base=0, channel_multiplier=P)
            pool.iota(tile_no_i[:, :], pattern=[[P, C]], base=0, channel_multiplier=1)
            pool.iota(all_no_i[:, :], pattern=[[1, C * P]], base=0, channel_multiplier=0)
            pool.memset(upto[:, :], 1.0).then_inc(consts, 1)
            pool.wait_ge(consts, 1)
            pool.affine_select(out=upto[:, :], in_=upto[:, :], pattern=[[1, P]], base=0,
                               channel_multiplier=-1, compare_op=ALU.is_ge, fill=0.0).then_inc(consts, 1)
            pool.wait_ge(rows_stored, 16)
            pool.wait_ge(steps_ready, 1)
            for c in range(C):
                pool.indirect_dma_start(out=picked[:, c, :], out_offset=None, in_=tiles_dram,
                                        in_offset=bass.IndirectOffsetOnAxis(ap=t_of_i[:, c:c + 1], axis=0)).then_inc(gathered, 16)

        @block.vector
        def _(v):
            link = chain(v, link_s)
            v.wait_ge(consts, 2)
            link(v.tensor_copy(dup[:, :], lane_no_i[:, :]))
            link(v.tensor_scalar(dup2[:, :], dup[:, :], float(some * P), FAR, ALU.is_ge, ALU.mult))
            link(v.tensor_scalar(dup[:, :], dup[:, :], float(some * P + first_own), None, ALU.is_lt))
            link(v.tensor_tensor(dup[:, :], dup[:, :], dup2[:, :], ALU.mult))
            link(v.tensor_copy(tile_no[:, :], tile_no_i[:, :]))
            link(v.tensor_copy(all_no[:, :], all_no_i[:, :]))
            v.wait_ge(loaded, 96)
            link(v.tensor_copy(rows[:, :, :, :], raw[:, :, :, :]))
            link(v.tensor_reduce(hi[:, :], rows[:, :, 0, :], AX_X, ALU.max))
            v.tensor_tensor(rows[:, whole, 0, :], rows[:, whole, 0, :], dup[:, :], ALU.add).then_inc(rows_ready, 1)
            v.wait_ge(rows_ready, 1)
            link(v.tensor_reduce(lo[:, :], rows[:, :, 0, :], AX_X, ALU.min))
            link(v.tensor_copy(hi_i[:, :], hi[:, :]))
            link(v.tensor_copy(lo_i[:, :], lo[:, :]))
            link(v.tensor_scalar(hi_i[:, :], hi_i[:, :], 7, None, ALU.arith_shift_right))
            link(v.tensor_scalar(lo_i[:, :], lo_i[:, :], 7, None, ALU.arith_shift_right))
            link(v.tensor_copy(hi[:, :], hi_i[:, :]))
            link(v.tensor_copy(lo[:, :], lo_i[:, :]))
            link(v.tensor_tensor(cnt[:, :], hi[:, :], lo[:, :], ALU.subtract))
            link(v.tensor_scalar(hi[:, :], tile_no[:, :], float(T), None, ALU.is_lt))
            v.scalar_tensor_tensor(cnt[:, :], cnt[:, :], 1.0, hi[:, :], ALU.add, ALU.mult).then_inc(counted, 1)
            v.wait_ge(counted, 1)
            v.wait_ge(summed, 1)
            link(v.tensor_copy(incl[:, :], p_small[:, 0:C]))
            link(v.tensor_tensor(start[:, :], cnt[:, :], incl[:, :], ALU.subtract))
            v.tensor_tensor(start[:, :], start[:, :], lo[:, :], ALU.add).then_inc(placed, 1)
            v.wait_ge(spread, 1)
            link(v.tensor_copy(incl_r[:, :], p_rows[:, 0, 0:C * P]))
            link(v.tensor_copy(start_r[:, :], p_rows[:, 1, 0:C * P]))
            for c in range(C):
                link(v.tensor_scalar(junk[:, :], incl_r[:, :], tile_no[:, c:c + 1], 0.0, ALU.is_le, ALU.add, accum_out=t_of[:, c:c + 1]))
            link(v.tensor_scalar(t_of[:, :], t_of[:, :], float(T - 1), None, ALU.min))
            for c in range(C):
                link(v.scalar_tensor_tensor(junk[:, :], all_no[:, :], t_of[:, c:c + 1], start_r[:, :], ALU.is_equal, ALU.mult, accum_out=b_of[:, c:c + 1]))
            v.tensor_copy(t_of_i[:, :], t_of[:, :]).then_inc(steps_ready, 1)
            link(v.tensor_tensor(b_of[:, :], b_of[:, :], tile_no[:, :], ALU.add))
            link(v.tensor_scalar(b128[:, :], b_of[:, :], float(P), None, ALU.mult))
            link(v.tensor_scalar(b_in[:, :], b_of[:, :], float(k.NB - 1), 0.0, ALU.min, ALU.max))
            link(v.tensor_scalar(base[:, :], t_of[:, :], float(P), float(k.E - P), ALU.mult, ALU.min))
            v.wait_ge(gathered, 16 * C)
            for c in range(C):
                v.tensor_scalar(picked[:, c, 0:P], picked[:, c, 0:P], b128[:, c:c + 1], None, ALU.subtract).then_inc(rel_ready, 1)
            v.wait_ge(turned, 1)
            link(v.tensor_copy(k.drelS[:, :], p_rows[:, 0, 0:C * P]))
            link(v.tensor_copy(k.srcS[:, :], p_rows[:, 1, 0:C * P]))
            v.tensor_copy(junk[:, 0:1], base[:, 0:1]).then_inc(rel_ready, 1)
            v.wait_ge(turned, 2)
            link(v.tensor_copy(k.baseT[0:1, :], p_rows[0:1, 0, 0:C * P]))
            link(v.tensor_copy(k.blkT[0:1, :], p_rows[0:1, 1, 0:C * P]))

        @block.tensor
        def _(pe):
            pe.wait_ge(consts, 2)
            pe.wait_ge(counted, 1)
            for c in range(C):
                last = pe.matmul(p_small[:, c:c + 1], upto[:, :], cnt[:, c:c + 1], start=True, stop=(c == 0))
                for d in range(c):
                    last = pe.matmul(p_small[:, c:c + 1], k.ones[:, :], cnt[:, d:d + 1], start=False, stop=(d == c - 1))
            last.then_inc(summed, 1)

            def spread_rows(i, a):
                for c in range(C):
                    last = pe.matmul(p_rows[:, i, c * P:(c + 1) * P], a[:, c:c + 1].to_broadcast([P, P]), k.ident[:, :], start=True, stop=True)
                return last
            pe.wait_ge(placed, 1)
            spread_rows(0, incl)
            spread_rows(1, start).then_inc(spread, 1)
            pe.wait_ge(rel_ready, C)
            for c in range(C):
                for i in range(2):
                    last = pe.transpose(p_rows[:, i, c * P:(c + 1) * P], picked[:, c, i * P:(i + 1) * P], k.ident[:, :])
            last.then_inc(turned, 1)
            pe.wait_ge(rel_ready, C + 1)
            spread_rows(0, base)
            spread_rows(1, b_in).then_inc(turned, 1)



def layer_norm_stats(nc, k, name, src_of, rstd, shift):
    with ExitStack() as ctx:
        sb, ps, sem = scope(nc, ctx)
        st = sb("st", [P, k.NB, 6])
        mean, half, var = sb("mean", [P, k.NB]), sb("half", [P, k.NB]), sb("var", [P, k.NB])
        stats, var_ready, std_ready, link_s = sem(f"{name}_stats"), sem(f"{name}_var_ready"), sem(f"{name}_std_ready"), sem(f"{name}_dve_chain")
        block = ctx.enter_context(nc.Block())

        @block.vector
        def _(v):
            link = chain(v, link_s)
            with v.Fori(0, k.NB // 2) as j:
                for u in range(2):
                    v.bn_stats(st[:, bass.ds(2 * j + u, 1), :].rearrange("p b s -> p (b s)"), src_of(2 * j + u)).then_inc(stats, 1)
            v.wait_ge(stats, k.NB)
            link(v.tensor_tensor(mean[:, :], st[:, :, 1], st[:, :, 4], ALU.add))
            link(v.tensor_tensor(half[:, :], st[:, :, 1], st[:, :, 4], ALU.subtract))
            link(v.tensor_tensor(var[:, :], st[:, :, 2], st[:, :, 5], ALU.add))
            link(v.tensor_scalar(half[:, :], half[:, :], 0.5, None, ALU.mult))
            link(v.tensor_tensor(half[:, :], half[:, :], half[:, :], ALU.mult))
            link(v.tensor_scalar(var[:, :], var[:, :], 1.0 / k.D, EPS, ALU.mult, ALU.add))
            v.tensor_tensor(var[:, :], var[:, :], half[:, :], ALU.add).then_inc(var_ready, 1)
            v.wait_ge(std_ready, 1)
            link(v.reciprocal(rstd[:, :], var[:, :]))
            link(v.scalar_tensor_tensor(shift[:, :], mean[:, :], -0.5, rstd[:, :], ALU.mult, ALU.mult))

        @block.scalar
        def _(act):
            act.wait_ge(var_ready, 1)
            act.activation(var[:, :], var[:, :], ACT.Sqrt).then_inc(std_ready, 1)


def norm_relu(nc, k, name, table=None):
    with ExitStack() as ctx:
        sb, ps, sem = scope(nc, ctx)
        rstd, shift = sb("rstd", [P, k.NB]), sb("shift", [P, k.NB])
        layer_norm_stats(nc, k, name, lambda b: k.X[:, bass.ds(b, 1), :].rearrange("p b d -> p (b d)"), rstd, shift)
        normed, ones_set, stored = sem(f"{name}_normed"), sem(f"{name}_ones_set"), sem(f"{name}_stored")
        with nc.Block() as block:
            @block.scalar
            def _(act):
                with act.Fori(0, k.NB // 2) as j:
                    for u in range(2):
                        b = 2 * j + u
                        act.activation(k.H[:, bass.ds(b, 1), 0:k.D], k.X[:, bass.ds(b, 1), :], ACT.Relu,
                                       bias=shift[:, bass.ds(b, 1)], scale=rstd[:, bass.ds(b, 1)]).then_inc(normed, 1)
                act.wait_ge(normed, k.NB)

            if table is not None:
                @block.gpsimd
                def _(pool):
                    pool.memset(k.H[:, :, k.D:k.D + 2], 1.0).then_inc(ones_set, 1)

                @block.sync
                def _(sp):
                    sp.wait_ge(normed, k.NB)
                    sp.wait_ge(ones_set, 1)
                    sp.dma_start(table.rearrange("(b p) w -> p b w", p=P), k.H[:, :, :]).then_inc(stored, 16)
                    sp.wait_ge(stored, 16)


def node_product(nc, k, name, loads, width, row, stage, finish):
    with ExitStack() as ctx:
        sb, ps, sem = scope(nc, ctx)
        dmas, weights, bias = loads(sb)
        chunks = len(weights)
        inb = [sb(f"in_rows{u}", [P, row]) for u in range(2)]
        turned = [sb(f"turned_sb{u}", [P, chunks * P]) for u in range(2)]
        p_turn = [ps(f"p_turn{u}", [P, chunks * P]) for u in range(2)]
        p_out = [ps(f"p_out{u}", [P, 512]) for u in range(2)]
        w_loaded = sem(f"{name}_w_loaded")
        staged = [sem(f"{name}_staged{u}") for u in range(2)]
        turned_p = [sem(f"{name}_turned{u}") for u in range(2)]
        copied = [sem(f"{name}_copied{u}") for u in range(2)]
        product = [sem(f"{name}_product{u}") for u in range(2)]
        finished = [sem(f"{name}_finished{u}") for u in range(2)]
        fin_engine, fin, extra = finish
        out_sb = [sb(f"out_sb{u}", [P, width]) for u in range(2)] if extra else None
        stored = [sem(f"{name}_stored{u}") for u in range(2)] if extra else None
        rounds = k.NB // 2
        block = ctx.enter_context(nc.Block())

        def stage_loop(eng, f):
            with eng.Fori(0, rounds) as j:
                for u in range(2):
                    eng.wait_ge(turned_p[u], j)
                    f(eng, inb[u], 2 * j + u).then_inc(staged[u], 1)

        def finish_one(eng, j, u):
            eng.wait_ge(product[u], j + 1)
            if extra:
                eng.wait_ge(stored[u], 16 * j)
            fin(eng, p_out[u], 2 * j + u, out_sb[u] if extra else None).then_inc(finished[u], 1)

        @block.sync
        def _(sp):
            for to, of in dmas:
                sp.dma_start(to, of).then_inc(w_loaded, 16)
            if extra:
                with sp.Fori(0, rounds) as j:
                    for u in range(2):
                        sp.wait_ge(finished[u], j + 1)
                        sp.dma_start(extra[bass.ds((2 * j + u) * P, P), :], out_sb[u][:, :]).then_inc(stored[u], 16)
                for u in range(2):
                    sp.wait_ge(stored[u], 16 * rounds)

        @block.tensor
        def _(pe):
            pe.wait_ge(w_loaded, 16 * len(dmas))
            with pe.Fori(0, rounds) as j:
                for u in range(2):
                    pe.wait_ge(staged[u], len(stage) * (j + 1))
                    pe.wait_ge(copied[u], j)
                    at = 0
                    for c, (K, _) in enumerate(weights):
                        last = pe.transpose(p_turn[u][0:K, c * P:(c + 1) * P], inb[u][:, at:at + K], k.ident[:, :])
                        at += K
                    last.then_inc(turned_p[u], 1)
                for u in range(2):
                    pe.wait_ge(copied[u], j + 1)
                    pe.wait_ge(finished[u], j)
                    for c, (K, w) in enumerate(weights):
                        last = pe.matmul(p_out[u][:, 0:width], turned[u][0:K, c * P:(c + 1) * P], w,
                                         start=(c == 0), stop=(c == chunks - 1 and bias is None))
                    if bias is not None:
                        last = pe.matmul(p_out[u][:, 0:width], k.ones[0:1, :], bias, start=False, stop=True)
                    last.then_inc(product[u], 1)

        Ks = [K for K, _ in weights]

        @block.scalar
        def _(act):
            with act.Fori(0, rounds) as j:
                for u in range(2):
                    act.wait_ge(turned_p[u], j + 1)
                    act.wait_ge(product[u], j)
                    n_full = sum(K == P for K in Ks)
                    last = act.copy(turned[u][:, 0:n_full * P], p_turn[u][:, 0:n_full * P])
                    for c, K in enumerate(Ks):
                        if K != P:
                            last = act.copy(turned[u][0:K, c * P:(c + 1) * P], p_turn[u][0:K, c * P:(c + 1) * P])
                    last.then_inc(copied[u], 1)
                if fin_engine == "scalar":
                    for u in range(2):
                        finish_one(act, j, u)
            if fin_engine == "scalar":
                for u in range(2):
                    act.wait_ge(finished[u], rounds)

        @block.gpsimd
        def _(pool):
            if "gpsimd" in stage:
                stage_loop(pool, stage["gpsimd"])

        @block.vector
        def _(v):
            with v.Fori(0, rounds) as j:
                if "vector" in stage:
                    for u in range(2):
                        v.wait_ge(turned_p[u], j)
                        stage["vector"](v, inb[u], 2 * j + u).then_inc(staged[u], 1)
                if fin_engine == "vector":
                    for u in range(2):
                        finish_one(v, j, u)
            if fin_engine == "vector":
                for u in range(2):
                    v.wait_ge(finished[u], rounds)


def rows_of(buf, b, lo, hi):
    return buf[:, bass.ds(b, 1), lo:hi].rearrange("p b d -> p (b d)")



def after(j, q, Q, by=1):
    return (j, q + by) if q + by < Q else (j + 1, q + by - Q)


def pipelined(eng, bodies, Q, step, depth):
    for lead in range(depth):
        step([None] * (depth - lead) + [(0, i) for i in range(lead + 1)])
    with eng.Fori(0, bodies - 1) as j:
        for q in range(Q):
            step([(j, q)] + [after(j, q, Q, by) for by in range(1, depth + 1)])
    for q in range(Q):
        step([(bodies - 1, q + by) if q + by < Q else None for by in range(depth + 1)])


def wait_used(eng, used, j, q, Q, back):
    if q - back >= 0:
        eng.wait_ge(used[q - back], j + 2)
    else:
        eng.wait_ge(used[q - back + Q], j + 1)


def index_feed(act, k, idx, index_ready, gathered, j, q, Q):
    if not_zero(j):
        act.wait_ge(gathered[q], 16 * QUAD * j)
    act.copy(idx[:, q * QUAD:(q + 1) * QUAD], k.srcS[:, bass.ds((j * Q + q) * QUAD, QUAD)]).then_inc(index_ready[q], 1)


def gather_quad(pool, k, table, G, idx, index_ready, rows_used, gathered, j, q, per=1):
    pool.wait_ge(index_ready[q], j + 1)
    pool.wait_ge(rows_used[q], per * (j + 1))
    hold(pool, k.held)
    for i in range(q * QUAD, (q + 1) * QUAD):
        pool.indirect_dma_start(out=G[:, i, :], out_offset=None, in_=table,
                                in_offset=bass.IndirectOffsetOnAxis(ap=idx[:, i:i + 1], axis=0)).then_inc(gathered[q], 16)


def pick_matrix(v, k, out, s, op=ALU.is_equal):
    return v.tensor_tensor(out, k.iota[:, :].unsqueeze(1).to_broadcast([P, QUAD, P]),
                           k.drelS[:, bass.ds(s, QUAD)].unsqueeze(2).to_broadcast([P, QUAD, P]), op)


def blocks_of(eng, k, s):
    _, values = k.nc.values_load_multi_w_load_instructions(
        k.blkT[0:1, bass.ds(s, QUAD)], engines=(eng.engine,), min_val=0, max_val=k.NB - 1,
        skip_runtime_bounds_check_because="step_tables clips the blocks to 0 .. NB - 1")
    return values


def load_attributes(sp, k, ea, ea_in, ea_loaded, j, q, Q):
    _, first_edges = k.nc.values_load_multi_w_load_instructions(
        k.baseT[0:1, bass.ds((j * Q + q) * QUAD, QUAD)], engines=(sp.engine,), min_val=0, max_val=k.E - P,
        skip_runtime_bounds_check_because="step_tables clips the tiles' first edges to 0 .. E - P")
    for r, at in enumerate(first_edges):
        sp.dma_start(ea_in[:, q * QUAD + r, :], ea[bass.ds(at, P), :]).then_inc(ea_loaded[q], 16)


def not_zero(n):
    return not isinstance(n, int) or n > 0


def sum_pass(nc, k, name, table, W, lo):
    Q = 4
    bodies = k.NSTEP // (Q * QUAD)
    with ExitStack() as ctx:
        sb, ps, sem = scope(nc, ctx)
        G = sb("G", [P, Q * QUAD, table.shape[1]])
        S = sb("S", [P, 2, QUAD, P])
        idx = sb("idx", [P, Q * QUAD], I32)
        psum = ps("p_sum", [P, 2, QUAD, 512])
        index_ready = [sem(f"{name}_index_ready{q}") for q in range(Q)]
        gathered = [sem(f"{name}_gathered{q}") for q in range(Q)]
        summed = [sem(f"{name}_summed{q}") for q in range(Q)]
        picks_ready, added = sem(f"{name}_picks_ready"), sem(f"{name}_added")
        block = ctx.enter_context(nc.Block())

        @block.scalar
        def _(act):
            for q in range(Q):
                index_feed(act, k, idx, index_ready, gathered, 0, q, Q)
            with act.Fori(0, bodies) as j:
                for q in range(Q):
                    index_feed(act, k, idx, index_ready, gathered, j + 1, q, Q)

        @block.gpsimd
        def _(pool):
            with pool.Fori(0, bodies) as j:
                for q in range(Q):
                    gather_quad(pool, k, table, G, idx, index_ready, summed, gathered, j, q)

        @block.tensor
        def _(pe):
            for s in summed:
                pe.sem_inc(s, 1)
            with pe.Fori(0, bodies) as j:
                for q in range(Q):
                    n = Q * j + q
                    pe.wait_ge(picks_ready, n + 1)
                    pe.wait_ge(gathered[q], 16 * QUAD * (j + 1))
                    pe.wait_ge(added, (n + 1) * QUAD)
                    for r in range(QUAD):
                        last = pe.matmul(psum[:, q % 2, r, 0:W], S[:, q % 2, r, :], G[:, q * QUAD + r, 0:W], start=True, stop=True)
                    last.then_inc(summed[q], 1)

        @block.vector
        def _(v):
            v.memset(k.AGG[:, :, lo:lo + W], 0.0).then_inc(added, 2 * QUAD)

            def step(quads):
                now, then = quads
                if then is not None:
                    j, q = then
                    wait_used(v, summed, j, q, Q, 2)
                    pick_matrix(v, k, S[:, q % 2, :, :], (Q * j + q) * QUAD).then_inc(picks_ready, 1)
                if now is not None:
                    j, q = now
                    n = Q * j + q
                    b = blocks_of(v, k, n * QUAD)
                    v.wait_ge(summed[q], j + 2)
                    for r in range(QUAD):
                        v.wait_ge(added, (n + 2) * QUAD + r)
                        v.tensor_tensor(rows_of(k.AGG, b[r], lo, lo + W), rows_of(k.AGG, b[r], lo, lo + W),
                                        psum[:, q % 2, r, 0:W], ALU.add).then_inc(added, 1)
            pipelined(v, bodies, Q, step, 1)
            v.wait_ge(added, 2 * QUAD + k.NSTEP)


def edge_mlp_pass(nc, k, name, table, ea, W1, Wg, W2, b2):
    D, A = k.D, ea.shape[1]
    assert 2 * A == P
    bodies = k.NSTEP // (2 * QUAD)
    with ExitStack() as ctx:
        sb, ps, sem = scope(nc, ctx)
        G = sb("G", [P, 2 * QUAD, 2 * D])
        S = sb("S", [P, QUAD, P])
        idx = sb("idx", [P, 2 * QUAD], I32)
        ea_in = sb("ea_in", [P, 2 * QUAD, A])
        parts = sb("parts", [P, QUAD, 2, A], F32R)
        partsT = sb("partsT", [P, QUAD * P], F32R)
        pre = sb("pre", [P, QUAD, 2 * D])
        gate = sb("gate", [P, 2, QUAD, D])
        coreT = sb("coreT", [P, 2, QUAD * P])
        msg = sb("msg", [P, QUAD, D])
        w_in = sb("w_in", [P, 2 * D])
        w_high, w_low = sb("w_high", [P, 2 * D], F32R), sb("w_low", [P, 2 * D], F32R)
        w2, ones2 = sb("w2", [P, 2, D]), sb("ones2", [2, P], F32R)
        b2_in, b2_high = sb("b2_in", [2, D]), sb("b2_high", [2, D], F32R)
        b2_parts = sb("b2_parts", [2, D], F32R)
        p_partsT = ps("p_partsT", [P, QUAD * P])
        p_pre = ps("p_pre", [P, 2, 2 * D])
        p_coreT = ps("p_coreT", [P, 2, QUAD * P])
        p_core = ps("p_core", [P, QUAD, D])
        p_sum = ps("p_sum", [P, 2, D])
        two = range(2)
        index_ready = [sem(f"{name}_index_ready{h}") for h in two]
        gathered = [sem(f"{name}_gathered{h}") for h in two]
        ea_loaded = [sem(f"{name}_ea_loaded{h}") for h in two]
        pre_added = [sem(f"{name}_pre_added{h}") for h in two]
        (w_loaded, w_split, high_ready, parts_ready, parts_turned, partsT_ready, pre_summed, pre_out, gate_out,
         core_turned, coreT_ready, core_out, msg_ready, picks_ready, pair_summed, added, b2_chain) = (sem(f"{name}_{n}") for n in (
             "w_loaded", "w_split", "high_ready", "parts_ready", "parts_turned", "partsT_ready", "pre_summed", "pre_out",
             "gate_out", "core_turned", "coreT_ready", "core_out", "msg_ready", "picks_ready", "pair_summed", "added", "b2_chain"))
        block = ctx.enter_context(nc.Block())

        @block.sync
        def _(sp):
            for half in two:
                for i, w in enumerate((W1, Wg)):
                    sp.dma_start(w_in[half * A:(half + 1) * A, i * D:(i + 1) * D], w[D:D + A, :]).then_inc(w_loaded, 16)
            sp.dma_start(w2[:, :, :], W2.rearrange("(c p) n -> p c n", p=P)).then_inc(w_loaded, 16)
            sp.dma_start(b2_in[:, :], b2.partition_broadcast(2)).then_inc(w_loaded, 16)
            with sp.Fori(0, bodies) as j:
                for h in two:
                    sp.wait_ge(parts_ready, 2 * j + h + 1)
                    load_attributes(sp, k, ea, ea_in, ea_loaded, j, h, 2)
            for h in two:
                sp.wait_ge(ea_loaded[h], 16 * QUAD * bodies)

        @block.gpsimd
        def _(pool):
            with pool.Fori(0, bodies) as j:
                for h in two:
                    gather_quad(pool, k, table, G, idx, index_ready, pre_added, gathered, j, h)

        @block.tensor
        def _(pe):
            def core_gate(j, h):
                n = 2 * j + h
                pe.wait_ge(parts_ready, n + 3)
                if not_zero(n):
                    pe.wait_ge(partsT_ready, n)
                for r in range(QUAD):
                    last = pe.transpose(p_partsT[:, r * P:(r + 1) * P], parts[:, r, :, :].rearrange("p a b -> p (a b)").bitcast(F32), k.ident[:, :])
                last.then_inc(parts_turned, 1)
                pe.wait_ge(partsT_ready, n + 1)
                for r in range(QUAD):
                    pe.wait_ge(pre_out, 2 + QUAD * n + r - 1)
                    pe.matmul(p_pre[:, r % 2, :], partsT[:, r * P:(r + 1) * P], w_high[:, :], start=True, stop=False)
                    pe.matmul(p_pre[:, r % 2, :], partsT[:, r * P:(r + 1) * P], w_low[:, :], start=False, stop=True).then_inc(pre_summed, 1)

            def turn_core(j, h):
                n = 2 * j + h
                pe.wait_ge(pre_added[h], j + 2)
                if not_zero(n):
                    pe.wait_ge(coreT_ready, n)
                for f in range(2):
                    for r in range(QUAD):
                        last = pe.transpose(p_coreT[:, f, r * P:(r + 1) * P], pre[:, r, f * P:(f + 1) * P], k.ident[:, :])
                last.then_inc(core_turned, 1)

            def core_product(j, h):
                n = 2 * j + h
                pe.wait_ge(coreT_ready, n + 1)
                pe.wait_ge(msg_ready, n + 1)
                for r in range(QUAD):
                    for f in range(2):
                        pe.matmul(p_core[:, r, :], coreT[:, f, r * P:(r + 1) * P], w2[:, f, :], start=(f == 0), stop=False)
                    last = pe.matmul(p_core[:, r, :], ones2[:, :], b2_parts[:, :], start=False, stop=True)
                last.then_inc(core_out, 1)

            def sums(j, h):
                n = 2 * j + h
                pe.wait_ge(msg_ready, n + 2)
                pe.wait_ge(picks_ready, n + 1)
                for q in range(2):
                    pe.wait_ge(added, n * QUAD + 2 * q + 2)
                    for r in (2 * q, 2 * q + 1):
                        last = pe.matmul(p_sum[:, r % 2, :], S[:, r, :], msg[:, r, :], start=True, stop=True)
                    last.then_inc(pair_summed, 1)

            pe.wait_ge(w_split, 5)
            core_gate(0, 0)
            turn_core(0, 0)

            def step(now, then):
                core_gate(*then)
                core_product(*now)
                turn_core(*then)
                sums(*now)

            with pe.Fori(0, bodies - 1) as j:
                step((j, 0), (j, 1))
                step((j, 1), (j + 1, 0))
            step((bodies - 1, 0), (bodies - 1, 1))
            core_product(bodies - 1, 1)
            sums(bodies - 1, 1)

        @block.scalar
        def _(act):
            def split_high(j, h):
                n = 2 * j + h
                act.wait_ge(ea_loaded[h], 16 * QUAD * (j + 1))
                if not_zero(n):
                    act.wait_ge(parts_turned, n)
                act.copy(parts[:, :, 0, :], ea_in[:, h * QUAD:(h + 1) * QUAD, :]).then_inc(high_ready, 1)

            def body(j, h, last=False):
                n = 2 * j + h
                act.wait_ge(parts_turned, n + 1)
                act.wait_ge(pre_summed, QUAD * n) if not_zero(n) else None
                act.copy(partsT[:, :], p_partsT[:, :]).then_inc(partsT_ready, 1)
                if not last:
                    split_high(*((j, 1) if h == 0 else (j + 1, 0)))
                act.wait_ge(pre_added[h], j + 2)
                act.wait_ge(msg_ready, n) if not_zero(n) else None
                act.activation(gate[:, h, :, :], pre[:, :, D:2 * D], ACT.Sigmoid).then_inc(gate_out, 1)
                index_feed(act, k, idx, index_ready, gathered, j + 1, h, 2)
                act.wait_ge(core_turned, n + 1)
                act.wait_ge(core_out, n) if not_zero(n) else None
                act.activation(coreT[:, 0, :], p_coreT[:, 0, :], ACT.Relu)
                act.activation(coreT[:, 1, :], p_coreT[:, 1, :], ACT.Relu).then_inc(coreT_ready, 1)

            for h in two:
                index_feed(act, k, idx, index_ready, gathered, 0, h, 2)
            split_high(0, 0)
            body(0, 0)
            body(0, 1)
            with act.Fori(1, bodies - 1) as j:
                body(j, 0)
                body(j, 1)
            body(bodies - 1, 0)
            body(bodies - 1, 1, last=True)

        @block.vector
        def _(v):
            def split_low(j, h):
                n = 2 * j + h
                v.wait_ge(high_ready, n + 1)
                v.wait_ge(ea_loaded[h], 16 * QUAD * (j + 1))
                v.tensor_tensor(parts[:, :, 1, :], ea_in[:, h * QUAD:(h + 1) * QUAD, :], parts[:, :, 0, :].bitcast(F32), ALU.subtract).then_inc(parts_ready, 1)

            def add_rows(j, h):
                n = 2 * j + h
                v.wait_ge(gathered[h], 16 * QUAD * (j + 1))
                if not_zero(n):
                    v.wait_ge(core_turned, n)
                    v.wait_ge(gate_out, n)
                for r in range(QUAD):
                    v.wait_ge(pre_summed, QUAD * n + r + 1)
                    v.tensor_tensor(pre[:, r, :], p_pre[:, r % 2, :], G[:, h * QUAD + r, :], ALU.add).then_inc(pre_out, 1)
                v.wait_ge(pre_out, 2 + QUAD * n + QUAD)
                v.sem_inc(pre_added[h], 1)

            def messages(j, h):
                n = 2 * j + h
                if not_zero(n):
                    v.wait_ge(pair_summed, 2 * n)
                pick_matrix(v, k, S[:, :, :], j * 2 * QUAD + h * QUAD).then_inc(picks_ready, 1)
                b = blocks_of(v, k, j * 2 * QUAD + h * QUAD)
                v.wait_ge(core_out, n + 1)
                v.wait_ge(gate_out, n + 1)
                v.tensor_tensor(msg[:, 0:2, :], p_core[:, 0:2, :], gate[:, h, 0:2, :], ALU.mult)
                v.tensor_tensor(msg[:, 2:4, :], p_core[:, 2:4, :], gate[:, h, 2:4, :], ALU.mult).then_inc(msg_ready, 1)
                for r in range(QUAD):
                    if r % 2 == 0:
                        v.wait_ge(pair_summed, 2 * n + r // 2 + 1)
                    v.wait_ge(added, 2 + n * QUAD + r)
                    v.tensor_tensor(rows_of(k.H, b[r], 0, D), rows_of(k.H, b[r], 0, D), p_sum[:, r % 2, :],
                                    ALU.add).then_inc(added, 1)

            for x in (*pre_added, msg_ready):
                v.sem_inc(x, 1)
            v.sem_inc(added, 2)
            v.sem_inc(pre_out, 2)
            v.sem_inc(parts_ready, 2)
            v.wait_ge(w_loaded, 96)
            v.memset(ones2[:, :].bitcast(F32), 1.0).then_inc(w_split, 1)
            v.tensor_copy(w_high[:, :], w_in[:, :]).then_inc(w_split, 1)
            v.tensor_copy(b2_high[:, :], b2_in[:, :]).then_inc(w_split, 1)
            v.wait_ge(w_split, 3)
            v.tensor_tensor(w_low[:, :], w_in[:, :], w_high[:, :].bitcast(F32), ALU.subtract).then_inc(w_split, 1)
            b2_split(v, k, b2_in, b2_high, b2_parts, b2_chain, w_split)
            split_low(0, 0)
            add_rows(0, 0)
            split_low(0, 1)
            add_rows(0, 1)
            messages(0, 0)

            with v.Fori(0, bodies - 1) as j:
                split_low(j + 1, 0)
                add_rows(j + 1, 0)
                messages(j, 1)
                split_low(j + 1, 1)
                add_rows(j + 1, 1)
                messages(j + 1, 0)
            messages(bodies - 1, 1)
            v.wait_ge(added, 2 + k.NSTEP)


def b2_split(v, k, b2_in, b2_high, b2_parts, b2_chain, w_split):
    v.tensor_tensor(b2_in[:, :], b2_in[:, :], b2_high[:, :].bitcast(F32), ALU.subtract).then_inc(b2_chain, 1)
    v.wait_ge(b2_chain, 1)
    v.tensor_scalar(b2_in[:, :], b2_in[:, :], k.ident[0:2, 1:2], None, ALU.mult).then_inc(b2_chain, 1)
    v.wait_ge(b2_chain, 2)
    v.scalar_tensor_tensor(b2_parts[:, :], b2_high[:, :].bitcast(F32), k.ident[0:2, 0:1], b2_in[:, :],
                           ALU.mult, ALU.add).then_inc(w_split, 1)



def attention_pass(nc, k, name, table, ea, v_row):
    D, A = k.D, ea.shape[1]
    W, Q = D + 1, 4
    bodies = k.NSTEP // (Q * QUAD)
    with ExitStack() as ctx:
        sb, ps, sem = scope(nc, ctx)
        G = sb("G", [P, Q * QUAD, D + 2])
        idx = sb("idx", [P, Q * QUAD], I32)
        ea_in = sb("ea_in", [P, Q * QUAD, A])
        masked = sb("masked", [P, 2, QUAD, P])
        weightT = sb("weightT", [P, 2, QUAD, P])
        weight = sb("weight", [P, 2, QUAD, P])
        minus_top = sb("minus_top", [P, k.NB])
        dot, logit = sb("dot", [P, 2, QUAD]), sb("logit", [P, 2, QUAD])
        step_top = sb("step_top", [P, QUAD])
        minus, rise, scale = sb("minus", [P, 2, QUAD]), sb("rise", [P, 2, QUAD]), sb("scale", [P, 2, QUAD])
        p_turn = ps("p_turn", [P, 2, QUAD, P])
        p_back = ps("p_back", [P, 2, QUAD, P])
        p_sum = ps("p_sum", [P, QUAD, 512])
        index_ready = [sem(f"{name}_index_ready{q}") for q in range(Q)]
        gathered = [sem(f"{name}_gathered{q}") for q in range(Q)]
        ea_loaded = [sem(f"{name}_ea_loaded{q}") for q in range(Q)]
        logits_ready = [sem(f"{name}_logits_ready{q}") for q in range(Q)]
        summed = [sem(f"{name}_summed{q}") for q in range(Q)]
        masked_ready, turned, turned_back, weight_ready = (sem(f"{name}_{n}") for n in ("masked_ready", "turned", "turned_back", "weight_ready"))
        exp_ready, added = sem(f"{name}_exp_ready"), sem(f"{name}_added")
        tops_ready, scale_ready, top_set, dots_ready, step_top_ready = (sem(f"{name}_{n}") for n in (
            "tops_ready", "scale_ready", "top_set", "dots_ready", "step_top_ready"))
        block = ctx.enter_context(nc.Block())

        @block.sync
        def _(sp):
            with sp.Fori(0, bodies) as j:
                for q in range(Q):
                    sp.wait_ge(logits_ready[q], j + 1)
                    load_attributes(sp, k, ea, ea_in, ea_loaded, j, q, Q)
            for q in range(Q):
                sp.wait_ge(ea_loaded[q], 16 * QUAD * bodies)

        @block.gpsimd
        def _(pool):
            with pool.Fori(0, bodies) as j:
                for q in range(Q):
                    gather_quad(pool, k, table, G, idx, index_ready, summed, gathered, j, q, QUAD)

        @block.tensor
        def _(pe):
            def turn(j, q):
                n = Q * j + q
                pe.wait_ge(masked_ready, n + 3)
                pe.wait_ge(exp_ready, (n + 1) * QUAD)
                for r in range(QUAD):
                    last = pe.transpose(p_turn[:, q % 2, r, :], masked[:, q % 2, r, :], k.ident[:, :])
                last.then_inc(turned, 1)

            def turn_back(j, q):
                n = Q * j + q
                pe.wait_ge(weight_ready, n + 1)
                for r in range(QUAD):
                    pe.wait_ge(exp_ready, (n + 2) * QUAD + r + 1)
                    last = pe.transpose(p_back[:, q % 2, r, :], weightT[:, q % 2, r, :], k.ident[:, :])
                last.then_inc(turned_back, 1)

            def sums(j, q):
                n = Q * j + q
                pe.wait_ge(weight_ready, n + 3)
                for r in range(QUAD):
                    pe.wait_ge(added, (n + 1) * QUAD + r + 1)
                    pe.matmul(p_sum[:, r, 0:W], weight[:, q % 2, r, :], G[:, q * QUAD + r, 0:W], start=True, stop=True).then_inc(summed[q], 1)

            def step(quads):
                now, then, later = quads
                if now is not None:
                    sums(*now)
                if later is not None:
                    turn(*later)
                if then is not None:
                    turn_back(*then)
            for s in summed:
                pe.sem_inc(s, QUAD)
            pe.sem_inc(turned, 2)
            pe.sem_inc(turned_back, 2)
            pipelined(pe, bodies, Q, step, 2)

        @block.scalar
        def _(act):
            def copy_weights(j, q):
                n = Q * j + q
                act.wait_ge(turned_back, n + 3)
                if q >= 2:
                    act.wait_ge(summed[q - 2], QUAD * (j + 2))
                else:
                    act.wait_ge(summed[q + 2], QUAD * (j + 1))
                act.copy(weight[:, q % 2, :, :], p_back[:, q % 2, :, :]).then_inc(weight_ready, 1)

            def mask(j, q):
                n = Q * j + q
                act.wait_ge(logits_ready[q], j + 2)
                for r in range(QUAD):
                    last = act.activation(masked[:, q % 2, r, :], masked[:, q % 2, r, :], ACT.Identity,
                                          bias=logit[:, q % 2, r:r + 1], scale=-BIG)
                last.then_inc(masked_ready, 1)

            def exps(j, q):
                n = Q * j + q
                act.wait_ge(tops_ready, n + 1)
                act.wait_ge(added, (n + 1) * QUAD)
                act.activation(scale[:, q % 2, :], rise[:, q % 2, :], ACT.Exp, scale=-1.0).then_inc(scale_ready, 1)
                act.wait_ge(turned_back, n + 1)
                for r in range(QUAD):
                    act.activation(weightT[:, q % 2, r, :], p_turn[:, q % 2, r, :], ACT.Exp,
                                   bias=minus[:, q % 2, r:r + 1]).then_inc(exp_ready, 1)

            def step(quads):
                now, then, later = quads
                if now is not None:
                    copy_weights(*now)
                    index_feed(act, k, idx, index_ready, gathered, now[0] + 1, now[1], Q)
                if later is not None:
                    mask(*later)
                if then is not None:
                    exps(*then)
            act.sem_inc(masked_ready, 2)
            act.sem_inc(weight_ready, 2)
            act.sem_inc(exp_ready, 2 * QUAD)
            for q in range(Q):
                index_feed(act, k, idx, index_ready, gathered, 0, q, Q)
            pipelined(act, bodies, Q, step, 2)

        @block.vector
        def _(v):
            for x in logits_ready:
                v.sem_inc(x, 1)
            v.memset(minus_top[:, :], -FLOOR).then_inc(top_set, 1)
            v.memset(k.AGG[:, :, 0:W], 0.0).then_inc(added, 2 * QUAD)
            def logits(j, q):
                n = Q * j + q
                v.wait_ge(gathered[q], 16 * QUAD * (j + 1))
                v.wait_ge(ea_loaded[q], 16 * QUAD * (j + 1))
                v.wait_ge(turned, n + 1)
                for r in range(QUAD):
                    i = q * QUAD + r
                    ins = v.tensor_tensor_reduce(ea_in[:, i, :], ea_in[:, i, :], v_row, 1.0, G[:, i, D + 1:D + 2],
                                                 ALU.mult, ALU.add, dot[:, q % 2, r:r + 1])
                ins.then_inc(dots_ready, 1)
                v.wait_ge(dots_ready, n + 1)
                v.scalar_tensor_tensor(logit[:, q % 2, :], dot[:, q % 2, :], 0.01, dot[:, q % 2, :], ALU.mult, ALU.max)
                pick_matrix(v, k, masked[:, q % 2, :, :], n * QUAD, ALU.not_equal).then_inc(logits_ready[q], 1)

            def maxima(j, q):
                n = Q * j + q
                b = blocks_of(v, k, n * QUAD)
                v.wait_ge(turned, n + 3)
                v.wait_ge(exp_ready, (n + 1) * QUAD)
                v.tensor_reduce(step_top[:, :], p_turn[:, q % 2, :, :], AX_X, ALU.max).then_inc(step_top_ready, 1)
                v.wait_ge(step_top_ready, n + 1)
                for r in range(QUAD):
                    top = minus_top[:, bass.ds(b[r], 1)]
                    v.wait_ge(top_set, n * QUAD + r + 1)
                    v.tensor_scalar(rise[:, q % 2, r:r + 1], step_top[:, r:r + 1], top, 0.0, ALU.add, ALU.max)
                    ins = v.tensor_scalar(minus[:, q % 2, r:r + 1], step_top[:, r:r + 1], -1.0, top, ALU.mult, ALU.min)
                    if r == QUAD - 1:
                        ins.then_inc(tops_ready, 1)
                    v.tensor_scalar(top, step_top[:, r:r + 1], -1.0, top, ALU.mult, ALU.min).then_inc(top_set, 1)

            def add(j, q):
                n = Q * j + q
                b = blocks_of(v, k, n * QUAD)
                v.wait_ge(scale_ready, n + 1)
                for r in range(QUAD):
                    v.wait_ge(summed[q], QUAD * (j + 1) + r + 1)
                    v.wait_ge(added, (n + 2) * QUAD + r)
                    v.scalar_tensor_tensor(rows_of(k.AGG, b[r], 0, W), rows_of(k.AGG, b[r], 0, W), scale[:, q % 2, r:r + 1],
                                           p_sum[:, r, 0:W], ALU.mult, ALU.add).then_inc(added, 1)

            def step(quads):
                now, then, later = quads
                if later is not None:
                    logits(*later)
                if then is not None:
                    maxima(*then)
                if now is not None:
                    add(*now)
            pipelined(v, bodies, Q, step, 2)
            v.wait_ge(added, 2 * QUAD + k.NSTEP)



def wide(a, n):
    return a.unsqueeze(2).to_broadcast([P, a.shape[1], n])


def every_block(a, nb):
    return a.unsqueeze(1).to_broadcast([P, nb, a.shape[1]])


def store_table(nc, k, name, table, of):
    with ExitStack() as ctx:
        sb, ps, sem = scope(nc, ctx)
        stored = sem(f"{name}_stored")
        with nc.Block() as block:
            @block.sync
            def _(sp):
                sp.dma_start(table.rearrange("(b p) w -> p b w", p=P), of).then_inc(stored, 16)
                sp.wait_ge(stored, 16)


def degrees(nc, k):
    with ExitStack() as ctx:
        sb, ps, sem = scope(nc, ctx)
        deg, plus = sb("deg", [P, k.NB]), sb("plus", [P, k.NB])
        link_s, plus_ready, root_ready = sem("deg_dve_chain"), sem("deg_plus_ready"), sem("deg_root_ready")
        with nc.Block() as block:
            @block.vector
            def _(v):
                link = chain(v, link_s)
                link(v.tensor_scalar(deg[:, :], k.AGG[:, :, k.D], 1.0, None, ALU.max))
                v.tensor_scalar(plus[:, :], k.AGG[:, :, k.D], 1.0, None, ALU.add).then_inc(plus_ready, 1)
                v.reciprocal(k.rdeg[:, :], deg[:, :])
                v.wait_ge(root_ready, 1)
                link(v.reciprocal(k.dinv[:, :], plus[:, :]))

            @block.scalar
            def _(act):
                act.wait_ge(plus_ready, 1)
                act.activation(plus[:, :], plus[:, :], ACT.Sqrt).then_inc(root_ready, 1)


def gated_output(nc, k, gamma, beta):
    D = k.D
    with ExitStack() as ctx:
        sb, ps, sem = scope(nc, ctx)
        rstd, shift = sb("rstd", [P, k.NB]), sb("shift", [P, k.NB])
        gam, bet = sb("gam", [P, D]), sb("bet", [P, D])
        loaded = sem("gout_loaded")
        layer_norm_stats(nc, k, "gout", lambda b: rows_of(k.H, b, 0, D), rstd, shift)
        normed, link_s = sem("gout_normed"), sem("gout_chain")
        with nc.Block() as block:
            @block.sync
            def _(sp):
                sp.dma_start(gam[:, :], gamma.partition_broadcast(P)).then_inc(loaded, 16)
                sp.dma_start(bet[:, :], beta.partition_broadcast(P)).then_inc(loaded, 16)

            @block.scalar
            def _(act):
                with act.Fori(0, k.NB // 2) as j:
                    for u in range(2):
                        b = 2 * j + u
                        act.activation(rows_of(k.H, b, 0, D), rows_of(k.H, b, 0, D), ACT.Identity,
                                       bias=shift[:, bass.ds(b, 1)], scale=rstd[:, bass.ds(b, 1)]).then_inc(normed, 1)

            @block.vector
            def _(v):
                link = chain(v, link_s)
                v.wait_ge(normed, k.NB)
                v.wait_ge(loaded, 32)
                for op, row in ((ALU.mult, gam), (ALU.add, bet)):
                    link(v.tensor_tensor(k.H[:, :, 0:D], k.H[:, :, 0:D], every_block(row[:, :], k.NB), op))
                link(v.tensor_tensor(k.X[:, :, :], k.X[:, :, :], k.H[:, :, 0:D], ALU.add))


def graph_norm(nc, k, name, lo, W, own, b, gain, beta):
    nbu, rest = k.NBU, k.N - (k.NBU - 1) * P
    Z, T = k.AGG[:, :, lo:lo + W], k.AGG[:, :, own:own + W]
    with ExitStack() as ctx:
        sb, ps, sem = scope(nc, ctx)
        b_row, g_row, be_row = sb("b_row", [P, W]), sb("g_row", [P, W]), sb("be_row", [P, W])
        mean, var, rstd = sb("mean_row", [P, W]), sb("var_row", [P, W]), sb("rstd_row", [P, W])
        p_mean, p_var = ps("p_mean", [P, 512]), ps("p_var", [P, 512])
        loaded, z_ready, sq_ready, col_sums, link_s, var_ready, std_ready = (sem(f"{name}_{n}") for n in (
            "loaded", "z_ready", "squares_ready", "column_sums", "dve_chain", "var_ready", "std_ready"))
        block = ctx.enter_context(nc.Block())

        @block.sync
        def _(sp):
            for to, of in ((b_row, b), (g_row, gain), (be_row, beta)):
                sp.dma_start(to[:, :], of.partition_broadcast(P)).then_inc(loaded, 16)

        @block.tensor
        def _(pe):
            for i, (psum, at) in enumerate(((p_mean, lo), (p_var, own))):
                pe.wait_ge((z_ready, sq_ready)[i], 1)
                pe.matmul(psum[:, 0:W], k.ones[:, :], k.AGG[:, 0, at:at + W], start=True, stop=False)
                with pe.Fori(1, nbu - 1) as m:
                    pe.matmul(psum[:, 0:W], k.ones[:, :], rows_of(k.AGG, m, at, at + W), start=False, stop=False)
                pe.matmul(psum[:, 0:W], k.valid[:, :], k.AGG[:, nbu - 1, at:at + W], start=False, stop=True).then_inc(col_sums, 1)

        @block.scalar
        def _(act):
            act.wait_ge(var_ready, 1)
            act.activation(var[:, :], var[:, :], ACT.Sqrt).then_inc(std_ready, 1)

        @block.vector
        def _(v):
            link = chain(v, link_s)
            link(v.tensor_tensor(Z, Z, T, ALU.add))
            link(v.tensor_tensor(Z, Z, wide(k.dinv[:, :], W), ALU.mult))
            v.wait_ge(loaded, 48)
            v.tensor_tensor(Z, Z, every_block(b_row[:, :], k.NB), ALU.add).then_inc(z_ready, 1)
            v.wait_ge(col_sums, 1)
            link(v.tensor_scalar(mean[:, :], p_mean[:, 0:W], 1.0 / k.N, None, ALU.mult))
            link(v.tensor_tensor(Z, Z, every_block(mean[:, :], k.NB), ALU.subtract))
            v.tensor_tensor(T, Z, Z, ALU.mult).then_inc(sq_ready, 1)
            v.wait_ge(col_sums, 2)
            v.tensor_scalar(var[:, :], p_var[:, 0:W], 1.0 / k.N, EPS, ALU.mult, ALU.add).then_inc(var_ready, 1)
            v.wait_ge(std_ready, 1)
            link(v.reciprocal(rstd[:, :], var[:, :]))
            link(v.tensor_tensor(rstd[:, :], rstd[:, :], g_row[:, :], ALU.mult))
            link(v.tensor_tensor(Z, Z, every_block(rstd[:, :], k.NB), ALU.mult))
            link(v.tensor_tensor(Z, Z, every_block(be_row[:, :], k.NB), ALU.add))
            link(v.tensor_scalar(Z, Z, 0.0, None, ALU.max))


def attention_constants(nc, k, attn, We, be, v_row, attn_row, const):
    D, A = We.shape
    with ExitStack() as ctx:
        sb, ps, sem = scope(nc, ctx)
        a_col, be_col = sb("a_col", [P, D // P]), sb("be_col", [P, D // P])
        we = sb("we", [P, D // P, A])
        p_v = ps("p_v", [P, 512])
        loaded, made, copied = sem("att_loaded"), sem("att_made"), sem("att_copied")
        block = ctx.enter_context(nc.Block())
        flat = attn.rearrange("a h c -> (a h c)")

        @block.sync
        def _(sp):
            for c in range(D // P):
                sp.dma_start(a_col[:, c:c + 1], flat[c * P:(c + 1) * P].unsqueeze(1)).then_inc(loaded, 16)
                sp.dma_start(be_col[:, c:c + 1], be[c * P:(c + 1) * P].unsqueeze(1)).then_inc(loaded, 16)
            sp.dma_start(we[:, :, :], We.rearrange("(c p) n -> p c n", p=P)).then_inc(loaded, 16)
            sp.dma_start(attn_row[:, :], flat.partition_broadcast(P)).then_inc(loaded, 16)

        @block.tensor
        def _(pe):
            pe.wait_ge(loaded, 16 * (2 * (D // P) + 2))
            for c in range(D // P):
                pe.matmul(p_v[:, 0:A], a_col[:, c:c + 1].to_broadcast([P, P]), we[:, c, :], start=(c == 0), stop=(c == D // P - 1))
            for c in range(D // P):
                last = pe.matmul(p_v[:, A:A + 1], a_col[:, c:c + 1].to_broadcast([P, P]), be_col[:, c:c + 1],
                                 start=(c == 0), stop=(c == D // P - 1))
            last.then_inc(made, 1)

        @block.vector
        def _(v):
            v.wait_ge(made, 1)
            v.tensor_copy(v_row[:, :], p_v[:, 0:A]).then_inc(copied, 1)
            v.tensor_copy(const[:, :], p_v[:, A:A + 1]).then_inc(copied, 1)
            v.wait_ge(copied, 2)


def attention_output(nc, k, out):
    D = k.D
    full, rest = k.N // P, k.N - k.N // P * P
    with ExitStack() as ctx:
        sb, ps, sem = scope(nc, ctx)
        rden = sb("rden", [P, k.NB])
        link_s, done, stored = sem("out_dve_chain"), sem("out_done"), sem("out_stored")
        block = ctx.enter_context(nc.Block())

        @block.vector
        def _(v):
            link = chain(v, link_s)
            link(v.tensor_scalar(rden[:, :], k.AGG[:, :, D], 1e-16, None, ALU.add))
            link(v.reciprocal(rden[:, :], rden[:, :]))
            link(v.tensor_tensor(k.AGG[:, :, 0:D], k.AGG[:, :, 0:D], wide(rden[:, :], D), ALU.mult))
            v.scalar_tensor_tensor(k.X[:, :, :], k.AGG[:, :, 0:D], 0.0, k.X[:, :, :], ALU.max, ALU.add).then_inc(done, 1)

        @block.sync
        def _(sp):
            sp.wait_ge(done, 1)
            sp.dma_start(out[0:full * P, :].rearrange("(b p) d -> p b d", p=P), k.X[:, 0:full, :]).then_inc(stored, 16)
            sp.dma_start(out[full * P:k.N, :], k.X[0:rest, full, :]).then_inc(stored, 16)
            sp.wait_ge(stored, 32)



def gnn(nc, x, src, dst, edge_attr_128, edge_attr_64,
        L0_W1_l, L0_b1, L0_W1_r, L0_W2_l, L0_b2, L0_W2_r,
        L1_W1, L1_b1, L1_W2, L1_b2, L1_Wg, L1_bg, L1_gamma, L1_beta,
        L2_W1, L2_b1, L2_g1, L2_be1, L2_W2, L2_b2, L2_g2, L2_be2, L2_Wfc, L2_bfc,
        L3_Wn, L3_bn, L3_We, L3_be, L3_attn, out):
    k = Core()
    k.nc = nc
    k.N, k.D = x.shape
    k.E = src.shape[0]
    k.T = ceil_div(k.E, P)
    k.NBU = ceil_div(k.N, P)
    k.NB = k.NBU + k.NBU % 2
    k.NSTEP = ceil_div(k.T + k.NBU - 1, 4 * QUAD) * 4 * QUAD
    k.NSTEP_PAD = ceil_div(k.NSTEP + 4 * QUAD, P) * P
    D, NB = k.D, k.NB
    d1, d2 = L2_W1.shape[1], L2_W2.shape[1]
    rows = NB * P

    def dram(name, w, n=rows):
        return nc.dram_tensor(name, [n, w], F32, kind="Internal").ap()

    table_h0, table_h1 = dram("table_h0", D + 2), dram("table_h1", D + 2)
    table_mlp, table_g1, table_g2 = dram("table_mlp", 2 * D), dram("table_g1", d1), dram("table_g2", d2)
    table_att = dram("table_att", D + 2)
    tiles_dram = dram("tiles_dram", 2 * P, k.NSTEP_PAD)

    with ExitStack() as ctx:
        sb, ps, sem = scope(nc, ctx)
        k.X = sb("X", [P, NB, D])
        k.srcS, k.drelS = sb("srcS", [P, k.NSTEP_PAD], I32), sb("drelS", [P, k.NSTEP_PAD])
        k.baseT, k.blkT = sb("baseT", [1, k.NSTEP_PAD], I32), sb("blkT", [1, k.NSTEP_PAD], I32)
        k.ident, k.iota, k.ones, k.valid = sb("ident", [P, P]), sb("iota", [P, P]), sb("ones", [P, P]), sb("valid", [P, P])
        k.rdeg, k.dinv = sb("rdeg", [P, NB]), sb("dinv", [P, NB])

        k.constants_made = sem("constants_made")
        k.held, k.held_pe = sem("held_pool"), sem("held_pe")
        load_and_constants(nc, k, x)
        step_tables(nc, k, src, dst, tiles_dram)
        k.H = sb("H", [P, NB, D + 2])

        def agg(scope_):
            k.AGG = scope_.enter_context(nc.sbuf_tensor(f"AGG_{next(SCOPES)}", [P, NB, D + 1], F32))

        def matrix(sb, name, w):
            K, n = w.shape
            dmas, pieces = [], []
            for c in range(ceil_div(K, P)):
                rows_c = min(P, K - c * P)
                t = sb(f"{name}{c}", [P, n])
                dmas.append((t[0:rows_c, :], w[c * P:c * P + rows_c, :]))
                pieces.append((rows_c, t[0:rows_c, :]))
            return dmas, pieces

        def bias_row(sb, b):
            t = sb("bias_row", [1, b.shape[0]])
            return [(t[:, :], b.unsqueeze(0))], t[:, :]

        first = ExitStack()
        agg(first)
        norm_relu(nc, k, "ln0", table_h0)
        sum_pass(nc, k, "sage1", table_h0, D + 1, 0)
        degrees(nc, k)

        def sage(name, Wl, b, Wr, finish):
            def loads(sb):
                d1_, p1 = matrix(sb, "wl", Wl)
                d2_, p2 = matrix(sb, "wr", Wr)
                d3_, bias = bias_row(sb, b)
                return d1_ + d2_ + d3_, p1 + p2, bias

            def mean(v, buf, blk):
                return v.tensor_scalar(buf[:, 0:D], rows_of(k.AGG, blk, 0, D), k.rdeg[:, bass.ds(blk, 1)], None, ALU.mult)

            def own(pool, buf, blk):
                return pool.tensor_copy(buf[:, D:2 * D], rows_of(k.H, blk, 0, D))
            node_product(nc, k, name, loads, D, 2 * D, {"vector": mean, "gpsimd": own}, finish)

        sage("sage1_out", L0_W1_l, L0_b1, L0_W1_r,
             ("scalar", lambda act, p, blk, o: act.activation(rows_of(k.H, blk, 0, D), p[:, 0:D], ACT.Relu), None))
        store_table(nc, k, "h1", table_h1, k.H[:, :, :])
        sum_pass(nc, k, "sage2", table_h1, D, 0)

        def add_to_x(v, p, blk, o):
            return v.tensor_tensor(rows_of(k.X, blk, 0, D), p[:, 0:D], rows_of(k.X, blk, 0, D), ALU.add)
        sage("sage2_out", L0_W2_l, L0_b2, L0_W2_r, ("vector", add_to_x, None))

        first.close()

        def own_h(pool, buf, blk):
            return pool.tensor_copy(buf[:, 0:D], rows_of(k.H, blk, 0, D))

        norm_relu(nc, k, "ln1")

        def mlp_loads(sb):
            both = [sb(f"w1g{c}", [P, 2 * D]) for c in range(D // P)]
            brow = sb("b1g", [1, 2 * D])
            dmas = [(both[c][:, i * D:(i + 1) * D], w[c * P:(c + 1) * P, :])
                    for c in range(D // P) for i, w in enumerate((L1_W1, L1_Wg))]
            dmas += [(brow[:, i * D:(i + 1) * D], b.unsqueeze(0)) for i, b in enumerate((L1_b1, L1_bg))]
            return dmas, [(P, w[:, :]) for w in both], brow[:, :]
        node_product(nc, k, "mlp_in", mlp_loads, 2 * D, D, {"gpsimd": own_h},
                     ("scalar", lambda act, p, blk, o: act.copy(o[:, :], p[:, :]), table_mlp))
        edge_mlp_pass(nc, k, "mlp", table_mlp, edge_attr_64, L1_W1, L1_Wg, L1_W2, L1_b2)
        gated_output(nc, k, L1_gamma, L1_beta)

        agg(ctx)
        norm_relu(nc, k, "ln2")

        def scaled(lo, W):
            return lambda act, p, blk, o: act.activation(rows_of(k.AGG, blk, lo, lo + W), p[:, 0:W], ACT.Copy,
                                                         scale=k.dinv[:, bass.ds(blk, 1)])
        node_product(nc, k, "gcn1_in", lambda sb: (*matrix(sb, "w", L2_W1), None), d1, D, {"gpsimd": own_h},
                     ("scalar", scaled(d1, d1), None))
        store_table(nc, k, "g1", table_g1, k.AGG[:, :, d1:2 * d1])
        sum_pass(nc, k, "gcn1", table_g1, d1, 0)
        graph_norm(nc, k, "bn1", 0, d1, d1, L2_b1, L2_g1, L2_be1)
        node_product(nc, k, "gcn2_in", lambda sb: (*matrix(sb, "w", L2_W2), None), d2, d1,
                     {"gpsimd": lambda pool, buf, blk: pool.tensor_copy(buf[:, 0:d1], rows_of(k.AGG, blk, 0, d1))},
                     ("scalar", scaled(d1 + d2, d2), None))
        store_table(nc, k, "g2", table_g2, k.AGG[:, :, d1 + d2:d1 + 2 * d2])
        sum_pass(nc, k, "gcn2", table_g2, d2, d1)
        graph_norm(nc, k, "bn2", d1, d2, d1 + d2, L2_b2, L2_g2, L2_be2)

        def fc_loads(sb):
            dmas, pieces = matrix(sb, "wfc", L2_Wfc)
            d, bias = bias_row(sb, L2_bfc)
            return dmas + d, pieces, bias
        node_product(nc, k, "fc", fc_loads, D, D + d1 + d2,
                     {"gpsimd": own_h, "vector": lambda v, buf, blk: v.tensor_scalar(buf[:, D:D + d1 + d2], rows_of(k.AGG, blk, 0, d1 + d2), 1.0, None, ALU.mult)},
                     ("vector", lambda v, p, blk, o: v.scalar_tensor_tensor(rows_of(k.X, blk, 0, D), p[:, 0:D], 0.0,
                                                                            rows_of(k.X, blk, 0, D), ALU.max, ALU.add), None))

        norm_relu(nc, k, "ln3")
        v_row = sb("v_row", [P, L3_We.shape[1]])
        inner = ExitStack()
        sb_in, _, sem_in = scope(nc, inner)
        attn_row, const = sb_in("attn_row", [P, D]), sb_in("const", [P, 1])
        attention_constants(nc, k, L3_attn, L3_We, L3_be, v_row, attn_row, const)
        wnT = sb_in("wnT", [P, D // P, D])
        turn_weights(nc, k, L3_Wn, wnT)
        prod, part = sb_in("prod", [P, D]), sb_in("part", [P, 2])
        node_rows_done = sem_in("att_in_rows")

        def att_loads(sb):
            d, bias = bias_row(sb, L3_bn)
            return d, [(P, wnT[:, c, :]) for c in range(D // P)], bias

        att_steps = [0]

        def att_row(v, p, blk, o):
            u = att_steps[0] % 2
            att_steps[0] += 1
            v.tensor_scalar(rows_of(k.H, blk, 0, D), p[:, 0:D], 1.0, None, ALU.mult)
            v.tensor_tensor_reduce(prod[:, :], p[:, 0:D], attn_row[:, :], 1.0, const[:, 0:1], ALU.mult, ALU.add,
                                   part[:, u:u + 1]).then_inc(node_rows_done, 1)
            v.wait_ge(node_rows_done, blk + 1)
            return v.tensor_scalar(rows_of(k.H, blk, D + 1, D + 2), part[:, u:u + 1], 1.0, None, ALU.mult)
        node_product(nc, k, "att_in", att_loads, D, D, {"gpsimd": own_h}, ("vector", att_row, None))
        store_table(nc, k, "att", table_att, k.H[:, :, :])
        inner.close()
        attention_pass(nc, k, "att", table_att, edge_attr_128, v_row[:, :])
        attention_output(nc, k, out)


def turn_weights(nc, k, W, wT):
    n, m = W.shape
    with ExitStack() as ctx:
        sb, ps, sem = scope(nc, ctx)
        w_in = sb("w_in", [P, n // P, m])
        p_w = ps("p_w", [P, m // P, n])
        loaded, turned, copied = sem("wn_loaded"), sem("wn_turned"), sem("wn_copied")
        block = ctx.enter_context(nc.Block())

        @block.sync
        def _(sp):
            sp.dma_start(w_in[:, :, :], W.rearrange("(a p) m -> p a m", p=P)).then_inc(loaded, 16)

        @block.tensor
        def _(pe):
            pe.wait_ge(loaded, 16)
            for c in range(m // P):
                for a in range(n // P):
                    last = pe.transpose(p_w[:, c, a * P:(a + 1) * P], w_in[:, a, c * P:(c + 1) * P], k.ident[:, :])
            last.then_inc(turned, 1)

        @block.vector
        def _(v):
            v.wait_ge(turned, 1)
            v.tensor_copy(wT[:, :, :], p_w[:, :, :]).then_inc(copied, 1)
            v.wait_ge(copied, 1)


_INS = ['x', 'src', 'dst', 'edge_attr_128', 'edge_attr_64', 'L0_gnn_W1_l', 'L0_gnn_b1', 'L0_gnn_W1_r', 'L0_gnn_W2_l',
        'L0_gnn_b2', 'L0_gnn_W2_r', 'L1_gnn_W1', 'L1_gnn_b1', 'L1_gnn_W2', 'L1_gnn_b2', 'L1_gnn_Wg', 'L1_gnn_bg',
        'L1_gnn_gamma', 'L1_gnn_beta', 'L2_gnn_W1', 'L2_gnn_b1', 'L2_gnn_g1', 'L2_gnn_be1', 'L2_gnn_W2', 'L2_gnn_b2',
        'L2_gnn_g2', 'L2_gnn_be2', 'L2_gnn_Wfc', 'L2_gnn_bfc', 'L3_gnn_Wn', 'L3_gnn_bn', 'L3_gnn_We', 'L3_gnn_be',
        'L3_gnn_attn']


def build(nc, shapes):
    args = [nc.dram_tensor(f"in_{name}_dram", shape, dt, kind="ExternalInput").ap() for name, shape, dt in shapes]
    out = nc.dram_tensor("out_0_dram", shapes[0][1], F32, kind="ExternalOutput").ap()
    gnn(nc, *args, out)


def kernel(**inputs):
    import numpy as _np
    import concourse.bacc as _bacc
    from concourse import mybir as _mybir
    from concourse.bass_utils import run_bass_kernel_spmd as _run

    nc = _bacc.Bacc("TRN2", target_bir_lowering=False, num_devices=1)
    arrays, shapes = {}, []
    for name in _INS:
        a = _np.ascontiguousarray(inputs[name])
        arrays[f"in_{name}_dram"] = a
        shapes.append((name, a.shape, _mybir.dt.from_np(a.dtype)))
    build(nc, shapes)
    r = _run(nc, [arrays], core_ids=[0])
    return r.results[0]["out_0_dram"]
```

```python
import itertools
from contextlib import ExitStack

import concourse.bass as bass
from concourse import mybir

ALU = mybir.AluOpType
ACT = mybir.ActivationFunctionType
F32 = mybir.dt.float32
F32R = mybir.dt.float32r
I32 = mybir.dt.int32
AX_X = mybir.AxisListType.X

P = 128
QUAD = 4
GROUP = 10
EPS = 1e-5
FAR = 2.0 ** 20
FARTHER = 2.0 ** 40
FLOOR = -1e23


CONSTANTS = 7
SCOPES = itertools.count()


def ceil_div(a, b):
    return -(-a // b)


class Core:
    pass


def scope(nc, ctx):
    n = next(SCOPES)

    def sb(name, shape, dt=F32):
        return ctx.enter_context(nc.sbuf_tensor(f"{name}_{n}", shape, dt))

    def ps(name, shape, dt=F32):
        return ctx.enter_context(nc.psum_tensor(f"{name}_{n}", shape, dt))

    sems = []

    def sem(name):
        sems.append(nc.alloc_semaphore(name))
        return sems[-1]

    def clear():
        if sems:
            nc.clear_and_free_semaphores(sems)
            nc.all_engine_barrier(sem_only=True)
    ctx.callback(clear)
    return sb, ps, sem


def hold(eng, held):
    eng.sem_inc(held, 1)


def chain(eng, sem, start=0):
    count = [0]

    def link(ins):
        count[0] += 1
        ins.then_inc(sem, 1)
        eng.wait_ge(sem, start + count[0])
    return link



def load_and_constants(nc, k, x):
    with ExitStack() as ctx:
        sb, ps, sem = scope(nc, ctx)
        zeroed, row_i = sem("x_pad_zeroed"), sb("row_i", [P, P], I32)
        made = k.constants_made
        block = ctx.enter_context(nc.Block())
        full = k.N // P
        rest = k.N - full * P

        @block.gpsimd
        def _(pool):
            pool.memset(k.X[:, full:k.NB, :], 0.0).then_inc(zeroed, 1)
            pool.memset(k.ones[:, :], 1.0).then_inc(made, 1)
            pool.memset(k.valid[:, :], 1.0).then_inc(made, 1)
            pool.memset(k.ident[:, :], 1.0).then_inc(made, 1)
            pool.iota(row_i[:, :], pattern=[[1, P]], base=0, channel_multiplier=0).then_inc(made, 1)
            pool.wait_ge(made, 4)
            pool.affine_select(out=k.ident[:, :], in_=k.ident[:, :], pattern=[[-1, P]], base=0,
                               channel_multiplier=1, compare_op=ALU.is_equal, fill=0.0).then_inc(made, 1)
            pool.affine_select(out=k.valid[:, :], in_=k.valid[:, :], pattern=[[0, P]], base=rest - 1,
                               channel_multiplier=-1, compare_op=ALU.is_ge, fill=0.0).then_inc(made, 1)
            pool.tensor_copy(k.iota[:, :], row_i[:, :]).then_inc(made, 1)
            pool.wait_ge(made, CONSTANTS)

        @block.scalar
        def _(act):
            act.dma_start(k.X[:, 0:full, :], x[0:full * P, :].rearrange("(b p) d -> p b d", p=P)).then_inc(k.x_loaded, 16)
            act.wait_ge(zeroed, 1)
            act.dma_start(k.X[0:rest, full, :], x[full * P:k.N, :]).then_inc(k.x_loaded, 16)


def step_tables(nc, k, src, dst, tiles_dram):
    T, C = k.T, k.NSTEP_PAD // P
    full = k.E // P
    whole = full // P
    some = full - whole * P
    first_own = P - (k.E - full * P)
    assert T == full + 1 and C * P >= T + k.NBU - 1 and C == whole + 1
    with ExitStack() as ctx:
        sb, ps, sem = scope(nc, ctx)
        raw = sb("raw", [P, C, 2, P], I32)
        rows = sb("rows", [P, C, 2, P])
        lane_no_i = sb("lane_no_i", [P, P], I32)
        tile_no_i = sb("tile_no_i", [P, C], I32)
        all_no_i = sb("all_no_i", [P, C * P], I32)
        upto = sb("upto", [P, P])
        dup, dup2 = sb("dup", [P, P]), sb("dup2", [P, P])
        tile_no, all_no = sb("tile_no", [P, C]), sb("all_no", [P, C * P])
        lo, hi = sb("lo", [P, C]), sb("hi", [P, C])
        lo_i, hi_i = sb("lo_i", [P, C], I32), sb("hi_i", [P, C], I32)
        cnt, incl, start = sb("cnt", [P, C]), sb("incl", [P, C]), sb("start", [P, C])
        incl_r, start_r = sb("incl_r", [P, C * P]), sb("start_r", [P, C * P])
        junk = sb("junk", [P, C * P])
        t_of, b_of, t_of_i = sb("t_of", [P, C]), sb("b_of", [P, C]), sb("t_of_i", [P, C], I32)
        base, b_in, b128 = sb("base", [P, C]), sb("b_in", [P, C]), sb("b128", [P, C])
        picked = sb("picked", [P, C, 2 * P])
        p_small = ps("p_small", [P, 512])
        p_rows = ps("p_rows", [P, 2, 1024])
        cleared, loaded, consts, counted, summed = (sem(n) for n in ("tab_cleared", "tab_loaded", "tab_consts", "tab_counted", "tab_summed"))
        placed, spread, rows_ready, rows_stored = (sem(n) for n in ("tab_placed", "tab_spread", "tab_rows_ready", "tab_rows_stored"))
        steps_ready, gathered, rel_ready, turned, link_s = (sem(n) for n in ("tab_steps_ready", "tab_gathered", "tab_rel_ready", "tab_turned", "tab_dve_chain"))
        taken = sem("tab_stats_taken")
        block = ctx.enter_context(nc.Block())

        @block.sync
        def _(sp):
            sp.wait_ge(cleared, 1)
            for i, a in enumerate((dst, src)):
                sp.dma_start(raw[:, 0:whole, i, :], a[0:whole * P * P].rearrange("(c p l) -> p c l", p=P, l=P)).then_inc(loaded, 16)
                sp.dma_start(raw[0:some, whole, i, :], a[whole * P * P:full * P].rearrange("(p l) -> p l", l=P)).then_inc(loaded, 16)
                sp.dma_start(raw[some:some + 1, whole, i, :], a[k.E - P:k.E].unsqueeze(0)).then_inc(loaded, 16)
            sp.wait_ge(rows_ready, 1)
            sp.dma_start(tiles_dram.rearrange("(c p) w -> p c w", p=P), rows[:, :, :, :].rearrange("p c a l -> p c (a l)")).then_inc(rows_stored, 16)

        @block.gpsimd
        def _(pool):
            pool.memset(raw[:, :, :, :], 0).then_inc(cleared, 1)
            pool.iota(lane_no_i[:, :], pattern=[[1, P]], base=0, channel_multiplier=P)
            pool.iota(tile_no_i[:, :], pattern=[[P, C]], base=0, channel_multiplier=1)
            pool.iota(all_no_i[:, :], pattern=[[1, C * P]], base=0, channel_multiplier=0)
            pool.memset(upto[:, :], 1.0).then_inc(consts, 1)
            pool.wait_ge(consts, 1)
            pool.affine_select(out=upto[:, :], in_=upto[:, :], pattern=[[1, P]], base=0,
                               channel_multiplier=-1, compare_op=ALU.is_ge, fill=0.0).then_inc(consts, 1)
            pool.wait_ge(rows_stored, 16)
            pool.wait_ge(steps_ready, 1)
            for c in range(C):
                pool.indirect_dma_start(out=picked[:, c, :], out_offset=None, in_=tiles_dram,
                                        in_offset=bass.IndirectOffsetOnAxis(ap=t_of_i[:, c:c + 1], axis=0)).then_inc(gathered, 16)

        @block.vector
        def _(v):
            link = chain(v, link_s)
            v.wait_ge(consts, 2)
            link(v.tensor_copy(dup[:, :], lane_no_i[:, :]))
            link(v.tensor_scalar(dup2[:, :], dup[:, :], float(some * P), FAR, ALU.is_ge, ALU.mult))
            link(v.tensor_scalar(dup[:, :], dup[:, :], float(some * P + first_own), None, ALU.is_lt))
            link(v.tensor_tensor(dup[:, :], dup[:, :], dup2[:, :], ALU.mult))
            link(v.tensor_copy(tile_no[:, :], tile_no_i[:, :]))
            link(v.tensor_copy(all_no[:, :], all_no_i[:, :]))
            v.wait_ge(loaded, 96)
            link(v.tensor_copy(rows[:, :, :, :], raw[:, :, :, :]))
            link(v.tensor_reduce(hi[:, :], rows[:, :, 0, :], AX_X, ALU.max))
            v.tensor_tensor(rows[:, whole, 0, :], rows[:, whole, 0, :], dup[:, :], ALU.add).then_inc(rows_ready, 1)
            v.wait_ge(rows_ready, 1)
            link(v.tensor_reduce(lo[:, :], rows[:, :, 0, :], AX_X, ALU.min))
            link(v.tensor_copy(hi_i[:, :], hi[:, :]))
            link(v.tensor_copy(lo_i[:, :], lo[:, :]))
            link(v.tensor_scalar(hi_i[:, :], hi_i[:, :], 7, None, ALU.arith_shift_right))
            link(v.tensor_scalar(lo_i[:, :], lo_i[:, :], 7, None, ALU.arith_shift_right))
            link(v.tensor_copy(hi[:, :], hi_i[:, :]))
            link(v.tensor_copy(lo[:, :], lo_i[:, :]))
            link(v.tensor_tensor(cnt[:, :], hi[:, :], lo[:, :], ALU.subtract))
            link(v.tensor_scalar(hi[:, :], tile_no[:, :], float(T), None, ALU.is_lt))
            v.scalar_tensor_tensor(cnt[:, :], cnt[:, :], 1.0, hi[:, :], ALU.add, ALU.mult).then_inc(counted, 1)
            v.wait_ge(counted, 1)
            v.wait_ge(summed, 1)
            link(v.tensor_copy(incl[:, :], p_small[:, 0:C]))
            link(v.tensor_tensor(start[:, :], cnt[:, :], incl[:, :], ALU.subtract))
            v.tensor_tensor(start[:, :], start[:, :], lo[:, :], ALU.add).then_inc(placed, 1)
            v.wait_ge(spread, 1)
            link(v.tensor_copy(incl_r[:, :], p_rows[:, 0, 0:C * P]))
            link(v.tensor_copy(start_r[:, :], p_rows[:, 1, 0:C * P]))
            for c in range(C):
                link(v.tensor_scalar(junk[:, :], incl_r[:, :], tile_no[:, c:c + 1], 0.0, ALU.is_le, ALU.add, accum_out=t_of[:, c:c + 1]))
            link(v.tensor_scalar(t_of[:, :], t_of[:, :], float(T - 1), None, ALU.min))
            for c in range(C):
                link(v.scalar_tensor_tensor(junk[:, :], all_no[:, :], t_of[:, c:c + 1], start_r[:, :], ALU.is_equal, ALU.mult, accum_out=b_of[:, c:c + 1]))
            v.tensor_copy(t_of_i[:, :], t_of[:, :]).then_inc(steps_ready, 1)
            link(v.tensor_tensor(b_of[:, :], b_of[:, :], tile_no[:, :], ALU.add))
            link(v.tensor_scalar(b128[:, :], b_of[:, :], float(P), None, ALU.mult))
            link(v.tensor_scalar(b_in[:, :], b_of[:, :], float(k.NB - 1), 0.0, ALU.min, ALU.max))
            link(v.tensor_scalar(base[:, :], t_of[:, :], float(P), float(k.E - P), ALU.mult, ALU.min))
            v.wait_ge(k.x_loaded, 32)
            with v.Fori(0, k.NB // GROUP) as j:
                for u in range(GROUP):
                    row_stats(v, k, rows_of(k.X, GROUP * j + u, 0, k.D), GROUP * j + u).then_inc(taken, 1)
            v.wait_ge(taken, k.NB)
            v.wait_ge(gathered, 16 * C)
            for c in range(C):
                v.tensor_scalar(picked[:, c, 0:P], picked[:, c, 0:P], b128[:, c:c + 1], None, ALU.subtract).then_inc(rel_ready, 1)
            v.wait_ge(turned, 1)
            link(v.tensor_copy(k.drelS[:, :], p_rows[:, 0, 0:C * P]))
            link(v.tensor_copy(k.srcS[:, :], p_rows[:, 1, 0:C * P]))
            v.tensor_copy(junk[:, 0:1], base[:, 0:1]).then_inc(rel_ready, 1)
            v.wait_ge(turned, 2)
            link(v.tensor_copy(k.baseT[0:1, :], p_rows[0:1, 0, 0:C * P]))
            link(v.tensor_copy(k.blkT[0:1, :], p_rows[0:1, 1, 0:C * P]))

        @block.tensor
        def _(pe):
            pe.wait_ge(consts, 2)
            pe.wait_ge(counted, 1)
            for c in range(C):
                last = pe.matmul(p_small[:, c:c + 1], upto[:, :], cnt[:, c:c + 1], start=True, stop=(c == 0))
                for d in range(c):
                    last = pe.matmul(p_small[:, c:c + 1], k.ones[:, :], cnt[:, d:d + 1], start=False, stop=(d == c - 1))
            last.then_inc(summed, 1)

            def spread_rows(i, a):
                for c in range(C):
                    last = pe.matmul(p_rows[:, i, c * P:(c + 1) * P], a[:, c:c + 1].to_broadcast([P, P]), k.ident[:, :], start=True, stop=True)
                return last
            pe.wait_ge(placed, 1)
            spread_rows(0, incl)
            spread_rows(1, start).then_inc(spread, 1)
            pe.wait_ge(rel_ready, C)
            for c in range(C):
                for i in range(2):
                    last = pe.transpose(p_rows[:, i, c * P:(c + 1) * P], picked[:, c, i * P:(i + 1) * P], k.ident[:, :])
            last.then_inc(turned, 1)
            pe.wait_ge(rel_ready, C + 1)
            spread_rows(0, base)
            spread_rows(1, b_in).then_inc(turned, 1)



def row_stats(v, k, src, b):
    return v.bn_stats(k.stats[:, bass.ds(b, 1), :].rearrange("p b s -> p (b s)"), src)


def layer_norm_constants(nc, k, name, rstd, shift, src=None):
    with ExitStack() as ctx:
        sb, ps, sem = scope(nc, ctx)
        mean, half, var = sb("mean", [P, k.NB]), sb("half", [P, k.NB]), sb("var", [P, k.NB])
        stats, var_ready, std_ready, link_s = sem(f"{name}_stats"), sem(f"{name}_var_ready"), sem(f"{name}_std_ready"), sem(f"{name}_dve_chain")
        block = ctx.enter_context(nc.Block())

        @block.vector
        def _(v):
            link = chain(v, link_s)
            if src is not None:
                with v.Fori(0, k.NB // GROUP) as j:
                    for u in range(GROUP):
                        row_stats(v, k, rows_of(src, GROUP * j + u, 0, k.D), GROUP * j + u).then_inc(stats, 1)
                v.wait_ge(stats, k.NB)
            st = k.stats
            link(v.tensor_tensor(mean[:, :], st[:, :, 1], st[:, :, 4], ALU.add))
            link(v.tensor_tensor(half[:, :], st[:, :, 1], st[:, :, 4], ALU.subtract))
            link(v.tensor_tensor(var[:, :], st[:, :, 2], st[:, :, 5], ALU.add))
            link(v.tensor_scalar(half[:, :], half[:, :], 0.5, None, ALU.mult))
            link(v.tensor_tensor(half[:, :], half[:, :], half[:, :], ALU.mult))
            link(v.tensor_scalar(var[:, :], var[:, :], 1.0 / k.D, EPS, ALU.mult, ALU.add))
            v.tensor_tensor(var[:, :], var[:, :], half[:, :], ALU.add).then_inc(var_ready, 1)
            v.wait_ge(std_ready, 1)
            link(v.reciprocal(rstd[:, :], var[:, :]))
            link(v.scalar_tensor_tensor(shift[:, :], mean[:, :], -0.5, rstd[:, :], ALU.mult, ALU.mult))

        @block.scalar
        def _(act):
            act.wait_ge(var_ready, 1)
            act.activation(var[:, :], var[:, :], ACT.Sqrt).then_inc(std_ready, 1)


def norm_relu(act, k, b):
    return act.activation(rows_of(k.H, b, 0, k.D), rows_of(k.X, b, 0, k.D), ACT.Relu,
                          bias=k.shift[:, bass.ds(b, 1)], scale=k.rstd[:, bass.ds(b, 1)])


def first_norm(nc, k, name, table):
    layer_norm_constants(nc, k, name, k.rstd, k.shift)
    with ExitStack() as ctx:
        sb, ps, sem = scope(nc, ctx)
        normed, ones_set, stored = sem(f"{name}_normed"), sem(f"{name}_ones_set"), sem(f"{name}_stored")
        with nc.Block() as block:
            @block.gpsimd
            def _(pool):
                pool.memset(k.H[:, :, k.D:k.D + 2], 1.0).then_inc(ones_set, 1)

            @block.scalar
            def _(act):
                with act.Fori(0, k.NB // GROUP) as j:
                    for u in range(GROUP):
                        norm_relu(act, k, GROUP * j + u).then_inc(normed, 1)

            @block.sync
            def _(sp):
                sp.wait_ge(ones_set, 1)
                rows = table.rearrange("(b p) w -> p b w", p=P)
                with sp.Fori(0, k.NB // GROUP) as j:
                    sp.wait_ge(normed, GROUP * (j + 1))
                    sp.dma_start(rows[:, bass.ds(GROUP * j, GROUP), :], k.H[:, bass.ds(GROUP * j, GROUP), :]).then_inc(stored, 16)
                sp.wait_ge(stored, 16 * (k.NB // GROUP))


def node_product(nc, k, name, loads, biases, width, row, stage, finish, prepare=None, store=None, keep=None, stats=False):
    with ExitStack() as ctx:
        sb, ps, sem = scope(nc, ctx)
        dmas, weights = loads(sb)
        chunks, Q = len(weights), 2
        both = range(Q)
        inb = [sb(f"in_rows{u}", [P, row]) for u in both]
        turned_sb = [sb(f"turned_sb{u}", [P, chunks * P]) for u in both]
        p_turn = [ps(f"p_turn{u}", [P, chunks * P]) for u in both]
        p_out = [ps(f"p_out{u}", [P, 512]) for u in both]
        out_sb = [sb(f"out_sb{u}", [P, width]) for u in both] if store is not None else [None, None]
        if biases:
            ones2 = sb("ones2", [2, P], F32R)
            b_in, b_high, b_parts = sb("b_in", [2, width]), sb("b_high", [2, width], F32R), sb("b_parts", [2, width], F32R)
            at = 0
            for b in biases:
                dmas = dmas + [(b_in[:, at:at + b.shape[0]], b.partition_broadcast(2))]
                at += b.shape[0]
        w_loaded, bias_ready, bias_chain, prepared = (sem(f"{name}_{n}") for n in ("w_loaded", "bias_ready", "bias_chain", "prepared"))
        staged = [sem(f"{name}_staged{u}") for u in both]
        turned, copied, product, finished = (sem(f"{name}_{n}") for n in ("turned", "copied", "product", "finished"))
        stored = [sem(f"{name}_stored{u}") for u in both]
        taken, kept = sem(f"{name}_stats_taken"), sem(f"{name}_kept")
        fin_engine, fin = finish
        rounds = k.NB // Q
        block = ctx.enter_context(nc.Block())

        def stage_one(eng, f, j, u):
            if prepare is not None:
                eng.wait_ge(prepared, Q * j + u + 1)
            eng.wait_ge(turned, Q * j + u + 1)
            f(eng, inb[u], Q * j + u).then_inc(staged[u], 1)

        def finish_one(eng, j, u):
            n = Q * j + u
            eng.wait_ge(product, n + 3)
            if store is not None:
                eng.wait_ge(stored[u], 16 * (j + 1))
            fin(eng, p_out[u], n, out_sb[u]).then_inc(finished, 1)

        @block.sync
        def _(sp):
            for s in stored:
                sp.sem_inc(s, 16)
            for to, of in dmas:
                sp.dma_start(to, of).then_inc(w_loaded, 16)
            if store is not None:
                with sp.Fori(0, rounds) as j:
                    for u in both:
                        sp.wait_ge(finished, Q * j + u + 3)
                        sp.dma_start(store[bass.ds((Q * j + u) * P, P), :], out_sb[u][:, :]).then_inc(stored[u], 16)
                for u in both:
                    sp.wait_ge(stored[u], 16 * (rounds + 1))
            if keep is not None:
                to = keep[0].rearrange("(b p) w -> p b w", p=P)
                with sp.Fori(0, k.NB // GROUP) as j:
                    sp.wait_ge(finished, GROUP * (j + 1) + 2)
                    sp.dma_start(to[:, bass.ds(GROUP * j, GROUP), :], keep[1][:, bass.ds(GROUP * j, GROUP), :]).then_inc(kept, 16)
                sp.wait_ge(kept, 16 * (k.NB // GROUP))

        @block.tensor
        def _(pe):
            def turn(j, u):
                n = Q * j + u
                pe.wait_ge(staged[u], len(stage) * (j + 1))
                pe.wait_ge(copied, n + 1)
                at = 0
                for c, (K, _) in enumerate(weights):
                    last = pe.transpose(p_turn[u][0:K, c * P:(c + 1) * P], inb[u][:, at:at + K], k.ident[:, :])
                    at += K
                last.then_inc(turned, 1)

            def multiply(j, u):
                n = Q * j + u
                pe.wait_ge(copied, n + 3)
                pe.wait_ge(finished, n + 1)
                for c, (K, w) in enumerate(weights):
                    last = pe.matmul(p_out[u][:, 0:width], turned_sb[u][0:K, c * P:(c + 1) * P], w,
                                     start=(c == 0), stop=(c == chunks - 1 and not biases))
                if biases:
                    last = pe.matmul(p_out[u][:, 0:width], ones2[:, :], b_parts[:, :], start=False, stop=True)
                last.then_inc(product, 1)

            def step(blocks):
                now, then = blocks
                if then is not None:
                    turn(*then)
                if now is not None:
                    multiply(*now)
            pe.sem_inc(turned, 2)
            pe.sem_inc(product, 2)
            pe.wait_ge(w_loaded, 16 * len(dmas))
            if biases:
                pe.wait_ge(bias_ready, 3)
            pipelined(pe, rounds, Q, step, 1)

        Ks = [K for K, _ in weights]

        @block.scalar
        def _(act):
            def copy_turned(j, u):
                n = Q * j + u
                act.wait_ge(turned, n + 3)
                act.wait_ge(product, n + 1)
                n_full = sum(K == P for K in Ks)
                last = act.copy(turned_sb[u][:, 0:n_full * P], p_turn[u][:, 0:n_full * P])
                for c, K in enumerate(Ks):
                    if K != P:
                        last = act.copy(turned_sb[u][0:K, c * P:(c + 1) * P], p_turn[u][0:K, c * P:(c + 1) * P])
                last.then_inc(copied, 1)

            def step(blocks):
                now, then, _, later = blocks
                if later is not None and prepare is not None:
                    prepare(act, Q * later[0] + later[1]).then_inc(prepared, 1)
                if then is not None:
                    copy_turned(*then)
                if now is not None and fin_engine == "scalar":
                    finish_one(act, *now)
            act.sem_inc(copied, 2)
            if fin_engine == "scalar":
                act.sem_inc(finished, 2)
            pipelined(act, rounds, Q, step, 3)
            act.wait_ge(copied, k.NB + 2)

        @block.gpsimd
        def _(pool):
            if "gpsimd" in stage:
                with pool.Fori(0, rounds) as j:
                    for u in both:
                        stage_one(pool, stage["gpsimd"], j, u)

        @block.vector
        def _(v):
            def step(blocks):
                past, now, _, later = blocks
                if later is not None and "vector" in stage:
                    stage_one(v, stage["vector"], *later)
                if now is not None and fin_engine == "vector":
                    finish_one(v, *now)
                if past is not None and stats:
                    n = Q * past[0] + past[1]
                    v.wait_ge(finished, n + 3)
                    row_stats(v, k, rows_of(k.X, n, 0, k.D), n).then_inc(taken, 1)
            if fin_engine == "vector":
                v.sem_inc(finished, 2)
            if biases:
                v.wait_ge(w_loaded, 16 * len(dmas))
                v.memset(ones2[:, :].bitcast(F32), 1.0).then_inc(bias_ready, 1)
                v.tensor_copy(b_high[:, :], b_in[:, :]).then_inc(bias_ready, 1)
                v.wait_ge(bias_ready, 2)
                row_parts(v, k, b_in, b_high, b_parts, bias_chain, bias_ready)
            pipelined(v, rounds, Q, step, 3)
            if fin_engine == "vector":
                v.wait_ge(finished, k.NB + 2)
            if stats:
                v.wait_ge(taken, k.NB)


def rows_of(buf, b, lo, hi):
    return buf[:, bass.ds(b, 1), lo:hi].rearrange("p b d -> p (b d)")



def after(j, q, Q, by=1):
    return j + (q + by) // Q, (q + by) % Q


def pipelined(eng, bodies, Q, step, depth):
    for lead in range(depth):
        step([None] * (depth - lead) + [after(0, i, Q, 0) for i in range(lead + 1)])
    whole = bodies - ceil_div(depth, Q)
    with eng.Fori(0, whole) as j:
        for q in range(Q):
            step([after(j, q, Q, by) for by in range(depth + 1)])
    for n in range(whole * Q, bodies * Q):
        step([after(0, n + by, Q, 0) if n + by < bodies * Q else None for by in range(depth + 1)])


def wait_used(eng, used, j, q, Q, back):
    if q - back >= 0:
        eng.wait_ge(used[q - back], j + 2)
    else:
        eng.wait_ge(used[q - back + Q], j + 1)


def index_feed(act, k, idx, index_ready, gathered, j, q, Q):
    if not_zero(j):
        act.wait_ge(gathered[q], 16 * QUAD * j)
    act.copy(idx[:, q * QUAD:(q + 1) * QUAD], k.srcS[:, bass.ds((j * Q + q) * QUAD, QUAD)]).then_inc(index_ready[q], 1)


def gather_quad(pool, k, table, G, idx, index_ready, rows_used, gathered, j, q, per=1):
    pool.wait_ge(index_ready[q], j + 1)
    pool.wait_ge(rows_used[q], per * (j + 1))
    hold(pool, k.held)
    for i in range(q * QUAD, (q + 1) * QUAD):
        pool.indirect_dma_start(out=G[:, i, :], out_offset=None, in_=table,
                                in_offset=bass.IndirectOffsetOnAxis(ap=idx[:, i:i + 1], axis=0)).then_inc(gathered[q], 16)


def pick_matrix(v, k, out, s):
    return v.tensor_tensor(out, k.iota[:, :].unsqueeze(1).to_broadcast([P, QUAD, P]),
                           k.drelS[:, bass.ds(s, QUAD)].unsqueeze(2).to_broadcast([P, QUAD, P]), ALU.is_equal)


def blocks_of(eng, k, s):
    _, values = k.nc.values_load_multi_w_load_instructions(
        k.blkT[0:1, bass.ds(s, QUAD)], engines=(eng.engine,), min_val=0, max_val=k.NB - 1,
        skip_runtime_bounds_check_because="step_tables clips the blocks to 0 .. NB - 1")
    return values


def load_attributes(sp, k, ea, ea_in, ea_loaded, j, q, Q):
    _, first_edges = k.nc.values_load_multi_w_load_instructions(
        k.baseT[0:1, bass.ds((j * Q + q) * QUAD, QUAD)], engines=(sp.engine,), min_val=0, max_val=k.E - P,
        skip_runtime_bounds_check_because="step_tables clips the tiles' first edges to 0 .. E - P")
    for r, at in enumerate(first_edges):
        sp.dma_start(ea_in[:, q * QUAD + r, :], ea[bass.ds(at, P), :]).then_inc(ea_loaded[q], 16)


def not_zero(n):
    return not isinstance(n, int) or n > 0


def sum_pass(nc, k, name, table, W, lo):
    Q = 4
    bodies = k.NSTEP // (Q * QUAD)
    with ExitStack() as ctx:
        sb, ps, sem = scope(nc, ctx)
        G = sb("G", [P, Q * QUAD, table.shape[1]])
        S = sb("S", [P, 2, QUAD, P])
        idx = sb("idx", [P, Q * QUAD], I32)
        psum = ps("p_sum", [P, 2, QUAD, 512])
        index_ready = [sem(f"{name}_index_ready{q}") for q in range(Q)]
        gathered = [sem(f"{name}_gathered{q}") for q in range(Q)]
        summed = [sem(f"{name}_summed{q}") for q in range(Q)]
        picks_ready, added = sem(f"{name}_picks_ready"), sem(f"{name}_added")
        block = ctx.enter_context(nc.Block())

        @block.scalar
        def _(act):
            for q in range(Q):
                index_feed(act, k, idx, index_ready, gathered, 0, q, Q)
            with act.Fori(0, bodies) as j:
                for q in range(Q):
                    index_feed(act, k, idx, index_ready, gathered, j + 1, q, Q)

        @block.gpsimd
        def _(pool):
            with pool.Fori(0, bodies) as j:
                for q in range(Q):
                    gather_quad(pool, k, table, G, idx, index_ready, summed, gathered, j, q)

        @block.tensor
        def _(pe):
            for s in summed:
                pe.sem_inc(s, 1)
            with pe.Fori(0, bodies) as j:
                for q in range(Q):
                    n = Q * j + q
                    pe.wait_ge(picks_ready, n + 1)
                    pe.wait_ge(gathered[q], 16 * QUAD * (j + 1))
                    pe.wait_ge(added, (n + 1) * QUAD)
                    for r in range(QUAD):
                        last = pe.matmul(psum[:, q % 2, r, 0:W], S[:, q % 2, r, :], G[:, q * QUAD + r, 0:W], start=True, stop=True)
                    last.then_inc(summed[q], 1)

        @block.vector
        def _(v):
            v.memset(k.AGG[:, :, lo:lo + W], 0.0).then_inc(added, 2 * QUAD)

            def step(quads):
                now, then = quads
                if then is not None:
                    j, q = then
                    wait_used(v, summed, j, q, Q, 2)
                    pick_matrix(v, k, S[:, q % 2, :, :], (Q * j + q) * QUAD).then_inc(picks_ready, 1)
                if now is not None:
                    j, q = now
                    n = Q * j + q
                    b = blocks_of(v, k, n * QUAD)
                    v.wait_ge(summed[q], j + 2)
                    for r in range(QUAD):
                        v.wait_ge(added, (n + 2) * QUAD + r)
                        v.tensor_tensor(rows_of(k.AGG, b[r], lo, lo + W), rows_of(k.AGG, b[r], lo, lo + W),
                                        psum[:, q % 2, r, 0:W], ALU.add).then_inc(added, 1)
            pipelined(v, bodies, Q, step, 1)
            v.wait_ge(added, 2 * QUAD + k.NSTEP)


def edge_mlp_pass(nc, k, name, table, ea, W1, Wg, W2, b2):
    D, A = k.D, ea.shape[1]
    assert 2 * A == P
    Q = 2
    bodies = k.NSTEP // (Q * QUAD)
    with ExitStack() as ctx:
        sb, ps, sem = scope(nc, ctx)
        G = sb("G", [P, 2 * QUAD, 2 * D])
        S = sb("S", [P, QUAD, P], F32R)
        idx = sb("idx", [P, 2 * QUAD], I32)
        ea_in = sb("ea_in", [P, 2 * QUAD, A])
        parts = sb("parts", [P, QUAD, 2, A], F32R)
        partsT = sb("partsT", [P, QUAD * P], F32R)
        pre = sb("pre", [P, QUAD, 2 * D])
        gate = sb("gate", [P, 2, QUAD, D])
        coreT = sb("coreT", [P, 2, QUAD * P])
        msg = sb("msg", [P, QUAD, D])
        msg_high, msg_low = sb("msg_high", [P, QUAD, D], F32R), sb("msg_low", [P, QUAD, D], F32R)
        w_in = sb("w_in", [P, 2 * D])
        w_high, w_low = sb("w_high", [P, 2 * D], F32R), sb("w_low", [P, 2 * D], F32R)
        w2, ones2 = sb("w2", [P, 2, D]), sb("ones2", [2, P], F32R)
        b2_in, b2_high = sb("b2_in", [2, D]), sb("b2_high", [2, D], F32R)
        b2_parts = sb("b2_parts", [2, D], F32R)
        p_partsT = ps("p_partsT", [P, QUAD * P])
        p_pre = ps("p_pre", [P, 2, 2 * D])
        p_coreT = ps("p_coreT", [P, 2, QUAD * P])
        p_core = ps("p_core", [P, QUAD, D])
        p_sum = ps("p_sum", [P, 2, D])
        index_ready = [sem(f"{name}_index_ready{h}") for h in range(Q)]
        gathered = [sem(f"{name}_gathered{h}") for h in range(Q)]
        ea_loaded = [sem(f"{name}_ea_loaded{h}") for h in range(Q)]
        high_ready, picks_ready, parts_ready, parts_turned, partsT_ready, gate_out, core_turned, coreT_ready = (
            sem(f"{name}_{n}") for n in ("high_ready", "picks_ready", "parts_ready", "parts_turned", "partsT_ready", "gate_out",
                                         "core_turned", "coreT_ready"))
        pre_added = [sem(f"{name}_pre_added{h}") for h in range(Q)]
        pre_summed, core_out, summed, added, msg_ready = (sem(f"{name}_{n}") for n in ("pre_summed", "core_out", "summed", "added", "msg_ready"))
        msg_high_ready, msg_low_ready = sem(f"{name}_msg_high_ready"), sem(f"{name}_msg_low_ready")
        w_loaded, w_split, b2_chain = (sem(f"{name}_{n}") for n in ("w_loaded", "w_split", "b2_chain"))
        block = ctx.enter_context(nc.Block())

        @block.sync
        def _(sp):
            for half in range(2):
                for i, w in enumerate((W1, Wg)):
                    sp.dma_start(w_in[half * A:(half + 1) * A, i * D:(i + 1) * D], w[D:D + A, :]).then_inc(w_loaded, 16)
            sp.dma_start(w2[:, :, :], W2.rearrange("(c p) n -> p c n", p=P)).then_inc(w_loaded, 16)
            sp.dma_start(b2_in[:, :], b2.partition_broadcast(2)).then_inc(w_loaded, 16)
            with sp.Fori(0, bodies) as j:
                for h in range(Q):
                    sp.wait_ge(parts_ready, Q * j + h + 1)
                    load_attributes(sp, k, ea, ea_in, ea_loaded, j, h, Q)
            for h in range(Q):
                sp.wait_ge(ea_loaded[h], 16 * QUAD * bodies)

        @block.gpsimd
        def _(pool):
            with pool.Fori(0, bodies) as j:
                for h in range(Q):
                    gather_quad(pool, k, table, G, idx, index_ready, pre_added, gathered, j, h, QUAD)

        @block.tensor
        def _(pe):
            def turn_parts(j, h):
                n = Q * j + h
                pe.wait_ge(parts_ready, n + 3)
                pe.wait_ge(partsT_ready, n + 1)
                for r in range(QUAD):
                    last = pe.transpose(p_partsT[:, r * P:(r + 1) * P], parts[:, r, :, :].rearrange("p a b -> p (a b)").bitcast(F32), k.ident[:, :])
                last.then_inc(parts_turned, 1)

            def core_gate(j, h, r):
                if r == 0:
                    pe.wait_ge(partsT_ready, Q * j + h + 2)
                if r >= 2:
                    pe.wait_ge(pre_added[h], QUAD * (j + 1) + r - 1)
                elif h == 1:
                    pe.wait_ge(pre_added[0], QUAD * (j + 1) + r + 3)
                else:
                    pe.wait_ge(pre_added[1], QUAD * j + r + 3)
                pe.matmul(p_pre[:, r % 2, :], partsT[:, r * P:(r + 1) * P], w_high[:, :], start=True, stop=False)
                pe.matmul(p_pre[:, r % 2, :], partsT[:, r * P:(r + 1) * P], w_low[:, :], start=False, stop=True).then_inc(pre_summed, 1)

            def turn_core(j, h):
                n = Q * j + h
                pe.wait_ge(pre_added[h], QUAD * (j + 2))
                pe.wait_ge(coreT_ready, n + 1)
                for f in range(2):
                    for r in range(QUAD):
                        last = pe.transpose(p_coreT[:, f, r * P:(r + 1) * P], pre[:, r, f * P:(f + 1) * P], k.ident[:, :])
                last.then_inc(core_turned, 1)

            def core_product(j, h, pair):
                n = Q * j + h
                pe.wait_ge(coreT_ready, n + 2)
                pe.wait_ge(msg_ready, 2 * n + 3 + pair)
                for r in (2 * pair, 2 * pair + 1):
                    for f in range(2):
                        pe.matmul(p_core[:, r, :], coreT[:, f, r * P:(r + 1) * P], w2[:, f, :], start=(f == 0), stop=False)
                    pe.matmul(p_core[:, r, :], ones2[:, :], b2_parts[:, :], start=False, stop=True).then_inc(core_out, 1)

            def sums(j, h, pair):
                n = Q * j + h
                if pair == 0:
                    pe.wait_ge(picks_ready, n + 1)
                pe.wait_ge(msg_low_ready, 2 * n + 1 + pair)
                pe.wait_ge(added, n * QUAD + 2 * pair + 2)
                for r in (2 * pair, 2 * pair + 1):
                    pe.matmul(p_sum[:, r % 2, :], S[:, r, :], msg_high[:, r, :], start=True, stop=False)
                    last = pe.matmul(p_sum[:, r % 2, :], S[:, r, :], msg_low[:, r, :], start=False, stop=True)
                last.then_inc(summed, 2)

            def step(quads):
                past, now, then, later = quads
                for pair in range(2):
                    if past is not None:
                        sums(*past, pair)
                    if then is not None:
                        core_gate(*then, 2 * pair)
                        core_gate(*then, 2 * pair + 1)
                    if pair == 0 and later is not None:
                        turn_parts(*later)
                    if now is not None:
                        core_product(*now, pair)
                if then is not None:
                    turn_core(*then)
            for x in (parts_turned, core_turned):
                pe.sem_inc(x, 1)
            for x in (pre_summed, core_out, summed):
                pe.sem_inc(x, QUAD)
            pe.wait_ge(w_split, 5)
            pipelined(pe, bodies, Q, step, 3)

        @block.scalar
        def _(act):
            def split_high(j, h):
                act.wait_ge(ea_loaded[h], 16 * QUAD * (j + 1))
                act.wait_ge(parts_turned, Q * j + h + 1)
                act.copy(parts[:, :, 0, :], ea_in[:, h * QUAD:(h + 1) * QUAD, :]).then_inc(high_ready, 1)

            def copy_parts(j, h):
                n = Q * j + h
                act.wait_ge(parts_turned, n + 2)
                act.wait_ge(pre_summed, QUAD * (n + 1))
                act.copy(partsT[:, :], p_partsT[:, :]).then_inc(partsT_ready, 1)

            def gates(j, h):
                act.wait_ge(pre_added[h], QUAD * (j + 2))
                act.wait_ge(msg_ready, 2 * (Q * j + h) + 2)
                act.activation(gate[:, h, :, :], pre[:, :, D:2 * D], ACT.Sigmoid).then_inc(gate_out, 1)

            def message_high(j, h, pair):
                n = Q * j + h
                r = 2 * pair
                act.wait_ge(msg_ready, 2 * n + 5 + pair)
                act.wait_ge(summed, QUAD * n + r + 2)
                act.copy(msg_high[:, r:r + 2, :], msg[:, r:r + 2, :]).then_inc(msg_high_ready, 1)

            def relu_core(j, h):
                n = Q * j + h
                act.wait_ge(core_turned, n + 2)
                act.wait_ge(core_out, QUAD * (n + 1))
                act.activation(coreT[:, 0, :], p_coreT[:, 0, :], ACT.Relu)
                act.activation(coreT[:, 1, :], p_coreT[:, 1, :], ACT.Relu).then_inc(coreT_ready, 1)

            def step(quads):
                past, now, _, later, last = quads
                if now is not None:
                    gates(*now)
                    index_feed(act, k, idx, index_ready, gathered, now[0] + 1, now[1], Q)
                    relu_core(*now)
                if past is not None:
                    message_high(*past, 1)
                if later is not None:
                    copy_parts(*later)
                if last is not None:
                    split_high(*last)
                if now is not None:
                    message_high(*now, 0)
            for x in (partsT_ready, gate_out, coreT_ready):
                act.sem_inc(x, 1)
            for h in range(Q):
                index_feed(act, k, idx, index_ready, gathered, 0, h, Q)
            pipelined(act, bodies, Q, step, 4)

        @block.vector
        def _(v):
            def split_low(j, h):
                v.wait_ge(high_ready, Q * j + h + 1)
                v.wait_ge(ea_loaded[h], 16 * QUAD * (j + 1))
                v.tensor_tensor(parts[:, :, 1, :], ea_in[:, h * QUAD:(h + 1) * QUAD, :], parts[:, :, 0, :].bitcast(F32), ALU.subtract).then_inc(parts_ready, 1)

            def add_rows(j, h, r):
                n = Q * j + h
                if r == 0:
                    v.wait_ge(gathered[h], 16 * QUAD * (j + 1))
                    v.wait_ge(core_turned, n + 1)
                    v.wait_ge(gate_out, n + 1)
                v.wait_ge(pre_summed, QUAD * (n + 1) + r + 1)
                v.tensor_tensor(pre[:, r, :], p_pre[:, r % 2, :], G[:, h * QUAD + r, :], ALU.add).then_inc(pre_added[h], 1)

            def accumulate(j, h, r, b):
                s = (Q * j + h) * QUAD + r
                if r % 2 == 0:
                    v.wait_ge(summed, s + QUAD + 2)
                v.wait_ge(added, s + 2)
                v.tensor_tensor(rows_of(k.H, b, 0, D), rows_of(k.H, b, 0, D), p_sum[:, r % 2, :], ALU.add).then_inc(added, 1)

            def picks(j, h):
                n = Q * j + h
                v.wait_ge(summed, QUAD * (n + 1))
                pick_matrix(v, k, S[:, :, :], n * QUAD).then_inc(picks_ready, 1)

            def messages(j, h, pair):
                n = Q * j + h
                r = 2 * pair
                v.wait_ge(gate_out, n + 2)
                v.wait_ge(core_out, QUAD * (n + 1) + r + 2)
                v.tensor_tensor(msg[:, r:r + 2, :], p_core[:, r:r + 2, :], gate[:, h, r:r + 2, :], ALU.mult).then_inc(msg_ready, 1)

            def message_low(j, h, pair):
                n = Q * j + h
                r = 2 * pair
                v.wait_ge(msg_high_ready, 2 * n + pair + 1)
                v.tensor_tensor(msg_low[:, r:r + 2, :], msg[:, r:r + 2, :], msg_high[:, r:r + 2, :].bitcast(F32),
                                ALU.subtract).then_inc(msg_low_ready, 1)

            def step(quads):
                past, now, then, _, last = quads
                if past is not None:
                    b = blocks_of(v, k, (Q * past[0] + past[1]) * QUAD)
                for pair in range(2):
                    for r in (2 * pair, 2 * pair + 1):
                        if past is not None:
                            accumulate(*past, r, b[r])
                        if then is not None:
                            add_rows(*then, r)
                    if pair == 0 and past is not None:
                        message_low(*past, 1)
                    if pair == 1 and now is not None:
                        picks(*now)
                        message_low(*now, 0)
                    if pair == 1 and last is not None:
                        split_low(*last)
                    if now is not None:
                        messages(*now, pair)

            for x in pre_added:
                v.sem_inc(x, QUAD)
            v.sem_inc(msg_ready, 4)
            v.sem_inc(added, 2)
            v.sem_inc(parts_ready, 2)
            v.wait_ge(w_loaded, 96)
            v.memset(ones2[:, :].bitcast(F32), 1.0).then_inc(w_split, 1)
            v.tensor_copy(w_high[:, :], w_in[:, :]).then_inc(w_split, 1)
            v.tensor_copy(b2_high[:, :], b2_in[:, :]).then_inc(w_split, 1)
            v.wait_ge(w_split, 3)
            v.tensor_tensor(w_low[:, :], w_in[:, :], w_high[:, :].bitcast(F32), ALU.subtract).then_inc(w_split, 1)
            row_parts(v, k, b2_in, b2_high, b2_parts, b2_chain, w_split)
            pipelined(v, bodies, Q, step, 4)
            v.wait_ge(added, 2 + k.NSTEP)


def row_parts(v, k, row, high, parts, links, done):
    v.tensor_tensor(row[:, :], row[:, :], high[:, :].bitcast(F32), ALU.subtract).then_inc(links, 1)
    v.wait_ge(links, 1)
    v.tensor_scalar(row[:, :], row[:, :], k.ident[0:2, 1:2], None, ALU.mult).then_inc(links, 1)
    v.wait_ge(links, 2)
    v.scalar_tensor_tensor(parts[:, :], high[:, :].bitcast(F32), k.ident[0:2, 0:1], row[:, :],
                           ALU.mult, ALU.add).then_inc(done, 1)


def attention_pass(nc, k, name, table, ea, v_row):
    D, A = k.D, ea.shape[1]
    W, Q = D + 1, 4
    bodies = k.NSTEP // (Q * QUAD)
    with ExitStack() as ctx:
        sb, ps, sem = scope(nc, ctx)
        G = sb("G", [P, Q * QUAD, D + 2])
        idx = sb("idx", [P, Q * QUAD], I32)
        ea_in = sb("ea_in", [P, Q * QUAD, A])
        masked = sb("masked", [P, 2, QUAD, P])
        weightT = sb("weightT", [P, 2, QUAD, P])
        weight = sb("weight", [P, 2, QUAD, P])
        minus_top = sb("minus_top", [P, k.NB])
        dot, logit = sb("dot", [P, 2, QUAD]), sb("logit", [P, 2, QUAD])
        step_top = sb("step_top", [P, 2, QUAD])
        minus, rise, scale = sb("minus", [P, 2, QUAD]), sb("rise", [P, 2, QUAD]), sb("scale", [P, 2, QUAD])
        p_turn = ps("p_turn", [P, 2, QUAD, P])
        p_back = ps("p_back", [P, 2, QUAD, P])
        p_sum = ps("p_sum", [P, QUAD, 512])
        index_ready = [sem(f"{name}_index_ready{q}") for q in range(Q)]
        gathered = [sem(f"{name}_gathered{q}") for q in range(Q)]
        ea_loaded = [sem(f"{name}_ea_loaded{q}") for q in range(Q)]
        logits_ready = [sem(f"{name}_logits_ready{q}") for q in range(Q)]
        summed = [sem(f"{name}_summed{q}") for q in range(Q)]
        masked_ready, turned, turned_back, weight_ready = (sem(f"{name}_{n}") for n in ("masked_ready", "turned", "turned_back", "weight_ready"))
        exp_ready, added = sem(f"{name}_exp_ready"), sem(f"{name}_added")
        tops_ready, scale_ready, top_set, dots_ready, step_top_ready, drel_scaled, distances_ready = (sem(f"{name}_{n}") for n in (
            "tops_ready", "scale_ready", "top_set", "dots_ready", "step_top_ready", "drel_scaled", "distances_ready"))
        block = ctx.enter_context(nc.Block())

        @block.sync
        def _(sp):
            with sp.Fori(0, bodies) as j:
                for q in range(Q):
                    sp.wait_ge(logits_ready[q], j + 1)
                    load_attributes(sp, k, ea, ea_in, ea_loaded, j, q, Q)
            for q in range(Q):
                sp.wait_ge(ea_loaded[q], 16 * QUAD * bodies)

        @block.gpsimd
        def _(pool):
            with pool.Fori(0, bodies) as j:
                for q in range(Q):
                    gather_quad(pool, k, table, G, idx, index_ready, summed, gathered, j, q, QUAD)

        @block.tensor
        def _(pe):
            def turn(j, q):
                n = Q * j + q
                pe.wait_ge(masked_ready, n + 3)
                pe.wait_ge(exp_ready, (n + 1) * QUAD)
                for r in range(QUAD):
                    last = pe.transpose(p_turn[:, q % 2, r, :], masked[:, q % 2, r, :], k.ident[:, :])
                last.then_inc(turned, 1)

            def turn_back(j, q):
                n = Q * j + q
                pe.wait_ge(weight_ready, n + 1)
                for r in range(QUAD):
                    pe.wait_ge(exp_ready, (n + 2) * QUAD + r + 1)
                    last = pe.transpose(p_back[:, q % 2, r, :], weightT[:, q % 2, r, :], k.ident[:, :])
                last.then_inc(turned_back, 1)

            def sums(j, q):
                n = Q * j + q
                pe.wait_ge(weight_ready, n + 3)
                for r in range(QUAD):
                    pe.wait_ge(added, (n + 1) * QUAD + r + 1)
                    pe.matmul(p_sum[:, r, 0:W], weight[:, q % 2, r, :], G[:, q * QUAD + r, 0:W], start=True, stop=True).then_inc(summed[q], 1)

            def step(quads):
                now, then, later = quads
                if now is not None:
                    sums(*now)
                if later is not None:
                    turn(*later)
                if then is not None:
                    turn_back(*then)
            for s in summed:
                pe.sem_inc(s, QUAD)
            pe.sem_inc(turned, 2)
            pe.sem_inc(turned_back, 2)
            pipelined(pe, bodies, Q, step, 2)

        @block.scalar
        def _(act):
            def copy_weights(j, q):
                n = Q * j + q
                act.wait_ge(turned_back, n + 3)
                if q >= 2:
                    act.wait_ge(summed[q - 2], QUAD * (j + 2))
                else:
                    act.wait_ge(summed[q + 2], QUAD * (j + 1))
                act.copy(weight[:, q % 2, :, :], p_back[:, q % 2, :, :]).then_inc(weight_ready, 1)

            def distances(j, q):
                n = Q * j + q
                act.wait_ge(turned, n + 1)
                for r in range(QUAD):
                    last = act.activation(masked[:, q % 2, r, :], k.iota[:, :], ACT.Square,
                                          bias=k.drelS[:, bass.ds(n * QUAD + r, 1)], scale=FARTHER)
                last.then_inc(distances_ready, 1)

            def mask(j, q):
                n = Q * j + q
                act.wait_ge(distances_ready, n + 1)
                act.wait_ge(logits_ready[q], j + 2)
                for r in range(QUAD):
                    last = act.activation(masked[:, q % 2, r, :], masked[:, q % 2, r, :], ACT.Identity,
                                          bias=logit[:, q % 2, r:r + 1], scale=-1.0)
                last.then_inc(masked_ready, 1)

            def exps(j, q):
                n = Q * j + q
                act.wait_ge(tops_ready, n + 1)
                act.wait_ge(added, (n + 1) * QUAD)
                act.activation(scale[:, q % 2, :], rise[:, q % 2, :], ACT.Exp, scale=-1.0).then_inc(scale_ready, 1)
                act.wait_ge(turned_back, n + 1)
                for r in range(QUAD):
                    act.activation(weightT[:, q % 2, r, :], p_turn[:, q % 2, r, :], ACT.Exp,
                                   bias=minus[:, q % 2, r:r + 1]).then_inc(exp_ready, 1)

            def step(quads):
                now, then, later = quads
                if now is not None:
                    copy_weights(*now)
                    index_feed(act, k, idx, index_ready, gathered, now[0] + 1, now[1], Q)
                if later is not None:
                    distances(*later)
                    mask(*later)
                if then is not None:
                    exps(*then)
            act.sem_inc(masked_ready, 2)
            act.sem_inc(weight_ready, 2)
            act.sem_inc(exp_ready, 2 * QUAD)
            act.wait_ge(drel_scaled, 1)
            for q in range(Q):
                index_feed(act, k, idx, index_ready, gathered, 0, q, Q)
            pipelined(act, bodies, Q, step, 2)

        @block.vector
        def _(v):
            for x in logits_ready:
                v.sem_inc(x, 1)
            v.tensor_scalar(k.drelS[:, :], k.drelS[:, :], -FARTHER, None, ALU.mult).then_inc(drel_scaled, 1)
            v.memset(minus_top[:, :], -FLOOR).then_inc(top_set, 1)
            v.memset(k.AGG[:, :, 0:W], 0.0).then_inc(added, 2 * QUAD)
            def dots(j, q):
                n = Q * j + q
                v.wait_ge(gathered[q], 16 * QUAD * (j + 1))
                v.wait_ge(ea_loaded[q], 16 * QUAD * (j + 1))
                v.wait_ge(masked_ready, n + 1)
                for r in range(QUAD):
                    i = q * QUAD + r
                    ins = v.tensor_tensor_reduce(ea_in[:, i, :], ea_in[:, i, :], v_row, 1.0, G[:, i, D + 1:D + 2],
                                                 ALU.mult, ALU.add, dot[:, q % 2, r:r + 1])
                ins.then_inc(dots_ready, 1)

            def logits(j, q):
                v.wait_ge(dots_ready, Q * j + q + 1)
                v.scalar_tensor_tensor(logit[:, q % 2, :], dot[:, q % 2, :], 0.01, dot[:, q % 2, :], ALU.mult, ALU.max).then_inc(logits_ready[q], 1)

            def step_maxima(j, q):
                n = Q * j + q
                v.wait_ge(turned, n + 3)
                v.tensor_reduce(step_top[:, q % 2, :], p_turn[:, q % 2, :, :], AX_X, ALU.max).then_inc(step_top_ready, 1)

            def raise_top(j, q, r, b):
                n = Q * j + q
                if r == 0:
                    v.wait_ge(step_top_ready, n + 1)
                    v.wait_ge(exp_ready, (n + 1) * QUAD)
                top = minus_top[:, bass.ds(b, 1)]
                v.wait_ge(top_set, n * QUAD + r + 1)
                v.tensor_scalar(rise[:, q % 2, r:r + 1], step_top[:, q % 2, r:r + 1], top, 0.0, ALU.add, ALU.max)
                minus_ready = v.tensor_scalar(minus[:, q % 2, r:r + 1], step_top[:, q % 2, r:r + 1], -1.0, top, ALU.mult, ALU.min)
                if r == QUAD - 1:
                    minus_ready.then_inc(tops_ready, 1)
                v.tensor_scalar(top, step_top[:, q % 2, r:r + 1], -1.0, top, ALU.mult, ALU.min).then_inc(top_set, 1)

            def add(j, q, r, b):
                n = Q * j + q
                if r == 0:
                    v.wait_ge(scale_ready, n + 1)
                v.wait_ge(summed[q], QUAD * (j + 1) + r + 1)
                v.wait_ge(added, (n + 2) * QUAD + r)
                v.scalar_tensor_tensor(rows_of(k.AGG, b, 0, W), rows_of(k.AGG, b, 0, W), scale[:, q % 2, r:r + 1],
                                       p_sum[:, r, 0:W], ALU.mult, ALU.add).then_inc(added, 1)

            def step(quads):
                now, then, later = quads
                if then is not None:
                    step_maxima(*then)
                if later is not None:
                    dots(*later)
                if then is not None:
                    b_then = blocks_of(v, k, (Q * then[0] + then[1]) * QUAD)
                if now is not None:
                    b_now = blocks_of(v, k, (Q * now[0] + now[1]) * QUAD)
                if later is not None:
                    logits(*later)
                for r in range(QUAD):
                    if then is not None:
                        raise_top(*then, r, b_then[r])
                    if now is not None:
                        add(*now, r, b_now[r])
            pipelined(v, bodies, Q, step, 2)
            v.wait_ge(added, 2 * QUAD + k.NSTEP)



def wide(a, n):
    return a.unsqueeze(2).to_broadcast([P, a.shape[1], n])


def every_block(a, nb):
    return a.unsqueeze(1).to_broadcast([P, nb, a.shape[1]])


def degrees(nc, k):
    with ExitStack() as ctx:
        sb, ps, sem = scope(nc, ctx)
        deg, plus = sb("deg", [P, k.NB]), sb("plus", [P, k.NB])
        link_s, plus_ready, root_ready = sem("deg_dve_chain"), sem("deg_plus_ready"), sem("deg_root_ready")
        with nc.Block() as block:
            @block.vector
            def _(v):
                link = chain(v, link_s)
                link(v.tensor_scalar(deg[:, :], k.AGG[:, :, k.D], 1.0, None, ALU.max))
                v.tensor_scalar(plus[:, :], k.AGG[:, :, k.D], 1.0, None, ALU.add).then_inc(plus_ready, 1)
                v.reciprocal(k.rdeg[:, :], deg[:, :])
                v.wait_ge(root_ready, 1)
                link(v.reciprocal(k.dinv[:, :], plus[:, :]))

            @block.scalar
            def _(act):
                act.wait_ge(plus_ready, 1)
                act.activation(plus[:, :], plus[:, :], ACT.Sqrt).then_inc(root_ready, 1)


def gated_output(nc, k, gamma, beta):
    D = k.D
    with ExitStack() as ctx:
        sb, ps, sem = scope(nc, ctx)
        gam, bet = sb("gam", [P, D]), sb("bet", [P, D])
        layer_norm_constants(nc, k, "gout", k.rstd, k.shift, k.H)
        loaded, normed, beta_added, scaled, added, taken = (sem(f"gout_{n}") for n in ("loaded", "normed", "beta_added", "scaled", "added", "taken"))
        Q = 2
        with nc.Block() as block:
            @block.sync
            def _(sp):
                sp.dma_start(gam[:, :], gamma.partition_broadcast(P)).then_inc(loaded, 16)
                sp.dma_start(bet[:, :], beta.partition_broadcast(P)).then_inc(loaded, 16)

            @block.scalar
            def _(act):
                with act.Fori(0, k.NB // Q) as j:
                    for u in range(Q):
                        b = Q * j + u
                        act.activation(rows_of(k.H, b, 0, D), rows_of(k.H, b, 0, D), ACT.Identity,
                                       bias=k.shift[:, bass.ds(b, 1)], scale=k.rstd[:, bass.ds(b, 1)]).then_inc(normed, 1)

            @block.gpsimd
            def _(pool):
                pool.wait_ge(loaded, 32)
                with pool.Fori(0, k.NB // Q) as j:
                    for u in range(Q):
                        x = rows_of(k.X, Q * j + u, 0, D)
                        pool.tensor_tensor(x, x, bet[:, :], ALU.add).then_inc(beta_added, 1)

            @block.vector
            def _(v):
                def step(blocks):
                    past, now, then = blocks
                    if then is not None:
                        n = Q * then[0] + then[1]
                        v.wait_ge(normed, n + 1)
                        v.tensor_tensor(rows_of(k.H, n, 0, D), rows_of(k.H, n, 0, D), gam[:, :], ALU.mult).then_inc(scaled, 1)
                    if now is not None:
                        n = Q * now[0] + now[1]
                        v.wait_ge(beta_added, n + 1)
                        v.wait_ge(scaled, n + 1)
                        v.tensor_tensor(rows_of(k.X, n, 0, D), rows_of(k.X, n, 0, D), rows_of(k.H, n, 0, D), ALU.add).then_inc(added, 1)
                    if past is not None:
                        n = Q * past[0] + past[1]
                        v.wait_ge(added, n + 1)
                        row_stats(v, k, rows_of(k.X, n, 0, D), n).then_inc(taken, 1)
                v.wait_ge(loaded, 32)
                pipelined(v, k.NB // Q, Q, step, 2)
                v.wait_ge(taken, k.NB)


def graph_norm(nc, k, name, lo, W, own, b, gain, beta):
    nbu, rest = k.NBU, k.N - (k.NBU - 1) * P
    groups = [(g, g + GROUP) for g in range(0, k.NB, GROUP)]
    with ExitStack() as ctx:
        sb, ps, sem = scope(nc, ctx)
        b_row, g_row, be_row = sb("b_row", [P, W]), sb("g_row", [P, W]), sb("be_row", [P, W])
        mean, var, rstd = sb("mean_row", [P, W]), sb("var_row", [P, W]), sb("rstd_row", [P, W])
        p_mean, p_var = ps("p_mean", [P, 512]), ps("p_var", [P, 512])
        loaded, z_ready, centered, sq_ready, col_sums, link_s, var_ready, std_ready, scaled, rectified = (sem(f"{name}_{n}") for n in (
            "loaded", "z_ready", "centered", "squares_ready", "column_sums", "dve_chain", "var_ready", "std_ready", "scaled", "rectified"))
        block = ctx.enter_context(nc.Block())

        def Z(g):
            return k.AGG[:, g[0]:g[1], lo:lo + W]

        def T(g):
            return k.AGG[:, g[0]:g[1], own:own + W]

        @block.sync
        def _(sp):
            for to, of in ((b_row, b), (g_row, gain), (be_row, beta)):
                sp.dma_start(to[:, :], of.partition_broadcast(P)).then_inc(loaded, 16)

        @block.tensor
        def _(pe):
            for psum, at, ready in ((p_mean, lo, z_ready), (p_var, own, sq_ready)):
                pe.wait_ge(ready, 1)
                for m in range(GROUP):
                    pe.matmul(psum[:, 0:W], k.ones[:, :], k.AGG[:, m, at:at + W], start=(m == 0), stop=False)
                with pe.Fori(1, len(groups) - 1) as g:
                    pe.wait_ge(ready, g + 1)
                    for m in range(GROUP):
                        pe.matmul(psum[:, 0:W], k.ones[:, :], rows_of(k.AGG, GROUP * g + m, at, at + W), start=False, stop=False)
                pe.wait_ge(ready, len(groups))
                for m in range(groups[-1][0], nbu):
                    last = pe.matmul(psum[:, 0:W], (k.valid if m == nbu - 1 else k.ones)[:, :], k.AGG[:, m, at:at + W],
                                     start=False, stop=(m == nbu - 1))
                last.then_inc(col_sums, 1)

        @block.scalar
        def _(act):
            for i, g in enumerate(groups):
                act.wait_ge(centered, i + 1)
                act.activation(T(g), Z(g), ACT.Square).then_inc(sq_ready, 1)
            act.wait_ge(var_ready, 1)
            act.activation(var[:, :], var[:, :], ACT.Sqrt).then_inc(std_ready, 1)
            for i, g in enumerate(groups):
                act.wait_ge(scaled, i + 1)
                act.activation(Z(g), Z(g), ACT.Relu).then_inc(rectified, 1)
            act.wait_ge(rectified, len(groups))

        @block.vector
        def _(v):
            link = chain(v, link_s)
            v.wait_ge(loaded, 48)
            for g in groups:
                blocks = g[1] - g[0]
                link(v.tensor_tensor(Z(g), Z(g), T(g), ALU.add))
                link(v.tensor_tensor(Z(g), Z(g), wide(k.dinv[:, g[0]:g[1]], W), ALU.mult))
                v.tensor_tensor(Z(g), Z(g), every_block(b_row[:, :], blocks), ALU.add).then_inc(z_ready, 1)
            v.wait_ge(col_sums, 1)
            link(v.tensor_scalar(mean[:, :], p_mean[:, 0:W], 1.0 / k.N, None, ALU.mult))
            for g in groups:
                v.tensor_tensor(Z(g), Z(g), every_block(mean[:, :], g[1] - g[0]), ALU.subtract).then_inc(centered, 1)
            v.wait_ge(col_sums, 2)
            v.tensor_scalar(var[:, :], p_var[:, 0:W], 1.0 / k.N, EPS, ALU.mult, ALU.add).then_inc(var_ready, 1)
            v.wait_ge(std_ready, 1)
            link(v.reciprocal(rstd[:, :], var[:, :]))
            link(v.tensor_tensor(rstd[:, :], rstd[:, :], g_row[:, :], ALU.mult))
            for g in groups:
                blocks = g[1] - g[0]
                link(v.tensor_tensor(Z(g), Z(g), every_block(rstd[:, :], blocks), ALU.mult))
                v.tensor_tensor(Z(g), Z(g), every_block(be_row[:, :], blocks), ALU.add).then_inc(scaled, 1)


def attention_constants(nc, k, attn, We, be, v_row, attn_row, const):
    D, A = We.shape
    with ExitStack() as ctx:
        sb, ps, sem = scope(nc, ctx)
        a_col, be_col = sb("a_col", [P, D // P]), sb("be_col", [P, D // P])
        we = sb("we", [P, D // P, A])
        p_v = ps("p_v", [P, 512])
        loaded, made, copied = sem("att_loaded"), sem("att_made"), sem("att_copied")
        block = ctx.enter_context(nc.Block())
        flat = attn.rearrange("a h c -> (a h c)")

        @block.sync
        def _(sp):
            for c in range(D // P):
                sp.dma_start(a_col[:, c:c + 1], flat[c * P:(c + 1) * P].unsqueeze(1)).then_inc(loaded, 16)
                sp.dma_start(be_col[:, c:c + 1], be[c * P:(c + 1) * P].unsqueeze(1)).then_inc(loaded, 16)
            sp.dma_start(we[:, :, :], We.rearrange("(c p) n -> p c n", p=P)).then_inc(loaded, 16)
            sp.dma_start(attn_row[:, :], flat.partition_broadcast(P)).then_inc(loaded, 16)

        @block.tensor
        def _(pe):
            pe.wait_ge(loaded, 16 * (2 * (D // P) + 2))
            for c in range(D // P):
                pe.matmul(p_v[:, 0:A], a_col[:, c:c + 1].to_broadcast([P, P]), we[:, c, :], start=(c == 0), stop=(c == D // P - 1))
            for c in range(D // P):
                last = pe.matmul(p_v[:, A:A + 1], a_col[:, c:c + 1].to_broadcast([P, P]), be_col[:, c:c + 1],
                                 start=(c == 0), stop=(c == D // P - 1))
            last.then_inc(made, 1)

        @block.vector
        def _(v):
            v.wait_ge(made, 1)
            v.tensor_copy(v_row[:, :], p_v[:, 0:A]).then_inc(copied, 1)
            v.tensor_copy(const[:, :], p_v[:, A:A + 1]).then_inc(copied, 1)
            v.wait_ge(copied, 2)


def attention_output(nc, k, out):
    D = k.D
    full, rest = k.N // P, k.N - k.N // P * P
    groups = [(g, g + GROUP) for g in range(0, k.NB, GROUP)]
    with ExitStack() as ctx:
        sb, ps, sem = scope(nc, ctx)
        rden = sb("rden", [P, k.NB])
        link_s, done, stored = sem("out_dve_chain"), sem("out_done"), sem("out_stored")
        block = ctx.enter_context(nc.Block())

        @block.vector
        def _(v):
            link = chain(v, link_s)
            link(v.tensor_scalar(rden[:, :], k.AGG[:, :, D], 1e-16, None, ALU.add))
            link(v.reciprocal(rden[:, :], rden[:, :]))
            for first, end in groups:
                sums, x = k.AGG[:, first:end, 0:D], k.X[:, first:end, :]
                link(v.tensor_tensor(sums, sums, wide(rden[:, first:end], D), ALU.mult))
                v.scalar_tensor_tensor(x, sums, 0.0, x, ALU.max, ALU.add).then_inc(done, 1)

        @block.sync
        def _(sp):
            for i, (first, end) in enumerate(groups):
                sp.wait_ge(done, i + 1)
                end = min(end, full)
                sp.dma_start(out[first * P:end * P, :].rearrange("(b p) d -> p b d", p=P), k.X[:, first:end, :]).then_inc(stored, 16)
            sp.dma_start(out[full * P:k.N, :], k.X[0:rest, full, :]).then_inc(stored, 16)
            sp.wait_ge(stored, 16 * (len(groups) + 1))



def gnn(nc, x, src, dst, edge_attr_128, edge_attr_64,
        L0_W1_l, L0_b1, L0_W1_r, L0_W2_l, L0_b2, L0_W2_r,
        L1_W1, L1_b1, L1_W2, L1_b2, L1_Wg, L1_bg, L1_gamma, L1_beta,
        L2_W1, L2_b1, L2_g1, L2_be1, L2_W2, L2_b2, L2_g2, L2_be2, L2_Wfc, L2_bfc,
        L3_Wn, L3_bn, L3_We, L3_be, L3_attn, out):
    k = Core()
    k.nc = nc
    k.N, k.D = x.shape
    k.E = src.shape[0]
    k.T = ceil_div(k.E, P)
    k.NBU = ceil_div(k.N, P)
    k.NB = ceil_div(k.NBU, GROUP) * GROUP
    k.NSTEP = ceil_div(k.T + k.NBU - 1, 4 * QUAD) * 4 * QUAD
    k.NSTEP_PAD = ceil_div(k.NSTEP + 4 * QUAD, P) * P
    D, NB = k.D, k.NB
    d1, d2 = L2_W1.shape[1], L2_W2.shape[1]
    rows = NB * P

    def dram(name, w, n=rows):
        return nc.dram_tensor(name, [n, w], F32, kind="Internal").ap()

    table_h0, table_h1 = dram("table_h0", D + 2), dram("table_h1", D + 2)
    table_mlp, table_g1, table_g2 = dram("table_mlp", 2 * D), dram("table_g1", d1), dram("table_g2", d2)
    table_att = dram("table_att", D + 2)
    tiles_dram = dram("tiles_dram", 2 * P, k.NSTEP_PAD)

    with ExitStack() as ctx:
        sb, ps, sem = scope(nc, ctx)
        k.X = sb("X", [P, NB, D])
        k.srcS, k.drelS = sb("srcS", [P, k.NSTEP_PAD], I32), sb("drelS", [P, k.NSTEP_PAD])
        k.baseT, k.blkT = sb("baseT", [1, k.NSTEP_PAD], I32), sb("blkT", [1, k.NSTEP_PAD], I32)
        k.ident, k.iota, k.ones, k.valid = sb("ident", [P, P]), sb("iota", [P, P]), sb("ones", [P, P]), sb("valid", [P, P])
        k.rdeg, k.dinv = sb("rdeg", [P, NB]), sb("dinv", [P, NB])
        k.stats, k.rstd, k.shift = sb("stats", [P, NB, 6]), sb("rstd", [P, NB]), sb("shift", [P, NB])

        k.constants_made, k.x_loaded = sem("constants_made"), sem("x_loaded")
        k.held = sem("held_pool")
        load_and_constants(nc, k, x)
        step_tables(nc, k, src, dst, tiles_dram)
        k.H = sb("H", [P, NB, D + 2])

        def agg(scope_):
            k.AGG = scope_.enter_context(nc.sbuf_tensor(f"AGG_{next(SCOPES)}", [P, NB, D + 1], F32))

        def matrix(sb, name, w):
            K, n = w.shape
            dmas, pieces = [], []
            for c in range(ceil_div(K, P)):
                rows_c = min(P, K - c * P)
                t = sb(f"{name}{c}", [P, n])
                dmas.append((t[0:rows_c, :], w[c * P:c * P + rows_c, :]))
                pieces.append((rows_c, t[0:rows_c, :]))
            return dmas, pieces

        def normed_rows(act, blk):
            return norm_relu(act, k, blk)

        first = ExitStack()
        agg(first)
        first_norm(nc, k, "ln0", table_h0)
        sum_pass(nc, k, "sage1", table_h0, D + 1, 0)
        degrees(nc, k)

        def sage(name, Wl, b, Wr, finish, keep=None, stats=False):
            def loads(sb):
                d1_, p1 = matrix(sb, "wl", Wl)
                d2_, p2 = matrix(sb, "wr", Wr)
                return d1_ + d2_, p1 + p2

            def mean(v, buf, blk):
                return v.tensor_scalar(buf[:, 0:D], rows_of(k.AGG, blk, 0, D), k.rdeg[:, bass.ds(blk, 1)], None, ALU.mult)

            def own(pool, buf, blk):
                return pool.tensor_copy(buf[:, D:2 * D], rows_of(k.H, blk, 0, D))
            node_product(nc, k, name, loads, [b], D, 2 * D, {"vector": mean, "gpsimd": own}, finish,
                         keep=keep, stats=stats)

        sage("sage1_out", L0_W1_l, L0_b1, L0_W1_r,
             ("scalar", lambda act, p, blk, o: act.activation(rows_of(k.H, blk, 0, D), p[:, 0:D], ACT.Relu)),
             keep=(table_h1, k.H))
        sum_pass(nc, k, "sage2", table_h1, D, 0)

        def add_to_x(v, p, blk, o):
            return v.tensor_tensor(rows_of(k.X, blk, 0, D), p[:, 0:D], rows_of(k.X, blk, 0, D), ALU.add)
        sage("sage2_out", L0_W2_l, L0_b2, L0_W2_r, ("vector", add_to_x), stats=True)
        first.close()

        def own_h(pool, buf, blk):
            return pool.tensor_copy(buf[:, 0:D], rows_of(k.H, blk, 0, D))

        layer_norm_constants(nc, k, "ln1", k.rstd, k.shift)

        def mlp_loads(sb):
            both = [sb(f"w1g{c}", [P, 2 * D]) for c in range(D // P)]
            dmas = [(both[c][:, i * D:(i + 1) * D], w[c * P:(c + 1) * P, :])
                    for c in range(D // P) for i, w in enumerate((L1_W1, L1_Wg))]
            return dmas, [(P, w[:, :]) for w in both]
        node_product(nc, k, "mlp_in", mlp_loads, [L1_b1, L1_bg], 2 * D, D, {"gpsimd": own_h},
                     ("vector", lambda v, p, blk, o: v.tensor_copy(o[:, :], p[:, :])), prepare=normed_rows, store=table_mlp)
        edge_mlp_pass(nc, k, "mlp", table_mlp, edge_attr_64, L1_W1, L1_Wg, L1_W2, L1_b2)
        gated_output(nc, k, L1_gamma, L1_beta)

        agg(ctx)
        layer_norm_constants(nc, k, "ln2", k.rstd, k.shift)

        def scaled(lo, W):
            return lambda act, p, blk, o: act.activation(rows_of(k.AGG, blk, lo, lo + W), p[:, 0:W], ACT.Copy,
                                                         scale=k.dinv[:, bass.ds(blk, 1)])
        node_product(nc, k, "gcn1_in", lambda sb: matrix(sb, "w", L2_W1), [], d1, D, {"gpsimd": own_h},
                     ("scalar", scaled(d1, d1)), prepare=normed_rows, keep=(table_g1, k.AGG[:, :, d1:2 * d1]))
        sum_pass(nc, k, "gcn1", table_g1, d1, 0)
        graph_norm(nc, k, "bn1", 0, d1, d1, L2_b1, L2_g1, L2_be1)
        node_product(nc, k, "gcn2_in", lambda sb: matrix(sb, "w", L2_W2), [], d2, d1,
                     {"gpsimd": lambda pool, buf, blk: pool.tensor_copy(buf[:, 0:d1], rows_of(k.AGG, blk, 0, d1))},
                     ("scalar", scaled(d1 + d2, d2)), keep=(table_g2, k.AGG[:, :, d1 + d2:d1 + 2 * d2]))
        sum_pass(nc, k, "gcn2", table_g2, d2, d1)
        graph_norm(nc, k, "bn2", d1, d2, d1 + d2, L2_b2, L2_g2, L2_be2)

        node_product(nc, k, "fc", lambda sb: matrix(sb, "wfc", L2_Wfc), [L2_bfc], D, D + d1 + d2,
                     {"gpsimd": own_h, "vector": lambda v, buf, blk: v.tensor_scalar(buf[:, D:D + d1 + d2], rows_of(k.AGG, blk, 0, d1 + d2), 1.0, None, ALU.mult)},
                     ("vector", lambda v, p, blk, o: v.scalar_tensor_tensor(rows_of(k.X, blk, 0, D), p[:, 0:D], 0.0,
                                                                            rows_of(k.X, blk, 0, D), ALU.max, ALU.add)), stats=True)

        layer_norm_constants(nc, k, "ln3", k.rstd, k.shift)
        v_row = sb("v_row", [P, L3_We.shape[1]])
        inner = ExitStack()
        sb_in, _, sem_in = scope(nc, inner)
        attn_row, const = sb_in("attn_row", [P, D]), sb_in("const", [P, 1])
        attention_constants(nc, k, L3_attn, L3_We, L3_be, v_row, attn_row, const)
        wnT = sb_in("wnT", [P, D // P, D])
        turn_weights(nc, k, L3_Wn, wnT)
        prod, part = sb_in("prod", [P, D]), sb_in("part", [P, 2])
        node_rows_done = sem_in("att_in_rows")

        def att_loads(sb):
            return [], [(P, wnT[:, c, :]) for c in range(D // P)]

        att_steps = [0]

        def att_row(v, p, blk, o):
            u = att_steps[0] % 2
            att_steps[0] += 1
            v.tensor_scalar(rows_of(k.H, blk, 0, D), p[:, 0:D], 1.0, None, ALU.mult)
            v.tensor_tensor_reduce(prod[:, :], p[:, 0:D], attn_row[:, :], 1.0, const[:, 0:1], ALU.mult, ALU.add,
                                   part[:, u:u + 1]).then_inc(node_rows_done, 1)
            v.wait_ge(node_rows_done, blk + 1)
            return v.tensor_scalar(rows_of(k.H, blk, D + 1, D + 2), part[:, u:u + 1], 1.0, None, ALU.mult)
        node_product(nc, k, "att_in", att_loads, [L3_bn], D, D, {"gpsimd": own_h}, ("vector", att_row), prepare=normed_rows,
                     keep=(table_att, k.H))
        inner.close()
        attention_pass(nc, k, "att", table_att, edge_attr_128, v_row[:, :])
        attention_output(nc, k, out)


def turn_weights(nc, k, W, wT):
    n, m = W.shape
    with ExitStack() as ctx:
        sb, ps, sem = scope(nc, ctx)
        w_in = sb("w_in", [P, n // P, m])
        p_w = ps("p_w", [P, m // P, n])
        loaded, turned, copied = sem("wn_loaded"), sem("wn_turned"), sem("wn_copied")
        block = ctx.enter_context(nc.Block())

        @block.sync
        def _(sp):
            sp.dma_start(w_in[:, :, :], W.rearrange("(a p) m -> p a m", p=P)).then_inc(loaded, 16)

        @block.tensor
        def _(pe):
            pe.wait_ge(loaded, 16)
            for c in range(m // P):
                for a in range(n // P):
                    last = pe.transpose(p_w[:, c, a * P:(a + 1) * P], w_in[:, a, c * P:(c + 1) * P], k.ident[:, :])
            last.then_inc(turned, 1)

        @block.vector
        def _(v):
            v.wait_ge(turned, 1)
            v.tensor_copy(wT[:, :, :], p_w[:, :, :]).then_inc(copied, 1)
            v.wait_ge(copied, 1)


_INS = ['x', 'src', 'dst', 'edge_attr_128', 'edge_attr_64', 'L0_gnn_W1_l', 'L0_gnn_b1', 'L0_gnn_W1_r', 'L0_gnn_W2_l',
        'L0_gnn_b2', 'L0_gnn_W2_r', 'L1_gnn_W1', 'L1_gnn_b1', 'L1_gnn_W2', 'L1_gnn_b2', 'L1_gnn_Wg', 'L1_gnn_bg',
        'L1_gnn_gamma', 'L1_gnn_beta', 'L2_gnn_W1', 'L2_gnn_b1', 'L2_gnn_g1', 'L2_gnn_be1', 'L2_gnn_W2', 'L2_gnn_b2',
        'L2_gnn_g2', 'L2_gnn_be2', 'L2_gnn_Wfc', 'L2_gnn_bfc', 'L3_gnn_Wn', 'L3_gnn_bn', 'L3_gnn_We', 'L3_gnn_be',
        'L3_gnn_attn']


def build(nc, shapes):
    args = [nc.dram_tensor(f"in_{name}_dram", shape, dt, kind="ExternalInput").ap() for name, shape, dt in shapes]
    out = nc.dram_tensor("out_0_dram", shapes[0][1], F32, kind="ExternalOutput").ap()
    gnn(nc, *args, out)


def kernel(**inputs):
    import numpy as _np
    import concourse.bacc as _bacc
    from concourse import mybir as _mybir
    from concourse.bass_utils import run_bass_kernel_spmd as _run

    nc = _bacc.Bacc("TRN2", target_bir_lowering=False, num_devices=1)
    arrays, shapes = {}, []
    for name in _INS:
        a = _np.ascontiguousarray(inputs[name])
        arrays[f"in_{name}_dram"] = a
        shapes.append((name, a.shape, _mybir.dt.from_np(a.dtype)))
    build(nc, shapes)
    r = _run(nc, [arrays], core_ids=[0])
    return r.results[0]["out_0_dram"]
```
